# Optimizing a Trainium2 kernel written in Bass

```python
import numpy as np
import jax
import jax.numpy as jnp

def _softmax(x, axis=-1):
    return jax.nn.softmax(x, axis=axis)

def _gelu(x):
    return jax.nn.gelu(x, approximate=True)

def _silu(x):
    return jax.nn.silu(x)

def _sigmoid(x):
    return jax.nn.sigmoid(x)

def _layernorm(x, axis=-1, eps=1e-05):
    m = jnp.mean(x, axis=axis, keepdims=True)
    v = jnp.var(x, axis=axis, keepdims=True)
    return (x - m) / jnp.sqrt(v + eps)

def _scatter_add(tgt, idx, src, axis=0):
    return tgt.at[idx].add(src)

def _segment_sum(src, seg, n):
    return jax.ops.segment_sum(src, seg, n)
kernel_name = 'mk_decoder_preln_d4_seqx_r8_a9a95b'

def setup_inputs(seed: int=0):
    np.random.seed(seed)
    _w = jnp.asarray

    def _rec_inputs():
        import jax
        import jax.numpy as jnp
        _rk = jax.random.key(seed)
        x = -0.0002928 + 1 * jax.random.normal(jax.random.fold_in(_rk, 1), (8, 256, 128), jnp.float32)
        _lenS = 256 - jax.random.randint(jax.random.fold_in(_rk, 7), (8,), 0, max(1, 256 // 4) + 1, jnp.int32)
        _lenS2 = 256 - jax.random.randint(jax.random.fold_in(_rk, 8), (8,), 0, max(1, 256 // 4) + 1, jnp.int32)
        _ctx_1024P = jax.random.normal(jax.random.fold_in(_rk, 11), (8, 16, 128), jnp.float32)
        _ctx_1024c = jax.random.dirichlet(jax.random.fold_in(_rk, 511), 0.3 * jnp.ones((16,), jnp.float32), (8, 256))
        _ctx_1024t = jnp.einsum('bsk,bkd->bsd', _ctx_1024c, _ctx_1024P)
        _ctx_1024t = _ctx_1024t * jax.lax.rsqrt(jnp.mean(jnp.square(_ctx_1024t)) + 1e-12) * 0.953939
        ctx_1024 = -1.39393e-06 + 0.999914 * (_ctx_1024t + 0.3 * jax.random.normal(jax.random.fold_in(_rk, 611), (8, 256, 128), jnp.float32))
        fside_BxSxS2_0 = jax.random.uniform(jax.random.fold_in(_rk, 12), (8, 256, 256), jnp.float32, 0.0, 1)
        _validS = jnp.arange(256)[None, :] < _lenS[:, None]
        _validS2 = jnp.arange(256)[None, :] < _lenS2[:, None]
        _causal = jnp.tril(jnp.ones((256, 256), dtype=bool))
        mask_BxSxS2_ik1 = jnp.where(jnp.broadcast_to(_validS2[:, None, :], (8, 256, 256)), 1, 0).astype(jnp.int32)
        mask_Bx1xSxS2_ik1 = jnp.where(jnp.broadcast_to(_validS2[:, None, None, :], (8, 1, 256, 256)), 1, 0).astype(jnp.int32)
        return (x, ctx_1024, fside_BxSxS2_0, mask_BxSxS2_ik1, mask_Bx1xSxS2_ik1)
    x, ctx_1024, fside_BxSxS2_0, mask_BxSxS2_ik1, mask_Bx1xSxS2_ik1 = _rec_inputs()

    def _L0_attn_setup():
        import jax, jax.numpy as jnp
        import numpy as np
        D_MODEL = 128
        NUM_HEADS = 16
        D_K = D_MODEL // NUM_HEADS
        THETA = 10000.0
        NEG_INF = -1000000000.0

        def _rope(x, positions):
            half = D_K // 2
            inv_freq = 1.0 / THETA ** (jnp.arange(0, D_K, 2, dtype=jnp.float32) / D_K)
            angles = positions.astype(jnp.float32)[:, None] * inv_freq
            cos, sin = (jnp.cos(angles), jnp.sin(angles))
            xe = x[..., 0::2]
            xo = x[..., 1::2]
            re = xe * cos - xo * sin
            ro = xe * sin + xo * cos
            return jnp.stack([re, ro], axis=-1).reshape(x.shape).astype(x.dtype)
        key = jax.random.key(seed)
        ks = jax.random.split(key, 5)
        sigma = np.sqrt(2.0 / (D_MODEL + D_MODEL))
        x = jax.random.normal(ks[0], (2, 256, D_MODEL), dtype=jnp.float32)
        mk = lambda k: (sigma * jax.random.normal(k, (D_MODEL, D_MODEL))).astype(jnp.float32)
        return {'x': x, 'Wq': mk(ks[1]), 'bq': jnp.zeros((D_MODEL,), jnp.float32), 'Wk': mk(ks[2]), 'bk': jnp.zeros((D_MODEL,), jnp.float32), 'Wv': mk(ks[3]), 'bv': jnp.zeros((D_MODEL,), jnp.float32), 'Wo': mk(ks[4]), 'bo': jnp.zeros((D_MODEL,), jnp.float32), 'token_positions': jnp.arange(256, dtype=jnp.int64) if jax.config.jax_enable_x64 else jnp.arange(256, dtype=jnp.int32)}
    _L0_attn_all = _L0_attn_setup()
    _L0_attn_in = {k: v for k, v in _L0_attn_all.items() if k in ('Wq', 'bq', 'Wk', 'bk', 'Wv', 'bv', 'Wo', 'bo', 'token_positions')}
    del _L0_attn_all

    def _L0_xattn_setup():
        import jax, jax.numpy as jnp
        import numpy as np
        NUM_HEADS = 16
        HIDDEN = 128
        B, S = (2, 256)

        def _split_heads(x, H):
            b, s, d = x.shape
            return x.reshape(b, s, H, d // H).transpose(0, 2, 1, 3)
        key = jax.random.key(seed)
        ks = jax.random.split(key, 14)
        D = HIDDEN
        scale = 1.0 / np.sqrt(D)
        inp = {'query': jax.random.normal(ks[0], (B, S, D), jnp.float32), 'key_in': jax.random.normal(ks[1], (B, S, D), jnp.float32), 'value': jax.random.normal(ks[2], (B, S, D), jnp.float32), 'group_prob': jax.random.uniform(ks[3], (B, S, S), jnp.float32), 'mask': jax.random.randint(ks[4], (B, S, S), 0, 2, jnp.int32), 'wq_k': jax.random.normal(ks[5], (D, D), jnp.float32) * scale, 'wq_b': jnp.zeros((D,), jnp.float32), 'wk_k': jax.random.normal(ks[6], (D, D), jnp.float32) * scale, 'wk_b': jnp.zeros((D,), jnp.float32), 'wv_k': jax.random.normal(ks[7], (D, D), jnp.float32) * scale, 'wv_b': jnp.zeros((D,), jnp.float32), 'wo_k': jax.random.normal(ks[8], (D, D), jnp.float32) * scale, 'wo_b': jnp.zeros((D,), jnp.float32)}
        return inp
    _L0_xattn_all = _L0_xattn_setup()
    _L0_xattn_in = {k: v for k, v in _L0_xattn_all.items() if k in ('wq_k', 'wq_b', 'wk_k', 'wk_b', 'wv_k', 'wv_b', 'wo_k', 'wo_b')}
    del _L0_xattn_all

    def _L0_ffn_setup():
        import jax, jax.numpy as jnp
        import numpy as np
        E = 8
        EPS = 1e-05
        key = jax.random.key(seed)
        ks = jax.random.split(key, 6)
        d, f = (128, 512)
        B, S = (2, 128)
        x = jax.random.normal(ks[0], (B, S, d), dtype=jnp.float32)
        c = jax.random.normal(ks[1], (d, E), dtype=jnp.float32)
        q, _ = jnp.linalg.qr(c)
        centroids = (0.1 * q.T).astype(jnp.float32)
        w1 = jax.random.normal(ks[2], (E, d, f), dtype=jnp.float32) / np.sqrt(d).astype(np.float32)
        b1 = jnp.zeros((E, f), dtype=jnp.float32)
        w2 = jax.random.normal(ks[3], (E, f, d), dtype=jnp.float32) * 0.02
        b2 = jnp.zeros((E, d), dtype=jnp.float32)
        gamma = jnp.ones((E, d), dtype=jnp.float32)
        beta = jnp.zeros((E, d), dtype=jnp.float32)
        return dict(x=x, centroids=centroids, w1=w1, b1=b1, w2=w2, b2=b2, gamma=gamma, beta=beta)
    _L0_ffn_all = _L0_ffn_setup()
    _L0_ffn_in = {k: v for k, v in _L0_ffn_all.items() if k in ('centroids', 'w1', 'b1', 'w2', 'b2', 'gamma', 'beta')}
    del _L0_ffn_all

    def _L1_attn_setup():
        import jax, jax.numpy as jnp
        import numpy as np
        D_MODEL = 128
        NUM_HEADS = 16
        D_K = D_MODEL // NUM_HEADS
        ROPE_THETA = 10000.0
        MAX_SEQ_LEN = 256

        def _rope_tables():
            dim_index = jnp.arange(D_K // 2, dtype=jnp.float32)
            pos = jnp.arange(MAX_SEQ_LEN, dtype=jnp.float32)
            theta_inv = ROPE_THETA ** (-2.0 * dim_index / D_K)
            ang = pos[:, None] * theta_inv[None, :]
            return (jnp.sin(ang), jnp.cos(ang))

        def _apply_rope(x, positions, sin, cos):
            s = sin[positions]
            c = cos[positions]
            x_even = x[..., ::2]
            x_odd = x[..., 1::2]
            y_even = x_even * c - x_odd * s
            y_odd = x_even * s + x_odd * c
            y = jnp.stack([y_even, y_odd], axis=-1)
            return y.reshape(x.shape)
        key = jax.random.key(seed)
        k0, k1, k2, k3, k4 = jax.random.split(key, 5)
        std = np.sqrt(2.0 / (D_MODEL + D_MODEL))
        in_features = jax.random.normal(k0, (2, 256, D_MODEL), dtype=jnp.float32)
        W_q = jax.random.normal(k1, (D_MODEL, D_MODEL), dtype=jnp.float32) * std
        W_k = jax.random.normal(k2, (D_MODEL, D_MODEL), dtype=jnp.float32) * std
        W_v = jax.random.normal(k3, (D_MODEL, D_MODEL), dtype=jnp.float32) * std
        W_o = jax.random.normal(k4, (D_MODEL, D_MODEL), dtype=jnp.float32) * std
        return {'in_features': in_features, 'W_q': W_q, 'W_k': W_k, 'W_v': W_v, 'W_o': W_o}
    _L1_attn_all = _L1_attn_setup()
    _L1_attn_in = {k: v for k, v in _L1_attn_all.items() if k in ('W_q', 'W_k', 'W_v', 'W_o')}
    del _L1_attn_all

    def _L1_xattn_setup():
        import jax, jax.numpy as jnp
        import numpy as np
        B, L, C, H = (2, 256, 128, 16)
        D = C // H
        key = jax.random.key(seed)
        ks = jax.random.split(key, 13)
        s = 1.0 / np.sqrt(C)
        inp = {'query': jax.random.normal(ks[0], (B, L, C), jnp.float32), 'key': jax.random.normal(ks[1], (B, L, C), jnp.float32), 'value': jax.random.normal(ks[2], (B, L, C), jnp.float32), 'mask': jax.random.randint(ks[3], (B, 1, L, L), 0, 2, jnp.int32), 'WQ': jax.random.normal(ks[4], (C, C), jnp.float32) * s, 'bQ': jnp.zeros((C,), jnp.float32), 'WK': jax.random.normal(ks[5], (C, C), jnp.float32) * s, 'bK': jnp.zeros((C,), jnp.float32), 'WV': jax.random.normal(ks[6], (C, C), jnp.float32) * s, 'bV': jnp.zeros((C,), jnp.float32), 'WO': jax.random.normal(ks[7], (C, C), jnp.float32) * s, 'bO': jnp.zeros((C,), jnp.float32)}
        return inp
    _L1_xattn_all = _L1_xattn_setup()
    _L1_xattn_in = {k: v for k, v in _L1_xattn_all.items() if k in ('WQ', 'bQ', 'WK', 'bK', 'WV', 'bV', 'WO', 'bO')}
    del _L1_xattn_all

    def _L1_ffn_setup():
        import jax, jax.numpy as jnp
        import numpy as np
        D_MODEL = 128
        MLP_DIM = 512
        N_EXPERTS = 8
        B, T = (4, 128)
        key = jax.random.key(seed)
        ks = jax.random.split(key, 7)
        scale_in = (1.0 / D_MODEL) ** 0.5
        scale_out = (1.0 / MLP_DIM) ** 0.5
        bound_g = (1.0 / D_MODEL) ** 0.5
        w_gate = jax.random.uniform(ks[0], (D_MODEL, N_EXPERTS), minval=-bound_g, maxval=bound_g, dtype=jnp.float32)
        b_gate = jax.random.uniform(ks[1], (N_EXPERTS,), minval=-bound_g, maxval=bound_g, dtype=jnp.float32)
        W1 = jax.random.uniform(ks[2], (N_EXPERTS, D_MODEL, MLP_DIM), minval=-scale_in, maxval=scale_in, dtype=jnp.float32)
        b1 = jnp.zeros((N_EXPERTS, MLP_DIM), dtype=jnp.float32)
        W2 = jax.random.uniform(ks[3], (N_EXPERTS, MLP_DIM, D_MODEL), minval=-scale_out, maxval=scale_out, dtype=jnp.float32)
        b2 = jnp.zeros((N_EXPERTS, D_MODEL), dtype=jnp.float32)
        x = jax.random.normal(ks[4], (B, T, D_MODEL), dtype=jnp.float32)
        return {'x': x, 'w_gate': w_gate, 'b_gate': b_gate, 'W1': W1, 'b1': b1, 'W2': W2, 'b2': b2}
    _L1_ffn_all = _L1_ffn_setup()
    _L1_ffn_in = {k: v for k, v in _L1_ffn_all.items() if k in ('w_gate', 'b_gate', 'W1', 'b1', 'W2', 'b2')}
    del _L1_ffn_all

    def _L2_attn_setup():
        import jax, jax.numpy as jnp
        import numpy as np
        DIM = 128
        DIM_HEADS = 128
        HEADS = 8
        DHEAD = DIM_HEADS // HEADS
        EPS = 1e-06

        def _l2norm(t, axis=-1):
            n = jnp.sqrt(jnp.sum(t * t, axis=axis, keepdims=True))
            return t / jnp.maximum(n, 1e-12)
        key = jax.random.key(seed)
        k1, k2, k3 = jax.random.split(key, 3)
        x = jax.random.normal(k1, (8, 512, DIM), dtype=jnp.float32)
        norm_weight = jnp.ones((DIM,), dtype=jnp.float32)
        w_qkv = jax.random.normal(k2, (3 * DIM_HEADS, DIM), dtype=jnp.float32) * (1.0 / np.sqrt(DIM))
        temperature = jnp.zeros((HEADS, 1, 1), dtype=jnp.float32)
        w_out = jax.random.normal(k3, (DIM, DIM_HEADS), dtype=jnp.float32) * (1.0 / np.sqrt(DIM_HEADS))
        return {'x': x, 'norm_weight': norm_weight, 'w_qkv': w_qkv, 'temperature': temperature, 'w_out': w_out}
    _L2_attn_all = _L2_attn_setup()
    _L2_attn_in = {k: v for k, v in _L2_attn_all.items() if k in ('norm_weight', 'w_qkv', 'temperature', 'w_out')}
    del _L2_attn_all

    def _L2_xattn_setup():
        import jax, jax.numpy as jnp
        import numpy as np
        EMBED_DIM = 128
        HEAD_DIM = 128
        GAMMA = 0.96875
        THETA = 10000.0
        SCALE_BASE = 512.0

        def _dup_interleave(x):
            return jnp.repeat(x, 2, axis=-1)

        def _rotate_half(x):
            x_even = x[..., ::2]
            x_odd = x[..., 1::2]
            return jnp.stack((-x_odd, x_even), axis=-1).reshape(x.shape)

        def _xpos(x, offset=0, inverse_scale=False):
            l = x.shape[-2]
            half = HEAD_DIM // 2
            scale_vec = (jnp.arange(0, HEAD_DIM, 2, dtype=jnp.float32) + 0.4 * HEAD_DIM) / (1.4 * HEAD_DIM)
            pos = jnp.arange(offset, offset + l, dtype=jnp.float32)
            scale = scale_vec[None, :] ** (pos / SCALE_BASE)[:, None]
            freqs = 1.0 / THETA ** (jnp.arange(half, dtype=jnp.float32) / half)
            sin_in = pos[:, None] * freqs[None, :]
            sin, cos = (jnp.sin(sin_in), jnp.cos(sin_in))
            if inverse_scale:
                scale = 1.0 / scale
            return x * _dup_interleave(cos * scale) + _rotate_half(x) * _dup_interleave(sin * scale)

        def _decay_mask(l, gamma):
            idx = jnp.arange(l, dtype=jnp.float32)
            diff = idx[:, None] - idx[None, :]
            return jnp.where(diff >= 0, gamma ** diff, 0.0)
        key = jax.random.key(seed)
        k1, k2, k3, k4, k5, k6 = jax.random.split(key, 6)
        B, L = (4, 256)
        s = 1.0 / np.sqrt(EMBED_DIM)
        return {'q': jax.random.normal(k1, (B, L, EMBED_DIM), dtype=jnp.float32), 'k': jax.random.normal(k2, (B, L, EMBED_DIM), dtype=jnp.float32), 'v': jax.random.normal(k3, (B, L, EMBED_DIM), dtype=jnp.float32), 'Wq': jax.random.normal(k4, (EMBED_DIM, HEAD_DIM), dtype=jnp.float32) * s, 'Wk': jax.random.normal(k5, (EMBED_DIM, HEAD_DIM), dtype=jnp.float32) * s, 'Wv': jax.random.normal(k6, (EMBED_DIM, HEAD_DIM), dtype=jnp.float32) * s}
    _L2_xattn_all = _L2_xattn_setup()
    _L2_xattn_in = {k: v for k, v in _L2_xattn_all.items() if k in ('Wq', 'Wk', 'Wv')}
    del _L2_xattn_all

    def _L2_ffn_setup():
        import jax, jax.numpy as jnp
        import numpy as np
        D_MODEL, D_FF, N_EXP = (128, 512, 8)
        key = jax.random.key(seed)
        ks = jax.random.split(key, 8)
        s = lambda fan_in: 1.0 / np.sqrt(fan_in)
        x = jax.random.normal(ks[0], (4, 256, D_MODEL), dtype=jnp.float32)
        Wr = jax.random.uniform(ks[1], (N_EXP, D_MODEL), jnp.float32, -s(D_MODEL), s(D_MODEL))
        br = jax.random.uniform(ks[2], (N_EXP,), jnp.float32, -s(D_MODEL), s(D_MODEL))
        W1 = jax.random.uniform(ks[3], (N_EXP, D_FF, D_MODEL), jnp.float32, -s(D_MODEL), s(D_MODEL))
        b1 = jax.random.uniform(ks[4], (N_EXP, D_FF), jnp.float32, -s(D_MODEL), s(D_MODEL))
        W2 = jax.random.uniform(ks[5], (N_EXP, D_MODEL, D_FF), jnp.float32, -s(D_FF), s(D_FF))
        b2 = jax.random.uniform(ks[6], (N_EXP, D_MODEL), jnp.float32, -s(D_FF), s(D_FF))
        return {'x': x, 'Wr': Wr, 'br': br, 'W1': W1, 'b1': b1, 'W2': W2, 'b2': b2}
    _L2_ffn_all = _L2_ffn_setup()
    _L2_ffn_in = {k: v for k, v in _L2_ffn_all.items() if k in ('Wr', 'br', 'W1', 'b1', 'W2', 'b2')}
    del _L2_ffn_all

    def _L3_attn_setup():
        import jax, jax.numpy as jnp
        from jax import lax
        import numpy as np
        D_MODEL = 128
        D_STATE = 64
        D_CONV = 4
        EXPAND = 2
        HEADDIM = 128
        NGROUPS = 1
        CHUNK = 32
        D_INNER = EXPAND * D_MODEL
        NHEADS = D_INNER // HEADDIM
        CONV_DIM = D_INNER + 2 * NGROUPS * D_STATE
        D_IN_PROJ = D_INNER + CONV_DIM + NHEADS

        def _segsum_exp(t):
            T = t.shape[-1]
            cs = jnp.cumsum(t, axis=-1)
            d = cs[..., :, None] - cs[..., None, :]
            mask = jnp.tril(jnp.ones((T, T), dtype=bool))
            return jnp.where(mask, jnp.exp(jnp.where(mask, d, 0.0)), 0.0)

        def _ssd_scan(x, dt, A, Bm, Cm, chunk):
            Bz, L, H, P = x.shape
            G, N = (Bm.shape[2], Bm.shape[3])
            nc = L // chunk
            rep = H // G
            Bh = jnp.repeat(Bm, rep, axis=2)
            Ch = jnp.repeat(Cm, rep, axis=2)
            xc = x.reshape(Bz, nc, chunk, H, P)
            dtc = dt.reshape(Bz, nc, chunk, H)
            Bc = Bh.reshape(Bz, nc, chunk, H, N)
            Cc = Ch.reshape(Bz, nc, chunk, H, N)
            dA = dtc * A[None, None, None, :]
            dAh = jnp.transpose(dA, (0, 1, 3, 2))
            A_cs = jnp.cumsum(dAh, axis=-1)
            Lmat = _segsum_exp(dAh)
            Y_diag = jnp.einsum('bcqhn,bckhn,bchqk,bckh,bckhp->bcqhp', Cc, Bc, Lmat, dtc, xc)
            decay_states = jnp.exp(A_cs[..., -1:] - A_cs)
            states = jnp.einsum('bckhn,bchk,bckh,bckhp->bchpn', Bc, decay_states, dtc, xc)
            chunk_total = jnp.transpose(A_cs[..., -1], (0, 2, 1))
            padded = jnp.pad(chunk_total, ((0, 0), (0, 0), (1, 0)))
            decay_chunk = _segsum_exp(padded)
            states_cat = jnp.concatenate([jnp.zeros_like(states[:, :1]), states], axis=1)
            new_states = jnp.einsum('bhzc,bchpn->bzhpn', decay_chunk, states_cat)
            prev = new_states[:, :-1]
            Y_off = jnp.einsum('bcqhn,bchpn,bchq->bcqhp', Cc, prev, jnp.exp(A_cs))
            return (Y_diag + Y_off).reshape(Bz, L, H, P)
        key = jax.random.key(seed)
        ks = jax.random.split(key, 8)
        x = jax.random.normal(ks[0], (2, 512, D_MODEL), dtype=jnp.float32)
        W_in = jax.random.normal(ks[1], (D_IN_PROJ, D_MODEL), dtype=jnp.float32) * 0.02
        conv_w = jax.random.normal(ks[2], (CONV_DIM, 1, D_CONV), dtype=jnp.float32) * 0.2
        conv_b = jnp.zeros((CONV_DIM,), dtype=jnp.float32)
        A_init = jax.random.uniform(ks[3], (NHEADS,), minval=1.0, maxval=16.0)
        A_log = jnp.log(A_init).astype(jnp.float32)
        dtv = jnp.exp(jax.random.uniform(ks[4], (NHEADS,)) * (np.log(0.1) - np.log(0.001)) + np.log(0.001))
        dtv = jnp.clip(dtv, 0.001, None)
        dt_bias = (dtv + jnp.log(-jnp.expm1(-dtv))).astype(jnp.float32)
        D_skip = jnp.ones((NHEADS,), dtype=jnp.float32)
        W_out = jax.random.normal(ks[5], (D_MODEL, D_INNER), dtype=jnp.float32) * 0.02
        return {'x': x, 'W_in': W_in, 'conv_w': conv_w, 'conv_b': conv_b, 'A_log': A_log, 'dt_bias': dt_bias, 'D_skip': D_skip, 'W_out': W_out}
    _L3_attn_all = _L3_attn_setup()
    _L3_attn_in = {k: v for k, v in _L3_attn_all.items() if k in ('W_in', 'conv_w', 'conv_b', 'A_log', 'dt_bias', 'D_skip', 'W_out')}
    del _L3_attn_all

    def _L3_xattn_setup():
        import jax, jax.numpy as jnp
        import numpy as np
        D_MODEL = 128
        NUM_HEADS = 16
        D_K = D_MODEL // NUM_HEADS
        SCALE = float(np.sqrt(D_K))
        key = jax.random.key(seed)
        ks = jax.random.split(key, 12)
        B, S = (4, 256)
        s = 1.0 / np.sqrt(D_MODEL)
        inp = {'query': jax.random.normal(ks[0], (B, S, D_MODEL), jnp.float32), 'key': jax.random.normal(ks[1], (B, S, D_MODEL), jnp.float32), 'value': jax.random.normal(ks[2], (B, S, D_MODEL), jnp.float32), 'Wq': jax.random.normal(ks[3], (D_MODEL, D_MODEL), jnp.float32) * s, 'bq': jax.random.normal(ks[4], (D_MODEL,), jnp.float32) * s, 'Wk': jax.random.normal(ks[5], (D_MODEL, D_MODEL), jnp.float32) * s, 'bk': jax.random.normal(ks[6], (D_MODEL,), jnp.float32) * s, 'Wv': jax.random.normal(ks[7], (D_MODEL, D_MODEL), jnp.float32) * s, 'bv': jax.random.normal(ks[8], (D_MODEL,), jnp.float32) * s, 'Wo': jax.random.normal(ks[9], (D_MODEL, D_MODEL), jnp.float32) * s, 'bo': jax.random.normal(ks[10], (D_MODEL,), jnp.float32) * s}
        return inp
    _L3_xattn_all = _L3_xattn_setup()
    _L3_xattn_in = {k: v for k, v in _L3_xattn_all.items() if k in ('Wq', 'bq', 'Wk', 'bk', 'Wv', 'bv', 'Wo', 'bo')}
    del _L3_xattn_all

    def _L3_ffn_setup():
        import jax, jax.numpy as jnp
        import numpy as np
        DIM = 128
        LATENT = 64
        INTER = 64
        SHARED = 512
        E = 8
        TOPK = 2
        NGROUP = 2
        TOPKG = 1
        NORM_TOPK = True
        SCALE = 1.0
        B, S = (2, 128)

        def relu2(x):
            r = jnp.maximum(x, 0.0)
            return r * r
        key = jax.random.key(seed)
        ks = jax.random.split(key, 8)

        def w(k, shape, std=0.02):
            return jax.random.normal(k, shape, dtype=jnp.float32) * std
        return {'x': jax.random.normal(ks[0], (B, S, DIM), dtype=jnp.float32), 'gate': w(ks[1], (E, DIM)), 'corr_bias': jnp.zeros((E,), jnp.float32), 'w1': w(ks[2], (E, INTER, LATENT)), 'w2': w(ks[3], (E, LATENT, INTER)), 'fc1_w': w(ks[4], (LATENT, DIM)), 'fc2_w': w(ks[5], (DIM, LATENT)), 'up_w': w(ks[6], (SHARED, DIM)), 'down_w': w(ks[7], (DIM, SHARED))}
    _L3_ffn_all = _L3_ffn_setup()
    _L3_ffn_in = {k: v for k, v in _L3_ffn_all.items() if k in ('gate', 'corr_bias', 'w1', 'w2', 'fc1_w', 'fc2_w', 'up_w', 'down_w')}
    del _L3_ffn_all
    return {'x': x, 'ctx_1024': ctx_1024, 'fside_BxSxS2_0': fside_BxSxS2_0, 'mask_BxSxS2_ik1': mask_BxSxS2_ik1, 'mask_Bx1xSxS2_ik1': mask_Bx1xSxS2_ik1, 'L0_attn_Wq': _L0_attn_in['Wq'], 'L0_attn_bq': _L0_attn_in['bq'], 'L0_attn_Wk': _L0_attn_in['Wk'], 'L0_attn_bk': _L0_attn_in['bk'], 'L0_attn_Wv': _L0_attn_in['Wv'], 'L0_attn_bv': _L0_attn_in['bv'], 'L0_attn_Wo': _L0_attn_in['Wo'], 'L0_attn_bo': _L0_attn_in['bo'], 'L0_attn_token_positions': _L0_attn_in['token_positions'], 'L0_xattn_wq_k': _L0_xattn_in['wq_k'], 'L0_xattn_wq_b': _L0_xattn_in['wq_b'], 'L0_xattn_wk_k': _L0_xattn_in['wk_k'], 'L0_xattn_wk_b': _L0_xattn_in['wk_b'], 'L0_xattn_wv_k': _L0_xattn_in['wv_k'], 'L0_xattn_wv_b': _L0_xattn_in['wv_b'], 'L0_xattn_wo_k': _L0_xattn_in['wo_k'], 'L0_xattn_wo_b': _L0_xattn_in['wo_b'], 'L0_ffn_centroids': _L0_ffn_in['centroids'], 'L0_ffn_w1': _L0_ffn_in['w1'], 'L0_ffn_b1': _L0_ffn_in['b1'], 'L0_ffn_w2': _L0_ffn_in['w2'], 'L0_ffn_b2': _L0_ffn_in['b2'], 'L0_ffn_gamma': _L0_ffn_in['gamma'], 'L0_ffn_beta': _L0_ffn_in['beta'], 'L1_attn_W_q': _L1_attn_in['W_q'], 'L1_attn_W_k': _L1_attn_in['W_k'], 'L1_attn_W_v': _L1_attn_in['W_v'], 'L1_attn_W_o': _L1_attn_in['W_o'], 'L1_xattn_WQ': _L1_xattn_in['WQ'], 'L1_xattn_bQ': _L1_xattn_in['bQ'], 'L1_xattn_WK': _L1_xattn_in['WK'], 'L1_xattn_bK': _L1_xattn_in['bK'], 'L1_xattn_WV': _L1_xattn_in['WV'], 'L1_xattn_bV': _L1_xattn_in['bV'], 'L1_xattn_WO': _L1_xattn_in['WO'], 'L1_xattn_bO': _L1_xattn_in['bO'], 'L1_ffn_w_gate': _L1_ffn_in['w_gate'], 'L1_ffn_b_gate': _L1_ffn_in['b_gate'], 'L1_ffn_W1': _L1_ffn_in['W1'], 'L1_ffn_b1': _L1_ffn_in['b1'], 'L1_ffn_W2': _L1_ffn_in['W2'], 'L1_ffn_b2': _L1_ffn_in['b2'], 'L2_attn_norm_weight': _L2_attn_in['norm_weight'], 'L2_attn_w_qkv': _L2_attn_in['w_qkv'], 'L2_attn_temperature': _L2_attn_in['temperature'], 'L2_attn_w_out': _L2_attn_in['w_out'], 'L2_xattn_Wq': _L2_xattn_in['Wq'], 'L2_xattn_Wk': _L2_xattn_in['Wk'], 'L2_xattn_Wv': _L2_xattn_in['Wv'], 'L2_ffn_Wr': _L2_ffn_in['Wr'], 'L2_ffn_br': _L2_ffn_in['br'], 'L2_ffn_W1': _L2_ffn_in['W1'], 'L2_ffn_b1': _L2_ffn_in['b1'], 'L2_ffn_W2': _L2_ffn_in['W2'], 'L2_ffn_b2': _L2_ffn_in['b2'], 'L3_attn_W_in': _L3_attn_in['W_in'], 'L3_attn_conv_w': _L3_attn_in['conv_w'], 'L3_attn_conv_b': _L3_attn_in['conv_b'], 'L3_attn_A_log': _L3_attn_in['A_log'], 'L3_attn_dt_bias': _L3_attn_in['dt_bias'], 'L3_attn_D_skip': _L3_attn_in['D_skip'], 'L3_attn_W_out': _L3_attn_in['W_out'], 'L3_xattn_Wq': _L3_xattn_in['Wq'], 'L3_xattn_bq': _L3_xattn_in['bq'], 'L3_xattn_Wk': _L3_xattn_in['Wk'], 'L3_xattn_bk': _L3_xattn_in['bk'], 'L3_xattn_Wv': _L3_xattn_in['Wv'], 'L3_xattn_bv': _L3_xattn_in['bv'], 'L3_xattn_Wo': _L3_xattn_in['Wo'], 'L3_xattn_bo': _L3_xattn_in['bo'], 'L3_ffn_gate': _L3_ffn_in['gate'], 'L3_ffn_corr_bias': _L3_ffn_in['corr_bias'], 'L3_ffn_w1': _L3_ffn_in['w1'], 'L3_ffn_w2': _L3_ffn_in['w2'], 'L3_ffn_fc1_w': _L3_ffn_in['fc1_w'], 'L3_ffn_fc2_w': _L3_ffn_in['fc2_w'], 'L3_ffn_up_w': _L3_ffn_in['up_w'], 'L3_ffn_down_w': _L3_ffn_in['down_w']}

def reference(x, ctx_1024, fside_BxSxS2_0, mask_BxSxS2_ik1, mask_Bx1xSxS2_ik1, L0_attn_Wq, L0_attn_bq, L0_attn_Wk, L0_attn_bk, L0_attn_Wv, L0_attn_bv, L0_attn_Wo, L0_attn_bo, L0_attn_token_positions, L0_xattn_wq_k, L0_xattn_wq_b, L0_xattn_wk_k, L0_xattn_wk_b, L0_xattn_wv_k, L0_xattn_wv_b, L0_xattn_wo_k, L0_xattn_wo_b, L0_ffn_centroids, L0_ffn_w1, L0_ffn_b1, L0_ffn_w2, L0_ffn_b2, L0_ffn_gamma, L0_ffn_beta, L1_attn_W_q, L1_attn_W_k, L1_attn_W_v, L1_attn_W_o, L1_xattn_WQ, L1_xattn_bQ, L1_xattn_WK, L1_xattn_bK, L1_xattn_WV, L1_xattn_bV, L1_xattn_WO, L1_xattn_bO, L1_ffn_w_gate, L1_ffn_b_gate, L1_ffn_W1, L1_ffn_b1, L1_ffn_W2, L1_ffn_b2, L2_attn_norm_weight, L2_attn_w_qkv, L2_attn_temperature, L2_attn_w_out, L2_xattn_Wq, L2_xattn_Wk, L2_xattn_Wv, L2_ffn_Wr, L2_ffn_br, L2_ffn_W1, L2_ffn_b1, L2_ffn_W2, L2_ffn_b2, L3_attn_W_in, L3_attn_conv_w, L3_attn_conv_b, L3_attn_A_log, L3_attn_dt_bias, L3_attn_D_skip, L3_attn_W_out, L3_xattn_Wq, L3_xattn_bq, L3_xattn_Wk, L3_xattn_bk, L3_xattn_Wv, L3_xattn_bv, L3_xattn_Wo, L3_xattn_bo, L3_ffn_gate, L3_ffn_corr_bias, L3_ffn_w1, L3_ffn_w2, L3_ffn_fc1_w, L3_ffn_fc2_w, L3_ffn_up_w, L3_ffn_down_w):
    import jax
    import jax.numpy as jnp

    def _L0_attn_ref(x, Wq, bq, Wk, bk, Wv, bv, Wo, bo, token_positions):
        import jax, jax.numpy as jnp
        import numpy as np
        D_MODEL = 128
        NUM_HEADS = 16
        D_K = D_MODEL // NUM_HEADS
        THETA = 10000.0
        NEG_INF = -1000000000.0

        def _rope(x, positions):
            half = D_K // 2
            inv_freq = 1.0 / THETA ** (jnp.arange(0, D_K, 2, dtype=jnp.float32) / D_K)
            angles = positions.astype(jnp.float32)[:, None] * inv_freq
            cos, sin = (jnp.cos(angles), jnp.sin(angles))
            xe = x[..., 0::2]
            xo = x[..., 1::2]
            re = xe * cos - xo * sin
            ro = xe * sin + xo * cos
            return jnp.stack([re, ro], axis=-1).reshape(x.shape).astype(x.dtype)
        B, S, D = x.shape
        Q = x @ Wq.T + bq
        K = x @ Wk.T + bk
        V = x @ Wv.T + bv

        def split_heads(t):
            return t.reshape(B, S, NUM_HEADS, D_K).transpose(0, 2, 1, 3)
        Q, K, V = (split_heads(Q), split_heads(K), split_heads(V))
        pos = jnp.arange(S)
        Q = _rope(Q, pos)
        K = _rope(K, pos)
        scale = 1.0 / jnp.sqrt(jnp.float32(D_K))
        scores = jnp.einsum('bhqd,bhkd->bhqk', Q, K) * scale
        causal = jnp.tril(jnp.ones((S, S), dtype=bool))
        scores = jnp.where(causal, scores, NEG_INF)
        weights = jax.nn.softmax(scores, axis=-1)
        attn = jnp.einsum('bhqk,bhkd->bhqd', weights, V)
        concat = attn.transpose(0, 2, 1, 3).reshape(B, S, D)
        return concat @ Wo.T + bo

    def _L0_xattn_ref(query, key_in, value, group_prob, mask, wq_k, wq_b, wk_k, wk_b, wv_k, wv_b, wo_k, wo_b):
        import jax, jax.numpy as jnp
        import numpy as np
        NUM_HEADS = 16
        HIDDEN = 128
        B, S = (2, 256)

        def _split_heads(x, H):
            b, s, d = x.shape
            return x.reshape(b, s, H, d // H).transpose(0, 2, 1, 3)
        H = NUM_HEADS
        dh = query.shape[-1] // H
        q = _split_heads(query @ wq_k + wq_b, H)
        k = _split_heads(key_in @ wk_k + wk_b, H)
        v = _split_heads(value @ wv_k + wv_b, H)
        logits = jnp.einsum('bhqd,bhkd->bhqk', q, k) / jnp.sqrt(jnp.asarray(dh, q.dtype))
        neg = (1.0 - mask.astype(q.dtype)) * -1000000000.0
        logits = logits + neg[:, None, :, :]
        attn = jax.nn.softmax(logits, axis=-1)
        attn = attn * group_prob[:, None, :, :]
        out = jnp.einsum('bhqk,bhkd->bhqd', attn, v)
        out = out.transpose(0, 2, 1, 3).reshape(query.shape[0], -1, H * dh)
        return out @ wo_k + wo_b

    def _L0_ffn_ref(x, centroids, w1, b1, w2, b2, gamma, beta):
        import jax, jax.numpy as jnp
        import numpy as np
        E = 8
        EPS = 1e-05
        B, S, d = x.shape
        feats = x.reshape(-1, d)
        aff = feats @ centroids.T
        eid = jnp.argmax(aff, axis=1)
        mu = jnp.mean(feats, axis=-1, keepdims=True)
        var = jnp.var(feats, axis=-1, keepdims=True)
        xhat = (feats - mu) * jax.lax.rsqrt(var + EPS)
        out = jnp.zeros_like(feats)
        for e in range(E):
            mask = (eid == e).astype(feats.dtype)[:, None]
            h = xhat * gamma[e] + beta[e]
            y = feats + jax.nn.relu(h @ w1[e] + b1[e]) @ w2[e] + b2[e]
            alpha = jax.nn.sigmoid(feats @ centroids[e])[:, None]
            out = out + mask * (alpha * y + (1.0 - alpha) * feats)
        return out.reshape(B, S, d)

    def _L1_attn_ref(in_features, W_q, W_k, W_v, W_o):
        import jax, jax.numpy as jnp
        import numpy as np
        D_MODEL = 128
        NUM_HEADS = 16
        D_K = D_MODEL // NUM_HEADS
        ROPE_THETA = 10000.0
        MAX_SEQ_LEN = 256

        def _rope_tables():
            dim_index = jnp.arange(D_K // 2, dtype=jnp.float32)
            pos = jnp.arange(MAX_SEQ_LEN, dtype=jnp.float32)
            theta_inv = ROPE_THETA ** (-2.0 * dim_index / D_K)
            ang = pos[:, None] * theta_inv[None, :]
            return (jnp.sin(ang), jnp.cos(ang))

        def _apply_rope(x, positions, sin, cos):
            s = sin[positions]
            c = cos[positions]
            x_even = x[..., ::2]
            x_odd = x[..., 1::2]
            y_even = x_even * c - x_odd * s
            y_odd = x_even * s + x_odd * c
            y = jnp.stack([y_even, y_odd], axis=-1)
            return y.reshape(x.shape)
        B, S, _ = in_features.shape
        sin, cos = _rope_tables()
        positions = jnp.arange(S)

        def proj(W):
            y = jnp.einsum('bsd,od->bso', in_features, W)
            return y.reshape(B, S, NUM_HEADS, D_K).transpose(0, 2, 1, 3)
        Q = _apply_rope(proj(W_q), positions, sin, cos)
        K = _apply_rope(proj(W_k), positions, sin, cos)
        V = proj(W_v)
        scores = jnp.einsum('bhnd,bhmd->bhnm', Q, K) / jnp.sqrt(jnp.float32(D_K))
        causal = jnp.tril(jnp.ones((S, S), dtype=bool))
        scores = jnp.where(causal[None, None], scores, -jnp.inf)
        attn = jax.nn.softmax(scores, axis=-1)
        head = jnp.einsum('bhnm,bhmd->bhnd', attn, V)
        head = head.transpose(0, 2, 1, 3).reshape(B, S, D_MODEL)
        return jnp.einsum('bso,do->bsd', head, W_o.T.T) if False else jnp.einsum('bsi,oi->bso', head, W_o)

    def _L1_xattn_ref(query, key, value, mask, WQ, bQ, WK, bK, WV, bV, WO, bO):
        import jax, jax.numpy as jnp
        import numpy as np
        B, L, C, H = (2, 256, 128, 16)
        D = C // H
        b = query.shape[0]
        Q = query @ WQ + bQ
        K = key @ WK + bK
        V = value @ WV + bV

        def split_heads(x):
            return x.reshape(b, -1, H, D).transpose(0, 2, 1, 3)
        Qh, Kh, Vh = (split_heads(Q), split_heads(K), split_heads(V))
        scores = jnp.einsum('bhqd,bhkd->bhqk', Qh, Kh) / jnp.sqrt(jnp.float32(D))
        scores = jnp.where(mask == 0, jnp.float32(-1000000000.0), scores)
        attn = jax.nn.softmax(scores, axis=-1)
        Z = jnp.einsum('bhqk,bhkd->bhqd', attn, Vh)
        Z = Z.transpose(0, 2, 1, 3).reshape(b, Q.shape[1], C)
        return Z @ WO + bO

    def _L1_ffn_ref(x, w_gate, b_gate, W1, b1, W2, b2):
        import jax, jax.numpy as jnp
        import numpy as np
        D_MODEL = 128
        MLP_DIM = 512
        N_EXPERTS = 8
        B, T = (4, 128)
        b, t, d = x.shape
        x_flat = x.reshape(b * t, d)
        logits = x_flat @ w_gate + b_gate
        probs = jax.nn.softmax(logits, axis=-1)
        route_p = jnp.max(probs, axis=-1)
        route_idx = jnp.argmax(probs, axis=-1)
        h = jnp.einsum('nd,edm->enm', x_flat, W1) + b1[:, None, :]
        h = jax.nn.relu(h)
        y = jnp.einsum('enm,emd->end', h, W2) + b2[:, None, :]
        n = b * t
        out = y[route_idx, jnp.arange(n)] * route_p[:, None]
        return out.reshape(b, t, d)

    def _L2_attn_ref(x, norm_weight, w_qkv, temperature, w_out):
        import jax, jax.numpy as jnp
        import numpy as np
        DIM = 128
        DIM_HEADS = 128
        HEADS = 8
        DHEAD = DIM_HEADS // HEADS
        EPS = 1e-06

        def _l2norm(t, axis=-1):
            n = jnp.sqrt(jnp.sum(t * t, axis=axis, keepdims=True))
            return t / jnp.maximum(n, 1e-12)
        b, n, _ = x.shape
        ms = jnp.mean(x * x, axis=-1, keepdims=True)
        xn = x * jax.lax.rsqrt(ms + EPS) * norm_weight
        qkv = jnp.einsum('bnc,oc->bno', xn, w_qkv)
        qkv = qkv.reshape(b, n, 3, HEADS, DHEAD).transpose(2, 0, 3, 4, 1)
        q, k, v = (qkv[0], qkv[1], qkv[2])
        q = _l2norm(q)
        k = _l2norm(k)
        q = q * jnp.exp(temperature)
        sim = jnp.einsum('bhin,bhjn->bhij', q, k)
        attn = jax.nn.softmax(sim, axis=-1)
        out = jnp.einsum('bhij,bhjn->bhin', attn, v)
        out = out.transpose(0, 3, 1, 2).reshape(b, n, HEADS * DHEAD)
        return jnp.einsum('bnc,oc->bno', out, w_out)

    def _L2_xattn_ref(q, k, v, Wq, Wk, Wv):
        import jax, jax.numpy as jnp
        import numpy as np
        EMBED_DIM = 128
        HEAD_DIM = 128
        GAMMA = 0.96875
        THETA = 10000.0
        SCALE_BASE = 512.0

        def _dup_interleave(x):
            return jnp.repeat(x, 2, axis=-1)

        def _rotate_half(x):
            x_even = x[..., ::2]
            x_odd = x[..., 1::2]
            return jnp.stack((-x_odd, x_even), axis=-1).reshape(x.shape)

        def _xpos(x, offset=0, inverse_scale=False):
            l = x.shape[-2]
            half = HEAD_DIM // 2
            scale_vec = (jnp.arange(0, HEAD_DIM, 2, dtype=jnp.float32) + 0.4 * HEAD_DIM) / (1.4 * HEAD_DIM)
            pos = jnp.arange(offset, offset + l, dtype=jnp.float32)
            scale = scale_vec[None, :] ** (pos / SCALE_BASE)[:, None]
            freqs = 1.0 / THETA ** (jnp.arange(half, dtype=jnp.float32) / half)
            sin_in = pos[:, None] * freqs[None, :]
            sin, cos = (jnp.sin(sin_in), jnp.cos(sin_in))
            if inverse_scale:
                scale = 1.0 / scale
            return x * _dup_interleave(cos * scale) + _rotate_half(x) * _dup_interleave(sin * scale)

        def _decay_mask(l, gamma):
            idx = jnp.arange(l, dtype=jnp.float32)
            diff = idx[:, None] - idx[None, :]
            return jnp.where(diff >= 0, gamma ** diff, 0.0)
        qh = _xpos(q @ Wq, offset=0, inverse_scale=False)
        kh = _xpos(k @ Wk, offset=0, inverse_scale=True)
        vh = v @ Wv
        L = qh.shape[-2]
        mask = _decay_mask(L, GAMMA)
        scores = jnp.einsum('bld,bmd->blm', qh, kh) * mask[None, :, :]
        return scores @ vh

    def _L2_ffn_ref(x, Wr, br, W1, b1, W2, b2):
        import jax, jax.numpy as jnp
        import numpy as np
        D_MODEL, D_FF, N_EXP = (128, 512, 8)
        B, S, D = x.shape
        xf = x.reshape(-1, D)
        logits = xf @ Wr.T + br
        expert_idx = jnp.argmax(logits, axis=-1)
        h = jax.nn.relu(jnp.einsum('td,efd->etf', xf, W1) + b1[:, None, :])
        y = jnp.einsum('etf,edf->etd', h, W2) + b2[:, None, :]
        out = y[expert_idx, jnp.arange(xf.shape[0])]
        return out.reshape(B, S, D)

    def _L3_attn_ref(x, W_in, conv_w, conv_b, A_log, dt_bias, D_skip, W_out):
        import jax, jax.numpy as jnp
        from jax import lax
        import numpy as np
        D_MODEL = 128
        D_STATE = 64
        D_CONV = 4
        EXPAND = 2
        HEADDIM = 128
        NGROUPS = 1
        CHUNK = 32
        D_INNER = EXPAND * D_MODEL
        NHEADS = D_INNER // HEADDIM
        CONV_DIM = D_INNER + 2 * NGROUPS * D_STATE
        D_IN_PROJ = D_INNER + CONV_DIM + NHEADS

        def _segsum_exp(t):
            T = t.shape[-1]
            cs = jnp.cumsum(t, axis=-1)
            d = cs[..., :, None] - cs[..., None, :]
            mask = jnp.tril(jnp.ones((T, T), dtype=bool))
            return jnp.where(mask, jnp.exp(jnp.where(mask, d, 0.0)), 0.0)

        def _ssd_scan(x, dt, A, Bm, Cm, chunk):
            Bz, L, H, P = x.shape
            G, N = (Bm.shape[2], Bm.shape[3])
            nc = L // chunk
            rep = H // G
            Bh = jnp.repeat(Bm, rep, axis=2)
            Ch = jnp.repeat(Cm, rep, axis=2)
            xc = x.reshape(Bz, nc, chunk, H, P)
            dtc = dt.reshape(Bz, nc, chunk, H)
            Bc = Bh.reshape(Bz, nc, chunk, H, N)
            Cc = Ch.reshape(Bz, nc, chunk, H, N)
            dA = dtc * A[None, None, None, :]
            dAh = jnp.transpose(dA, (0, 1, 3, 2))
            A_cs = jnp.cumsum(dAh, axis=-1)
            Lmat = _segsum_exp(dAh)
            Y_diag = jnp.einsum('bcqhn,bckhn,bchqk,bckh,bckhp->bcqhp', Cc, Bc, Lmat, dtc, xc)
            decay_states = jnp.exp(A_cs[..., -1:] - A_cs)
            states = jnp.einsum('bckhn,bchk,bckh,bckhp->bchpn', Bc, decay_states, dtc, xc)
            chunk_total = jnp.transpose(A_cs[..., -1], (0, 2, 1))
            padded = jnp.pad(chunk_total, ((0, 0), (0, 0), (1, 0)))
            decay_chunk = _segsum_exp(padded)
            states_cat = jnp.concatenate([jnp.zeros_like(states[:, :1]), states], axis=1)
            new_states = jnp.einsum('bhzc,bchpn->bzhpn', decay_chunk, states_cat)
            prev = new_states[:, :-1]
            Y_off = jnp.einsum('bcqhn,bchpn,bchq->bcqhp', Cc, prev, jnp.exp(A_cs))
            return (Y_diag + Y_off).reshape(Bz, L, H, P)
        Bz, L, _ = x.shape
        proj = x @ W_in.T
        z = proj[..., :D_INNER]
        xBC = proj[..., D_INNER:D_INNER + CONV_DIM]
        dt_raw = proj[..., D_INNER + CONV_DIM:]
        xBC_t = jnp.transpose(xBC, (0, 2, 1))
        conv = lax.conv_general_dilated(xBC_t, conv_w, (1,), [(D_CONV - 1, 0)], dimension_numbers=('NCH', 'OIH', 'NCH'), feature_group_count=CONV_DIM)
        xBC = jnp.transpose(conv + conv_b[None, :, None], (0, 2, 1))
        xBC = jax.nn.silu(xBC)
        x_ssm = xBC[..., :D_INNER].reshape(Bz, L, NHEADS, HEADDIM)
        B_ssm = xBC[..., D_INNER:D_INNER + NGROUPS * D_STATE].reshape(Bz, L, NGROUPS, D_STATE)
        C_ssm = xBC[..., D_INNER + NGROUPS * D_STATE:].reshape(Bz, L, NGROUPS, D_STATE)
        dt = jax.nn.softplus(dt_raw + dt_bias[None, None, :])
        A = -jnp.exp(A_log)
        y = _ssd_scan(x_ssm, dt, A, B_ssm, C_ssm, CHUNK)
        y = y + x_ssm * D_skip[None, None, :, None]
        y = y.reshape(Bz, L, D_INNER)
        y = y * jax.nn.silu(z)
        return y @ W_out.T

    def _L3_xattn_ref(query, key, value, Wq, bq, Wk, bk, Wv, bv, Wo, bo):
        import jax, jax.numpy as jnp
        import numpy as np
        D_MODEL = 128
        NUM_HEADS = 16
        D_K = D_MODEL // NUM_HEADS
        SCALE = float(np.sqrt(D_K))
        B, Sq, _ = query.shape
        Skv = key.shape[1]

        def proj(x, W, b, S):
            y = jnp.einsum('bsd,ed->bse', x, W) + b
            return y.reshape(B, S, NUM_HEADS, D_K).transpose(0, 2, 1, 3)
        Q = proj(query, Wq, bq, Sq)
        K = proj(key, Wk, bk, Skv)
        V = proj(value, Wv, bv, Skv)
        scores = jnp.einsum('bhqd,bhkd->bhqk', Q, K) / SCALE
        attn = jax.nn.softmax(scores, axis=-1)
        out = jnp.einsum('bhqk,bhkd->bhqd', attn, V)
        out = out.transpose(0, 2, 1, 3).reshape(B, Sq, D_MODEL)
        out = jnp.einsum('bsd,ed->bse', out, Wo) + bo
        return out

    def _L3_ffn_ref(x, gate, corr_bias, w1, w2, fc1_w, fc2_w, up_w, down_w):
        import jax, jax.numpy as jnp
        import numpy as np
        DIM = 128
        LATENT = 64
        INTER = 64
        SHARED = 512
        E = 8
        TOPK = 2
        NGROUP = 2
        TOPKG = 1
        NORM_TOPK = True
        SCALE = 1.0
        B, S = (2, 128)

        def relu2(x):
            r = jnp.maximum(x, 0.0)
            return r * r
        Bv, Sv, D = x.shape
        xf = x.reshape(-1, D)
        N = xf.shape[0]
        scores = jax.nn.sigmoid(xf.astype(jnp.float32) @ gate.T)
        sfc = scores + corr_bias
        gs = E // NGROUP
        if NGROUP > 1:
            group_scores = jax.lax.top_k(sfc.reshape(N, NGROUP, gs), 2)[0].sum(-1)
            gidx = jax.lax.top_k(group_scores, TOPKG)[1]
            gmask = jnp.zeros((N, NGROUP), sfc.dtype).at[jnp.arange(N)[:, None], gidx].set(1.0)
            smask = jnp.repeat(gmask, gs, axis=1)
            sfc = jnp.where(smask > 0, sfc, 0.0)
        sel = jax.lax.top_k(sfc, TOPK)[1]
        top_scores = jnp.take_along_axis(scores, sel, axis=1)
        if NORM_TOPK:
            top_scores = top_scores / (top_scores.sum(-1, keepdims=True) + 1e-20)
        flat = sel.reshape(-1)
        perm = jnp.argsort(flat, stable=True)
        sorted_eid = flat[perm]
        scores_sorted = top_scores.reshape(-1)[perm]
        tok = perm // TOPK
        lat = xf @ fc1_w.T
        xs = lat[tok]
        out = jnp.zeros_like(xs)
        for e in range(E):
            he = relu2(xs @ w1[e].T) @ w2[e].T
            out = jnp.where((sorted_eid == e)[:, None], he, out)
        out = out * scores_sorted[:, None]
        comb = jnp.zeros((N, LATENT), out.dtype).at[tok].add(out)
        routed = comb @ fc2_w.T * SCALE
        shared = relu2(xf @ up_w.T) @ down_w.T
        return (routed + shared).reshape(Bv, Sv, D)
    x = x + _L0_attn_ref(_layernorm(x, axis=-1), L0_attn_Wq, L0_attn_bq, L0_attn_Wk, L0_attn_bk, L0_attn_Wv, L0_attn_bv, L0_attn_Wo, L0_attn_bo, L0_attn_token_positions)
    x = x + _L0_xattn_ref(_layernorm(x, axis=-1), ctx_1024, ctx_1024, fside_BxSxS2_0, mask_BxSxS2_ik1, L0_xattn_wq_k, L0_xattn_wq_b, L0_xattn_wk_k, L0_xattn_wk_b, L0_xattn_wv_k, L0_xattn_wv_b, L0_xattn_wo_k, L0_xattn_wo_b)
    x = x + _L0_ffn_ref(_layernorm(x, axis=-1), L0_ffn_centroids, L0_ffn_w1, L0_ffn_b1, L0_ffn_w2, L0_ffn_b2, L0_ffn_gamma, L0_ffn_beta)
    x = x + _L1_attn_ref(_layernorm(x, axis=-1), L1_attn_W_q, L1_attn_W_k, L1_attn_W_v, L1_attn_W_o)
    x = x + _L1_xattn_ref(_layernorm(x, axis=-1), ctx_1024, ctx_1024, mask_Bx1xSxS2_ik1, L1_xattn_WQ, L1_xattn_bQ, L1_xattn_WK, L1_xattn_bK, L1_xattn_WV, L1_xattn_bV, L1_xattn_WO, L1_xattn_bO)
    x = x + _L1_ffn_ref(_layernorm(x, axis=-1), L1_ffn_w_gate, L1_ffn_b_gate, L1_ffn_W1, L1_ffn_b1, L1_ffn_W2, L1_ffn_b2)
    x = x + _L2_attn_ref(_layernorm(x, axis=-1), L2_attn_norm_weight, L2_attn_w_qkv, L2_attn_temperature, L2_attn_w_out)
    x = x + _L2_xattn_ref(_layernorm(x, axis=-1), ctx_1024, ctx_1024, L2_xattn_Wq, L2_xattn_Wk, L2_xattn_Wv)
    x = x + _L2_ffn_ref(_layernorm(x, axis=-1), L2_ffn_Wr, L2_ffn_br, L2_ffn_W1, L2_ffn_b1, L2_ffn_W2, L2_ffn_b2)
    x = x + _L3_attn_ref(_layernorm(x, axis=-1), L3_attn_W_in, L3_attn_conv_w, L3_attn_conv_b, L3_attn_A_log, L3_attn_dt_bias, L3_attn_D_skip, L3_attn_W_out)
    x = x + _L3_xattn_ref(_layernorm(x, axis=-1), ctx_1024, ctx_1024, L3_xattn_Wq, L3_xattn_bq, L3_xattn_Wk, L3_xattn_bk, L3_xattn_Wv, L3_xattn_bv, L3_xattn_Wo, L3_xattn_bo)
    x = x + _L3_ffn_ref(_layernorm(x, axis=-1), L3_ffn_gate, L3_ffn_corr_bias, L3_ffn_w1, L3_ffn_w2, L3_ffn_fc1_w, L3_ffn_fc2_w, L3_ffn_up_w, L3_ffn_down_w)
    return x

_drawn_inputs = setup_inputs


def setup_inputs(seed=0):
    import zlib

    import numpy as np

    out = dict(_drawn_inputs(seed))
    spreads = {'L0_attn_bq': (0.0, 0.437),
     'L0_attn_bk': (0.0, 0.487),
     'L0_attn_bv': (0.0, 0.1),
     'L0_attn_bo': (0.0, 0.1),
     'L0_xattn_wq_b': (0.0, 0.575),
     'L0_xattn_wk_b': (0.0, 0.8),
     'L0_xattn_wv_b': (0.0, 0.1),
     'L0_xattn_wo_b': (0.0, 0.1),
     'L0_ffn_b1': (0.0, 0.8),
     'L0_ffn_b2': (0.0, 0.327),
     'L0_ffn_gamma': (1.0, 0.6),
     'L0_ffn_beta': (0.0, 0.8),
     'L1_xattn_bQ': (0.0, 0.8),
     'L1_xattn_bK': (0.0, 0.8),
     'L1_xattn_bV': (0.0, 0.1),
     'L1_xattn_bO': (0.0, 0.1),
     'L1_ffn_b1': (0.0, 0.8),
     'L1_ffn_b2': (0.0, 0.656),
     'L2_attn_norm_weight': (1.0, 0.6),
     'L2_attn_temperature': (0.0, 0.8),
     'L3_attn_conv_b': (0.0, 0.8),
     'L3_attn_D_skip': (1.0, 0.6),
     'L3_ffn_corr_bias': (0.0, 0.8)}
    factors = {'L1_ffn_b_gate': 8.0,
     'L2_ffn_Wr': 8.0,
     'L2_ffn_br': 8.0,
     'L2_ffn_W1': 8.0,
     'L2_ffn_b1': 8.0,
     'L2_ffn_W2': 8.0,
     'L2_ffn_b2': 8.0,
     'L3_attn_W_in': 8.0,
     'L3_attn_conv_w': 8.0,
     'L3_attn_A_log': 8.0,
     'L3_attn_dt_bias': 8.0,
     'L3_attn_W_out': 8.0,
     'L3_xattn_Wq': 8.0,
     'L3_xattn_bq': 8.0,
     'L3_xattn_Wk': 8.0,
     'L3_xattn_bk': 8.0,
     'L3_xattn_Wv': 8.0,
     'L3_xattn_bv': 8.0,
     'L3_xattn_Wo': 8.0,
     'L3_xattn_bo': 8.0,
     'L3_ffn_gate': 8.0,
     'L3_ffn_w1': 8.0,
     'L3_ffn_w2': 8.0,
     'L3_ffn_fc1_w': 8.0,
     'L3_ffn_fc2_w': 8.0,
     'L3_ffn_up_w': 8.0,
     'L3_ffn_down_w': 8.0}
    for name, (base, spread) in spreads.items():
        noise = np.random.default_rng([zlib.crc32(name.encode()), seed]).standard_normal(out[name].shape)
        drawn = base * np.exp(spread * noise) if base else spread * noise
        out[name] = jnp.asarray(drawn.astype(out[name].dtype))
    for name, factor in factors.items():
        out[name] = (out[name] * factor).astype(out[name].dtype)
    return out
```

```python
from contextlib import ExitStack

import concourse.bass as bass
import numpy as np
from concourse import mybir

F32 = mybir.dt.float32
BF16 = mybir.dt.bfloat16
I32 = mybir.dt.int32
ALU = mybir.AluOpType
ACT = mybir.ActivationFunctionType
AX = mybir.AxisListType.X

P = 128
B, S, D = 8, 256, 128
NSEQ = 2
NPASS = B // NSEQ
NT = NSEQ * S
T = NT // P
TS = S // P
H, DH = 16, 8
E, F = 8, 512
FC = F // P
TAPS = 4
EPS = 1e-5
BIG = 2.0 ** 100

Q_PARTS = (0, 1, 2, 0, 1, 0)
K_PARTS = (0, 0, 0, 1, 1, 2)
Q_RUNS = ((0, 3, 1), (3, 2, 1), (5, 1, 1))
K_RUNS = ((0, 3, 0), (3, 2, 0), (5, 1, 0))
NSTACK = len(Q_PARTS) * DH
NMAX = 3


ATTN = ("L0a", "L0x", "L1a", "L1x", "L3x")
STAGES = ("L0a", "L0x", "L0f", "L1a", "L1x", "L1f", "L2a", "L2x", "L2f", "L3a", "L3x", "L3f")

COMMON = [("ident", P), ("neg_q", P), ("neg_k", P), ("rope_cos", S), ("rope_sin", S), ("tri", P), ("ones", P),
          ("countdown", E)]
WEIGHTS = {st: [(f"{st}_{n}", k) for n, k in (
    ("wq", P), ("wqs", P), ("wk", P), ("wks", P), ("wv", P), ("wo", P),
    ("bq", 1), ("bqs", 1), ("bk", 1), ("bks", 1), ("bv", P), ("bo", P))] for st in ATTN}
WEIGHTS["L0f"] = [("L0_gate", E), ("L0_b1", E * FC), ("L0_b2", P), ("L0_gamma", E), ("L0_beta", E)]
WEIGHTS["L1f"] = [("L1_gate", E), ("L1_gate_bias", E), ("L1_b1", E * FC), ("L1_b2", P)]
WEIGHTS["L2f"] = [("L2_gate", E), ("L2_gate_bias", E), ("L2_b1", E * FC), ("L2_b2", P)]
WEIGHTS["L2a"] = [("L2a_qkv", 3 * P), ("L2a_out", P), ("L2a_norm", 1), ("L2a_temp", 1), ("block_diag", P)]
WEIGHTS["L2x"] = [("L2x_q", P), ("L2x_qs", P), ("L2x_k", P), ("L2x_ks", P), ("L2x_v", P),
                  ("xq_cos", S), ("xq_sin", S), ("xk_cos", S), ("xk_sin", S), ("decay0", S)]
WEIGHTS["L3a"] = [("L3a_z", 2 * P), ("L3a_xs", 2 * P), ("L3a_b", 64), ("L3a_c", 64), ("L3a_dt", 2),
                  ("L3a_taps_xs", TAPS * 2 * P), ("L3a_taps_b", TAPS * 64), ("L3a_taps_c", TAPS * 64),
                  ("L3a_bias_xs", 2), ("L3a_bias_b", 1), ("L3a_bias_c", 1), ("L3a_alog", 2), ("L3a_dtb", 2),
                  ("L3a_skip", 2), ("L3a_out", 2 * P)]
WEIGHTS["L3f"] = [("L3f_gate", E), ("L3f_corr", E), ("L3f_fc1", P), ("L3f_w1", E * 64), ("L3f_w2", 4 * P),
                  ("L3f_fc2", P), ("L3f_up", 4 * P), ("L3f_down", 4 * P), ("pick_pairs", 4 * P)]


def ranges(pairs):
    out, at = {}, 0
    for name, n in pairs:
        out[name] = (at, at + n)
        at += n
    return out


COLS = {}
for _pairs in (COMMON, *WEIGHTS.values()):
    COLS.update(ranges(_pairs))
width = lambda pairs: sum(n for _, n in pairs)
STAGE_COLS = max(width(pairs) for pairs in WEIGHTS.values())

SEMS = """x_in w_in stage_w ffn_w0 ffn_w1 ffn_w2 ctx_tok ctx_psum ctx_done setup out_done
ln_mv ln_r0 xn_ready xT_psum xT_ready xh_ready xhT_psum xhT_ready
kv_ready q_psum k_psum v_psum v_ready
q_p1 q_rest q_p2 q_p3 q_full k_p1 k_rest k_p2 k_p3 k_full
q_bounce k_bounce q_stack k_stack m_bounce m_stack0 m_stack1 mask_in mask_ready gp_in
s_psum s_max m_parts mT_psum mT_ready st_psum p_ready pg_ready pv_done o_ready
tr_psum a_ready aT_psum aT_ready y_psum xb_ready
gate_psum gate_mask maskT_psum maskT_ready gexp_in gexp_out he_ready z_psum h_raw g_psum h_ready h_used
yT_psum yT_ready a_in a_out b_in b_out c_in c_out d_in d_out e_in e_out f_in f_out
dve_step act_step pool_step
iter_done go_pe go_act go_dve go_pool""".split()
KEEP = ("x_in", "w_in", "stage_w", "ffn_w0", "ffn_w1", "ffn_w2", "ctx_tok", "ctx_psum", "ctx_done", "setup", "out_done",
        "go_pe", "go_act", "go_dve", "go_pool")


class Step:

    def __init__(self, eng, sem):
        self.eng, self.sem, self.n = eng, sem, 0

    def mark(self, ins):
        self.n += 1
        return ins.then_inc(self.sem, 1)

    def __call__(self, ins):
        self.mark(ins)
        self.eng.wait_ge(self.sem, self.n)


class Core:

    def __init__(self, nc, ctx, dram):
        self.nc, self.dram = nc, dram
        self.sem = {n: ctx.enter_context(nc.semaphore(n)) for n in SEMS}
        sb = lambda name, shape, dt=F32: ctx.enter_context(nc.sbuf_tensor(name, shape, dt))
        self.X = sb("X", [P, B * TS, D])
        self.ctxT = sb("ctxT", [P, B * S])
        self.W = sb("W", [P, width(COMMON)])
        self.stage_W = [sb(f"stage_W{k}", [P, STAGE_COLS]) for k in range(2)]
        self.at = 0
        self.ffn = [[sb(f"ffn_w{n}_{k}", [P, E * F]) for n in (1, 2)] for k in range(2)]
        self.ident_b = sb("ident_b", [P, P], BF16)
        self.neg_q = sb("neg_q", [P, P], BF16)
        self.neg_k = sb("neg_k", [P, P], BF16)
        self.pick = sb("pick", [P, E * P], BF16)
        self.n_setup = 0
        self.PS = ctx.enter_context(nc.psum_tensor("PS", [P, 8, 512], F32))

    def buffers(self, stack):
        st = STAGES[self.at]
        return lambda name, shape, dt=F32: stack.enter_context(self.nc.sbuf_tensor(f"{st}_{name}", shape, dt))

    def w(self, name, rows=P):
        a, b = COLS[name]
        src = self.W if name in dict(COMMON) else self.stage_W[self.at % 2]
        return src[0:rows, a:b]


def load_next_weights(core, sp):
    if core.at + 1 < len(STAGES):
        st = STAGES[core.at + 1]
        sp.dma_start(core.stage_W[(core.at + 1) % 2][:, 0:width(WEIGHTS[st])], core.dram[f"small_{st}"])\
            .then_inc(core.sem["stage_w"], 16)


def await_next_weights(core, sp):
    if core.at + 1 < len(STAGES):
        sp.wait_ge(core.sem["stage_w"], 16 * (core.at + 2))


def end_pass(core, eng, go):
    eng.drain().then_inc(core.sem["iter_done"], 1)
    eng.wait_ge(core.sem[go], 1)
    eng.sem_clear(core.sem[go])


def end_pass_sync(core, sp):
    sp.wait_ge(core.sem["iter_done"], 4)
    for name in SEMS:
        if name not in KEEP:
            sp.sem_clear(core.sem[name])
    for go in ("go_pe", "go_act", "go_dve", "go_pool"):
        sp.sem_inc(core.sem[go], 1)


def ln_buffers(core, c):
    sb = core.buffers(c)
    return dict(st=sb("ln_st", [P, T, 6]), mv=sb("ln_mv_", [P, 2, T, 2]), lnv=sb("ln_lnv", [P, 2, T]),
                r0=sb("ln_r0_", [P, 2, T]), sq=sb("ln_sq", [P, 2, T]), w=sb("ln_w", [P, 2, T]),
                r=sb("ln_r", [P, 2, T]), xn=sb("xn", [P, T, D]), xT=sb("xT", [P, NT]))


def tokens_of(core, it):
    return core.X[:, bass.ds(it * T, T), :]


def tile_of(core, it, t):
    return core.X[:, bass.ds(it * T + t, 1), :].rearrange("p a d -> p (a d)")


def dve_layernorm(core, dve, step, L, src, dst, ready, n=0, rms=False, eps=EPS):
    v, s = core.nc.vector, core.sem
    mv, u = L["mv"][:, n], L["sq"][:, n]
    for t in range(T):
        last = step.mark(v.bn_stats(L["st"][:, t, :], src(t)))
    dve.wait_ge(s["dve_step"], step.n)
    for t in range(T):
        last = step.mark(v.bn_aggr(mv[:, t, :], L["st"][:, t, :]))
    dve.wait_ge(s["dve_step"], step.n)
    if rms:
        step(v.tensor_tensor(u, mv[:, :, 0], mv[:, :, 0], ALU.mult))
        step(v.tensor_tensor(mv[:, :, 1], mv[:, :, 1], u, ALU.add))
    step(v.tensor_scalar(L["w"][:, n], mv[:, :, 1], eps, None, ALU.add))
    v.tensor_copy(L["r"][:, n], L["w"][:, n]).then_inc(s["ln_mv"], 1)
    dve.wait_ge(s["ln_r0"], n + 1)
    step(v.tensor_tensor(u, L["r0"][:, n], L["r0"][:, n], ALU.mult))
    step(v.tensor_tensor(u, u, L["w"][:, n], ALU.mult))
    step(v.tensor_scalar(u, u, -0.5, 1.5, ALU.mult, ALU.add))
    dve.wait_ge(s["ln_mv"], n + 1)
    step(v.tensor_tensor(L["r"][:, n], L["r0"][:, n], u, ALU.mult))
    for t in range(T):
        if rms:
            v.tensor_scalar(dst[:, t, :], src(t), L["r"][:, n, t:t + 1], None, ALU.mult)\
                .then_inc(ready, 1)
        else:
            v.tensor_scalar(dst[:, t, :], src(t), mv[:, t, 0:1], L["r"][:, n, t:t + 1],
                            ALU.subtract, ALU.mult).then_inc(ready, 1)


def act_layernorm(core, act, step, L, n=0):
    a, s = core.nc.scalar, core.sem
    act.wait_ge(s["ln_mv"], n + 1)
    step(a.activation(L["lnv"][:, n], L["r"][:, n], ACT.Ln))
    a.activation(L["r0"][:, n], L["lnv"][:, n], ACT.Exp, scale=-0.5).then_inc(s["ln_r0"], 1)


def pe_turn(core, pe, src, bank, ready, done, tiles=T):
    for t in range(tiles):
        pe.wait_ge(ready, t + 1)
        ins = core.nc.tensor.transpose(core.PS[:, bank, t * P:(t + 1) * P], src[:, t, :], core.w("ident"))
    ins.then_inc(done, 1)


def act_copy(core, act, out, src, wait, n, done):
    act.wait_ge(wait, n)
    core.nc.scalar.activation(out, src, ACT.Copy).then_inc(done, 1)


def dve_residual(core, dve, it, add, wait, base=None):
    dve.wait_ge(wait, 1)
    x = tokens_of(core, it)
    core.nc.vector.tensor_tensor(x, add.rearrange("p (t d) -> p t d", t=T), x if base is None else base, ALU.add)


def attention(core, st):
    nc, s, PS, w = core.nc, core.sem, core.PS, core.w
    rope = st in ("L0a", "L1a")
    causal = rope
    masked = st in ("L0x", "L1x")
    gated = st == "L0x"
    cross = not rope
    bias = st != "L1a"
    SCALE = float(1.0 / np.sqrt(np.float32(DH)))
    HP = H // 2
    NG = H // 4
    RING = 3

    with ExitStack() as c:
        sb = core.buffers(c)
        L = ln_buffers(core, c)
        Qm = core.Qm = sb("Qm", [P, 2, HP, NT], BF16)
        Kst = sb("Kst", [P, HP, NT], BF16)
        vaug = sb("vaug", [P, T, H, 32])
        Pr = sb("Pr", [P, RING, 4 * S])
        Osb = sb("Osb", [P, NSEQ, NG, S])
        qpart = sb("qpart", [P, 3, NT], BF16)
        kpart = sb("kpart", [P, 3, NT], BF16)
        tmp = {n: sb(f"{n}_tmp", [P, 3, NT]) for n in ("q", "k")} if rope else None
        rest = {n: sb(f"{n}_rest", [P, NT]) for n in ("q", "k")}
        mx = sb("mx", [P, NSEQ, TS, H])
        mrest = sb("mrest", [P, NSEQ, TS, H])
        mpart = sb("mpart", [P, T, NMAX, H], BF16)
        mT = sb("mT", [NMAX * H, NT], BF16)
        rden = sb("rden", [P, T, H])
        A, AT = L["xn"], L["xT"]
        Xb = sb("Xb", [P, T, D]) if bias else None
        kvT = sb("kvT", [P, NT]) if cross else L["xT"]
        if masked:
            msk = sb("msk", [P, 2, T, S], I32)
            neg = sb("neg", [P, 2, T, S], BF16)
        if gated:
            G = sb("G", [P, T, S])
            PG = sb("PG", [P, 2, 4 * S])
            den = sb("den", [P, 32])

        units_s = [(b, tt, g) for b in range(NSEQ) for tt in range(TS) for g in range(NG)]
        units_t = [(b, kt, g) for b in range(NSEQ) for kt in range(TS) for g in range(NG)]
        NU = len(units_s)
        PER = TS * NG

        core.n_setup += 5 if gated else 4

        with nc.Block() as block:

            @block.sync
            def _(sp):
                sp.wait_ge(s["setup"], core.n_setup)
                load_next_weights(core, sp)
                with sp.Fori(0, NPASS) as it:
                    if masked:
                        name = "mask0" if st == "L0x" else "mask1"
                        for k in range(2):
                            sp.dma_start(msk[:, k, :, :], core.dram[name + "qk"[k]][bass.ds(it * NSEQ, NSEQ)]
                                         .rearrange("b (t p) k -> p (b t) k", p=P)).then_inc(s["mask_in"], 16)
                    if gated:
                        sp.dma_start(G[:, :, :], core.dram["gate_prob"][bass.ds(it * NSEQ, NSEQ)]
                                     .rearrange("b (t p) k -> p (b t) k", p=P)).then_inc(s["gp_in"], 16)
                    for what, parts, src, runs in (("k", K_PARTS, kpart, K_RUNS), ("q", Q_PARTS, qpart, Q_RUNS)):
                        sp.wait_ge(s[what + "_p3"], 1)
                        sp.wait_ge(s[what + "_p2"], 1)
                        bounce = core.dram[what + "_bounce"]
                        for par in range(2):
                            for i, n, stride in runs:
                                rows = src[64 * par:64 * par + 64, :, :]
                                rows = (rows[:, parts[i]:parts[i] + n, :] if stride else
                                        rows[:, parts[i]:parts[i] + 1, :].broadcast_to([64, n, NT]))
                                sp.dma_start(bounce[par, i:i + n].rearrange("c r t -> r c t"), rows)\
                                    .then_inc(s[what + "_bounce"], 16)
                    for what, runs in (("k", K_RUNS), ("q", Q_RUNS)):
                        sp.wait_ge(s[what + "_bounce"], 16 * 2 * len(runs))
                        for par in range(2):
                            rows = slice(64 * par, 64 * par + NSTACK)
                            d = Kst[rows, :, :] if what == "k" else Qm[rows, par, :, :]
                            sp.dma_start(d, core.dram[what + "_bounce"][par].rearrange(
                                "c (d p) t -> (c d) p t", p=HP)).then_inc(s[what + "_stack"], 16)
                    for b in range(NSEQ):
                        sp.wait_ge(s["mT_ready"], b + 1)
                        cols = slice(b * S, (b + 1) * S)
                        sp.dma_start(core.dram["m_bounce"][:, cols], mT[:, cols]).then_inc(s["m_bounce"], 16)
                        sp.wait_ge(s["m_bounce"], 16 * (b + 1))
                        for par in range(2):
                            sp.dma_start(
                                Qm[64 * par + NSTACK:64 * par + NSTACK + NMAX, par, :, cols],
                                core.dram["m_bounce"].rearrange("(c r p) t -> r c p t", c=NMAX, r=2)[par][:, :, cols],
                            ).then_inc(s[f"m_stack{b}"], 16)
                    for name in ("q_stack", "k_stack", "m_stack0", "m_stack1"):
                        sp.wait_ge(s[name], 32)
                    end_pass_sync(core, sp)
                await_next_weights(core, sp)

            @block.gpsimd
            def _(pool):
                nc.gpsimd.memset(Qm[:, :, :, :], 0.0).then_inc(s["setup"], 1)
                nc.gpsimd.memset(Kst[:, :, :], -1.0).then_inc(s["setup"], 1)
                nc.gpsimd.memset(vaug[:, :, :, DH + 1:32], 0.0).then_inc(s["setup"], 1)
                nc.gpsimd.memset(vaug[:, :, :, DH:DH + 1], 0.0 if gated else 1.0).then_inc(s["setup"], 1)
                if gated:
                    nc.gpsimd.tensor_scalar(den[:, :], w("ones")[:, 0:32], 0.0, None, ALU.mult)\
                        .then_inc(s["pool_step"], 1)
                    pool.wait_ge(s["pool_step"], 1)
                    nc.gpsimd.memset(den[:, DH:DH + 1], 1.0).then_inc(s["setup"], 1)
                with pool.Fori(0, NPASS) as it:
                    if cross:
                        nc.gpsimd.tensor_copy(kvT[:, :], core.ctxT[:, bass.ds(it * NT, NT)]).then_inc(s["kv_ready"], 1)
                    if bias:
                        for t in range(T):
                            nc.gpsimd.tensor_tensor(Xb[:, t, :], tile_of(core, it, t), w(f"{st}_bo"),
                                                    ALU.add).then_inc(s["xb_ready"], 1)
                    if masked:
                        pool.wait_ge(s["mask_in"], 32)
                        for k in range(2):
                            if st == "L1x":
                                nc.gpsimd.tensor_scalar(neg[:, k], msk[:, k], 0.0, -BIG, ALU.is_equal,
                                                        ALU.mult).then_inc(s["mask_ready"], 1)
                            else:
                                nc.gpsimd.tensor_scalar(neg[:, k], msk[:, k], 2.0 ** 31, -2.0 ** 31, ALU.mult,
                                                        ALU.add).then_inc(s["mask_ready"], 1)
                    end_pass(core, pool, "go_pool")

            @block.tensor
            def _(pe):
                mm, tr = nc.tensor.matmul, nc.tensor.transpose
                free = dict(skip_group_check=True)
                pe.wait_ge(s["setup"], core.n_setup)
                with pe.Fori(0, NPASS) as it:
                    pe_turn(core, pe, L["xn"], 7, s["xn_ready"], s["xT_psum"])
                    if cross:
                        pe.wait_ge(s["kv_ready"], 1)
                    else:
                        pe.wait_ge(s["xT_ready"], 1)
                    if rope:
                        mm(PS[:, 3, :], w(f"{st}_wks"), kvT[:, :], start=True, stop=True)
                    mm(PS[:, 2, :], w(f"{st}_wk"), kvT[:, :], start=True, stop=True).then_inc(s["k_psum"], 1)
                    pe.wait_ge(s["xT_ready"], 1)
                    if rope:
                        mm(PS[:, 1, :], w(f"{st}_wqs"), L["xT"][:, :], start=True, stop=True)
                    mm(PS[:, 0, :], w(f"{st}_wq"), L["xT"][:, :], start=True, stop=True).then_inc(s["q_psum"], 1)
                    for t in range(T):
                        ins = mm(PS[:, 4, t * P:(t + 1) * P], kvT[:, t * P:(t + 1) * P], w(f"{st}_wv"),
                                 start=(t == 0), stop=True, **free)
                    ins.then_inc(s["v_psum"], 1)

                    def turn_max(b):
                        pe.wait_ge(s["m_parts"], b + 1)
                        for tt in range(TS):
                            t = b * TS + tt
                            ins = tr(PS[0:NMAX * H, 6 + b, tt * 64:tt * 64 + 64].bitcast(BF16),
                                     mpart[:, t].rearrange("p c h -> p (c h)"), core.ident_b[:, :])
                        ins.then_inc(s["mT_psum"], 1)

                    pe.wait_ge(s["k_stack"], 32)
                    pe.wait_ge(s["q_stack"], 32)
                    for u, (b, tt, g) in enumerate(units_s):
                        bank = 2 * (u % RING)
                        if u >= RING:
                            pe.wait_ge(s["s_max"], u - RING + 1)
                        if u == 2:
                            pe.wait_ge(s["v_ready"], 1)
                        if masked and u == 0:
                            pe.wait_ge(s["mask_ready"], 2)
                        nk = (tt + 1) * P if causal else S
                        q0 = b * S + tt * P
                        for pp in range(2):
                            for par in range(2):
                                rows = slice(64 * par, 64 * par + NSTACK)
                                ins = mm(PS[:, bank + par, pp * S:pp * S + nk], Qm[rows, par, 2 * g + pp, q0:q0 + P],
                                         Kst[rows, 2 * g + pp, b * S:b * S + nk], start=(pp == 0), stop=True, **free)
                        for par in range(2):
                            o = PS[:, bank + par, :].rearrange("p (a k) -> p a k", a=2)
                            if causal:
                                ins = mm(o[:, :, tt * P:tt * P + P], core.ident_b[:, :],
                                         core.neg_q[:, :].unsqueeze(1).broadcast_to([P, 2, P]),
                                         start=False, stop=True, **free)
                            if masked:
                                ins = mm(o, core.ident_b[:, :],
                                         neg[:, 0, b * TS + tt].unsqueeze(1).broadcast_to([P, 2, S]),
                                         start=False, stop=True, **free)
                        ins.then_inc(s["s_psum"], 1)
                        if b == 1 and u == PER + 2:
                            turn_max(0)
                    turn_max(1)

                    def times_v(v):
                        b, kt, g = units_t[v]
                        pe.wait_ge(s["p_ready"], v + 1)
                        if gated:
                            pe.wait_ge(s["pg_ready"], v + 1)
                        if b == 0 and kt == 0 and g == 0:
                            pe.wait_ge(s["mT_ready"], 2)
                        if b == 1 and kt == 0 and g == 0:
                            pe.wait_ge(s["o_ready"], 1)
                        q0 = kt * P if causal else 0
                        nq = S - q0
                        for j in range(4):
                            h = 4 * g + j
                            o = PS[32 * j:32 * j + 32, 6 + g // 2, (g % 2) * S + q0:(g % 2) * S + S]
                            opening = kt == 0 and g % 2 == 0
                            if gated:
                                ins = mm(o, vaug[:, b * TS + kt, h, :], PG[:, v % 2, j * nq:(j + 1) * nq],
                                         start=opening, stop=True, **free)
                                ins = mm(o, den[:, :], Pr[:, v % RING, j * nq:(j + 1) * nq],
                                         start=False, stop=True, **free)
                            else:
                                ins = mm(o, vaug[:, b * TS + kt, h, :], Pr[:, v % RING, j * nq:(j + 1) * nq],
                                         start=opening, stop=True, **free)
                        ins.then_inc(s["pv_done"], 1)

                    pe.wait_ge(s["s_max"], NU)
                    for v, (b, kt, g) in enumerate(units_t):
                        bank = 2 * (v % RING)
                        if kt == 0 and g == 0:
                            pe.wait_ge(s[f"m_stack{b}"], 32)
                        if v >= RING:
                            pe.wait_ge(s["p_ready"], v - RING + 1)
                        q0 = kt * P if causal else 0
                        nq = S - q0
                        k0 = b * S + kt * P
                        for pp in range(2):
                            o = PS[:, bank + pp, 0:2 * nq].rearrange("p (a q) -> p a q", a=2)
                            ins = mm(o, Kst[:, 2 * g + pp, k0:k0 + P], Qm[:, :, 2 * g + pp, b * S + q0:b * S + S],
                                     start=True, stop=True, **free)
                            if causal:
                                ins = mm(o[:, :, 0:P], core.ident_b[:, :],
                                         core.neg_k[:, :].unsqueeze(1).broadcast_to([P, 2, P]),
                                         start=False, stop=True, **free)
                            if masked:
                                ins = mm(o, core.ident_b[:, :],
                                         neg[:, 1, b * TS + kt].unsqueeze(1).broadcast_to([P, 2, S]),
                                         start=False, stop=True, **free)
                        ins.then_inc(s["st_psum"], 1)
                        if v >= 1:
                            times_v(v - 1)
                    times_v(NU - 1)

                    for t in range(T):
                        b, tt = t // TS, t % TS
                        pe.wait_ge(s["o_ready"], b + 1)
                        for g in range(NG):
                            ins = tr(PS[:, t, g * P:(g + 1) * P], Osb[:, b, g, tt * P:(tt + 1) * P], w("ident"))
                        ins.then_inc(s["tr_psum"], 1)
                    pe_turn(core, pe, A, 4, s["a_ready"], s["aT_psum"])
                    pe.wait_ge(s["aT_ready"], 1)
                    for t in range(T):
                        ins = mm(PS[:, 5, t * P:(t + 1) * P], AT[:, t * P:(t + 1) * P], w(f"{st}_wo"),
                                 start=(t == 0), stop=True, **free)
                    ins.then_inc(s["y_psum"], 1)
                    end_pass(core, pe, "go_pe")

            @block.scalar
            def _(act):
                a = nc.scalar.activation
                with act.Fori(0, NPASS) as it:
                    step = Step(act, s["act_step"])
                    act_layernorm(core, act, step, L)
                    act_copy(core, act, L["xT"][:, :], PS[:, 7, :], s["xT_psum"], 1, s["xT_ready"])
                    for what, bank, part in (("k", 2, kpart), ("q", 0, qpart)):
                        if rope:
                            act.wait_ge(s[what + "_full"], 1)
                            a(part[:, 0, :], tmp[what][:, 2, :], ACT.Copy).then_inc(s[what + "_p1"], 1)
                        else:
                            act.wait_ge(s[what + "_psum"], 1)
                            a(part[:, 0, :], PS[:, bank, :], ACT.Identity, bias=w(f"{st}_b{what}"))\
                                .then_inc(s[what + "_p1"], 1)
                    for what, part in (("k", kpart), ("q", qpart)):
                        act.wait_ge(s[what + "_rest"], 1)
                        a(part[:, 1, :], rest[what][:, :], ACT.Copy).then_inc(s[what + "_p2"], 1)
                    for b in range(NSEQ - 1):
                        act.wait_ge(s["mT_psum"], b + 1)
                        a(mT[:, b * S:(b + 1) * S], PS[0:NMAX * H, 6 + b, 0:P].bitcast(BF16), ACT.Copy)\
                            .then_inc(s["mT_ready"], 1)
                    act.wait_ge(s["mT_psum"], 2)
                    a(mT[:, S:2 * S], PS[0:NMAX * H, 7, 0:P].bitcast(BF16), ACT.Copy).then_inc(s["mT_ready"], 1)
                    for v, (b, kt, g) in enumerate(units_t):
                        act.wait_ge(s["st_psum"], v + 1)
                        if v >= RING:
                            act.wait_ge(s["pv_done"], v - RING + 1)
                        nq = S - kt * P if causal else S
                        a(Pr[:, v % RING, 0:4 * nq].rearrange("p (a k) -> p a k", a=2),
                          PS[:, 2 * (v % RING):2 * (v % RING) + 2, 0:2 * nq], ACT.Exp, scale=SCALE)\
                            .then_inc(s["p_ready"], 1)
                    act_copy(core, act, AT[:, :], PS[:, 4, :], s["aT_psum"], 1, s["aT_ready"])
                    end_pass(core, act, "go_act")

            @block.vector
            def _(dve):
                v = nc.vector
                with dve.Fori(0, NPASS) as it:
                    step = Step(dve, s["dve_step"])
                    dve_layernorm(core, dve, step, L, lambda t: tile_of(core, it, t), L["xn"], s["xn_ready"])
                    two = lambda ap: ap.rearrange("p (b t) -> p b t", b=NSEQ)
                    for what, bank, part in (("k", 2, kpart), ("q", 0, qpart)):
                        dve.wait_ge(s[what + "_psum"], 1)
                        if rope:
                            for i, (tab, bs) in enumerate((("rope_cos", ""), ("rope_sin", "s"))):
                                step.mark(v.scalar_tensor_tensor(
                                    two(tmp[what][:, i, :]), two(PS[:, bank + i, :]), w(f"{st}_b{what}{bs}"),
                                    w(tab).unsqueeze(1).broadcast_to([P, NSEQ, S]), ALU.add, ALU.mult))
                            dve.wait_ge(s["dve_step"], step.n)
                            v.tensor_tensor(tmp[what][:, 2, :], tmp[what][:, 0, :], tmp[what][:, 1, :], ALU.add)\
                                .then_inc(s[what + "_full"], 1)
                    for what, bank, part in (("k", 2, kpart), ("q", 0, qpart)):
                        dve.wait_ge(s[what + "_p1"], 1)
                        if rope:
                            v.tensor_tensor(rest[what][:, :], tmp[what][:, 2, :], part[:, 0, :], ALU.subtract)\
                                .then_inc(s[what + "_rest"], 1)
                        else:
                            v.scalar_tensor_tensor(rest[what][:, :], PS[:, bank, :], w(f"{st}_b{what}"),
                                                   part[:, 0, :], ALU.add, ALU.subtract)\
                                .then_inc(s[what + "_rest"], 1)
                    for what, part in (("k", kpart), ("q", qpart)):
                        dve.wait_ge(s[what + "_p2"], 1)
                        v.tensor_tensor(part[:, 2, :], rest[what][:, :], part[:, 1, :], ALU.subtract)\
                            .then_inc(s[what + "_p3"], 1)
                    dve.wait_ge(s["v_psum"], 1)
                    for t in range(T):
                        ins = v.tensor_tensor(
                            vaug[:, t, :, 0:DH], PS[:, 4, t * P:(t + 1) * P].rearrange("p (h d) -> p h d", h=H),
                            w(f"{st}_bv").rearrange("p (h d) -> p h d", h=H), ALU.add)
                    ins.then_inc(s["v_ready"], 1)
                    for u, (b, tt, g) in enumerate(units_s):
                        dve.wait_ge(s["s_psum"], u + 1)
                        nk = (tt + 1) * P if causal else S
                        bank = 2 * (u % RING)
                        o = mx[:, b, tt, :].rearrange("p (r a) -> p r a", r=2)[:, :, 2 * g:2 * g + 2]
                        v.tensor_reduce(o, PS[:, bank:bank + 2, :].rearrange("p r (a k) -> p r a k", a=2)[:, :, :, 0:nk],
                                        AX, ALU.max).then_inc(s["s_max"], 1)
                        if u % PER == PER - 1:
                            dve.wait_ge(s["s_max"], u + 1)
                            part = mpart[:, b * TS:(b + 1) * TS]
                            step(v.tensor_copy(part[:, :, 0, :], mx[:, b]))
                            step(v.tensor_tensor(mrest[:, b], mx[:, b], part[:, :, 0, :], ALU.subtract))
                            step(v.tensor_copy(part[:, :, 1, :], mrest[:, b]))
                            v.tensor_tensor(part[:, :, 2, :], mrest[:, b], part[:, :, 1, :], ALU.subtract)\
                                .then_inc(s["m_parts"], 1)

                    def take_out(b):
                        dve.wait_ge(s["pv_done"], PER * (b + 1))
                        v.tensor_copy(Osb[:, b].rearrange("p g q -> p (g q)"),
                                      PS[:, 6:8, :].rearrange("p a q -> p (a q)")).then_inc(s["o_ready"], 1)

                    for x, (b, kt, g) in enumerate(units_t):
                        if gated:
                            dve.wait_ge(s["p_ready"], x + 1)
                            if x >= 2:
                                dve.wait_ge(s["pv_done"], x - 1)
                            if x == 0:
                                dve.wait_ge(s["gp_in"], 16)
                            v.tensor_tensor(PG[:, x % 2, :].rearrange("p (h q) -> p h q", h=4),
                                            Pr[:, x % RING, :].rearrange("p (h q) -> p h q", h=4),
                                            G[:, b * TS + kt, :].unsqueeze(1).broadcast_to([P, 4, S]), ALU.mult)\
                                .then_inc(s["pg_ready"], 1)
                        if x % PER == PER - 1:
                            take_out(b)
                    for t in range(T):
                        dve.wait_ge(s["tr_psum"], t + 1)
                        o = PS[:, t, :].rearrange("p (h r) -> p h r", r=32)
                        step(v.reciprocal(rden[:, t, :].unsqueeze(2), o[:, :, DH:DH + 1]))
                        v.tensor_tensor(A[:, t, :].rearrange("p (h d) -> p h d", h=H), o[:, :, 0:DH],
                                        rden[:, t, :].unsqueeze(2).broadcast_to([P, H, DH]), ALU.mult)\
                            .then_inc(s["a_ready"], 1)
                    if bias:
                        dve.wait_ge(s["xb_ready"], T)
                    dve_residual(core, dve, it, PS[:, 5, :], s["y_psum"], Xb[:, :, :] if bias else None)
                    end_pass(core, dve, "go_dve")


def experts(core, st):
    nc, s, PS, w = core.nc, core.sem, core.PS, core.w
    slot = {"L0f": 0, "L1f": 1, "L2f": 0}[st]
    ly = st[:2]
    W1 = core.ffn[slot][0][:, :].rearrange("p (e f) -> p e f", e=E)
    W2 = core.ffn[slot][1][:, :].rearrange("p (e c d) -> p e c d", e=E, c=FC)
    two_norms = st == "L0f"
    NK = E * FC
    RING = 3

    with ExitStack() as c:
        sb = core.buffers(c)
        L = ln_buffers(core, c)
        xh = sb("xh", [P, T, D]) if two_norms else None
        xhT = sb("xhT", [P, NT]) if two_norms else L["xT"]
        he = sb("he", [P, 2, NT]) if two_norms else None
        lg, eq, sc, msk = (sb(n, [P, T, E]) for n in ("lg", "eq", "sc", "msk"))
        mx, mc, gain = (sb(n, [P, T]) for n in ("mx", "mc", "gain"))
        mT = sb("mT", [P, NT])
        mTb = sb("mTb", [P, NT], BF16)
        b2 = sb("b2", [P, P])
        hs = sb("hs", [P, RING, NT])
        hm = sb("hm", [P, RING, NT])
        YT = sb("YT", [P, NT])
        core.n_setup += 2

        with nc.Block() as block:

            @block.sync
            def _(sp):
                if st == "L0f":
                    load_ffn(core, sp, "L1", 1)
                if st == "L1f":
                    load_ffn(core, sp, "L2", 0)
                load_next_weights(core, sp)
                with sp.Fori(0, NPASS) as it:
                    end_pass_sync(core, sp)
                await_next_weights(core, sp)

            @block.gpsimd
            def _(pool):
                nc.gpsimd.memset(mT[:, :], 0.0).then_inc(s["setup"], 1)
                nc.gpsimd.memset(mTb[:, :], 0.0).then_inc(s["setup"], 1)
                with pool.Fori(0, NPASS) as it:
                    if two_norms:
                        pool.wait_ge(s["xhT_ready"], 1)
                        for e in range(E):
                            if e >= 2:
                                pool.wait_ge(s["z_psum"], FC * (e - 1))
                            nc.gpsimd.tensor_scalar(he[:, e % 2, :], xhT[:, :], w("L0_gamma")[:, e:e + 1],
                                                    w("L0_beta")[:, e:e + 1], ALU.mult, ALU.add)\
                                .then_inc(s["he_ready"], 1)
                    end_pass(core, pool, "go_pool")

            @block.tensor
            def _(pe):
                mm, tr = nc.tensor.matmul, nc.tensor.transpose
                free = dict(skip_group_check=True)
                pe.wait_ge(s["setup"], core.n_setup)
                pe.wait_ge(s[f"ffn_w{ly[1]}"], 32)
                with pe.Fori(0, NPASS) as it:
                    pe_turn(core, pe, L["xn"], 7, s["xn_ready"], s["xT_psum"])
                    pe.wait_ge(s["xT_ready"], 1)
                    for t in range(T):
                        ins = mm(PS[:, 6, t * E:(t + 1) * E], L["xT"][:, t * P:(t + 1) * P], w(f"{ly}_gate"),
                                 start=(t == 0), stop=True, **free)
                    ins.then_inc(s["gate_psum"], 1)
                    if two_norms:
                        pe_turn(core, pe, xh, 5, s["xh_ready"], s["xhT_psum"])
                    pe.wait_ge(s["gate_mask"], 1)
                    for t in range(T):
                        ins = tr(PS[0:E, 4, t * P:(t + 1) * P], msk[:, t, :], w("ident"))
                    ins.then_inc(s["maskT_psum"], 1)
                    pe.wait_ge(s["maskT_ready"], 2)
                    mm(PS[:, 3, :], w(f"{ly}_b2"), mT[:, :], start=True, stop=False, **free)
                    if two_norms:
                        pe.wait_ge(s["xhT_ready"], 1)

                    def second(k):
                        pe.wait_ge(s["h_ready"], k + 1)
                        ins = mm(PS[:, 3, :], W2[:, k // FC, k % FC, :], hm[:, k % RING, :],
                                 start=False, stop=(k == NK - 1), **free)
                        ins.then_inc(s["h_used"], 1)

                    for k in range(NK):
                        e, ch = k // FC, k % FC
                        if ch == 0:
                            if e >= 2:
                                pe.wait_ge(s["h_ready"], FC * (e - 1))
                            mm(PS[:, 4 + e % 2, :], core.pick[:, e * P:(e + 1) * P], mTb[:, :],
                               start=True, stop=True, **free).then_inc(s["g_psum"], 1)
                            if two_norms:
                                pe.wait_ge(s["he_ready"], e + 1)
                        if k >= RING:
                            pe.wait_ge(s["h_raw"], k - RING + 1)
                        rhs = he[:, e % 2, :] if two_norms else xhT[:, :]
                        mm(PS[:, k % RING, :], W1[:, e, ch * P:(ch + 1) * P], rhs, start=True, stop=True, **free)\
                            .then_inc(s["z_psum"], 1)
                        if k >= 2:
                            second(k - 2)
                    second(NK - 2)
                    second(NK - 1)
                    pe.wait_ge(s["yT_ready"], 1)
                    for t in range(T):
                        ins = tr(PS[:, 7, t * P:(t + 1) * P], YT[:, t * P:(t + 1) * P], w("ident"))
                    ins.then_inc(s["y_psum"], 1)
                    end_pass(core, pe, "go_pe")

            @block.scalar
            def _(act):
                a = nc.scalar.activation
                act.wait_ge(s["setup"], core.n_setup)
                with act.Fori(0, NPASS) as it:
                    step = Step(act, s["act_step"])
                    act_layernorm(core, act, step, L)
                    act_copy(core, act, L["xT"][:, :], PS[:, 7, :], s["xT_psum"], 1, s["xT_ready"])
                    if two_norms:
                        act_layernorm(core, act, step, L, n=1)
                    if st == "L1f":
                        act.wait_ge(s["gexp_in"], 1)
                        a(sc[:, :, :], eq[:, :, :], ACT.Exp).then_inc(s["gexp_out"], 1)
                    if st == "L0f":
                        act.wait_ge(s["gexp_in"], 1)
                        a(gain[:, :], mx[:, :], ACT.Exp, scale=-1.0).then_inc(s["gexp_out"], 1)
                        act_copy(core, act, xhT[:, :], PS[:, 5, :], s["xhT_psum"], 1, s["xhT_ready"])
                    act.wait_ge(s["maskT_psum"], 1)
                    a(mT[0:E, :], PS[0:E, 4, :], ACT.Copy).then_inc(s["maskT_ready"], 1)
                    a(mTb[0:E, :], PS[0:E, 4, :], ACT.Copy).then_inc(s["maskT_ready"], 1)
                    for k in range(NK):
                        act.wait_ge(s["z_psum"], k + 1)
                        if k >= RING:
                            act.wait_ge(s["h_ready"], k - RING + 1)
                        a(hs[:, k % RING, :], PS[:, k % RING, :], ACT.Relu, bias=w(f"{ly}_b1")[:, k:k + 1])\
                            .then_inc(s["h_raw"], 1)
                    act_copy(core, act, YT[:, :], PS[:, 3, :], s["h_used"], NK, s["yT_ready"])
                    end_pass(core, act, "go_act")

            @block.vector
            def _(dve):
                v = nc.vector
                bc = lambda ap: ap.unsqueeze(2).broadcast_to([P, T, E])
                bt = lambda ap: ap.unsqueeze(1).broadcast_to([P, T, E])
                with dve.Fori(0, NPASS) as it:
                    step = Step(dve, s["dve_step"])
                    dve_layernorm(core, dve, step, L, lambda t: tile_of(core, it, t), L["xn"], s["xn_ready"])
                    if two_norms:
                        dve.wait_ge(s["xn_ready"], T)
                        dve_layernorm(core, dve, step, L, lambda t: L["xn"][:, t, :], xh, s["xh_ready"], n=1)
                    dve.wait_ge(s["gate_psum"], 1)
                    logits = PS[:, 6, 0:T * E].rearrange("p (t e) -> p t e", t=T)
                    if ly == "L0":
                        step(v.tensor_copy(lg[:, :, :], logits))
                    else:
                        step(v.tensor_tensor(lg[:, :, :], logits, bt(w(f"{ly}_gate_bias")), ALU.add))
                    step(v.tensor_reduce(mx[:, :], lg[:, :, :], AX, ALU.max))
                    step(v.tensor_tensor(eq[:, :, :], lg[:, :, :], bc(mx[:, :]), ALU.is_equal))
                    step(v.tensor_tensor(sc[:, :, :], eq[:, :, :], bt(w("countdown")), ALU.mult))
                    step(v.tensor_reduce(mc[:, :], sc[:, :, :], AX, ALU.max))
                    v.tensor_tensor(msk[:, :, :], sc[:, :, :], bc(mc[:, :]), ALU.is_equal).then_inc(s["gate_mask"], 1)
                    dve.wait_ge(s["gate_mask"], 1)
                    if st == "L0f":
                        step(v.tensor_scalar(mx[:, :], mx[:, :], -80.0, None, ALU.max))
                        v.tensor_copy(mc[:, :], mx[:, :]).then_inc(s["gexp_in"], 1)
                        dve.wait_ge(s["gexp_out"], 1)
                        dve.wait_ge(s["gexp_in"], 1)
                        step(v.tensor_scalar(gain[:, :], gain[:, :], 1.0, None, ALU.add))
                        step(v.reciprocal(gain[:, :], gain[:, :]))
                    if st == "L1f":
                        v.tensor_tensor(eq[:, :, :], lg[:, :, :], bc(mx[:, :]), ALU.subtract).then_inc(s["gexp_in"], 1)
                        dve.wait_ge(s["gexp_out"], 1)
                        step(v.tensor_reduce(gain[:, :], sc[:, :, :], AX, ALU.add))
                        step(v.reciprocal(gain[:, :], gain[:, :]))
                    for k in range(NK):
                        dve.wait_ge(s["h_raw"], k + 1)
                        dve.wait_ge(s["g_psum"], k // FC + 1)
                        if k >= RING:
                            dve.wait_ge(s["h_used"], k - RING + 1)
                        v.tensor_tensor(hm[:, k % RING, :], hs[:, k % RING, :], PS[:, 4 + (k // FC) % 2, :], ALU.mult)\
                            .then_inc(s["h_ready"], 1)
                    dve.wait_ge(s["y_psum"], 1)
                    if st == "L2f":
                        dve_residual(core, dve, it, PS[:, 7, :], s["y_psum"])
                    for t in range(T):
                        y = PS[:, 7, t * P:(t + 1) * P]
                        if st == "L1f":
                            v.scalar_tensor_tensor(tile_of(core, it, t), y, gain[:, t:t + 1], tile_of(core, it, t),
                                                   ALU.mult, ALU.add)
                        if st == "L0f":
                            step.mark(v.scalar_tensor_tensor(xh[:, t, :], y, gain[:, t:t + 1], L["xn"][:, t, :],
                                                             ALU.mult, ALU.add))
                    if st == "L0f":
                        dve.wait_ge(s["dve_step"], step.n)
                        v.tensor_tensor(tokens_of(core, it), tokens_of(core, it), xh[:, :, :], ALU.add)
                    end_pass(core, dve, "go_dve")


def load_ffn(core, eng, ly, slot):
    for n in (0, 1):
        eng.dma_start(core.ffn[slot][n][:, :], core.dram[f"{ly}_ffn{n + 1}"]).then_inc(core.sem[f"ffn_w{ly[1]}"], 16)


def channel_attention(core):
    nc, s, PS, w = core.nc, core.sem, core.PS, core.w
    with ExitStack() as c:
        sb = core.buffers(c)
        L = ln_buffers(core, c)
        f2 = sb("f2", [P, T, D])
        et = sb("et", [P, 1])
        junk = sb("junk", [P, S])
        ss, lns, rs, us = (sb(n, [P, 2, NSEQ]) for n in ("ss", "lns", "rs", "us"))
        qk = sb("qk", [P, 2, NT])
        qkt = sb("qkt", [P, 2, NT])
        vT = sb("vT", [P, NT])
        sm, ex, en = (sb(n, [P, NSEQ, P]) for n in ("sm", "ex", "en"))
        rm, rd = sb("rm", [P, NSEQ]), sb("rd", [P, NSEQ])
        aT = sb("aT", [P, NSEQ, P])
        oT = sb("oT", [P, NT])
        TINY, UP = 1e-24, 2.0 ** 20
        with nc.Block() as block:

            @block.sync
            def _(sp):
                load_next_weights(core, sp)
                with sp.Fori(0, NPASS) as it:
                    end_pass_sync(core, sp)
                await_next_weights(core, sp)

            @block.gpsimd
            def _(pool):
                with pool.Fori(0, NPASS) as it:
                    end_pass(core, pool, "go_pool")

            @block.tensor
            def _(pe):
                mm, tr = nc.tensor.matmul, nc.tensor.transpose
                free = dict(skip_group_check=True)
                with pe.Fori(0, NPASS) as it:
                    pe_turn(core, pe, f2, 7, s["xh_ready"], s["xT_psum"])
                    pe.wait_ge(s["xT_ready"], 1)
                    for n in range(3):
                        mm(PS[:, n, :], w("L2a_qkv")[:, n * P:(n + 1) * P], L["xT"][:, :], start=True, stop=True)\
                            .then_inc(s["q_psum"], 1)
                    for n in range(2):
                        pe.wait_ge(s["a_in"], 2 * n + 2)
                        for t in range(T):
                            ins = tr(PS[:, 3 + n, t * P:(t + 1) * P], qk[:, n, t * P:(t + 1) * P], w("ident"))
                        ins.then_inc(s["a_out"], 1)
                    pe.wait_ge(s["b_in"], 2)
                    for b in range(NSEQ):
                        for tt in range(TS):
                            t = b * TS + tt
                            ins = mm(PS[:, 5, b * P:(b + 1) * P], qkt[:, 0, t * P:(t + 1) * P],
                                     qkt[:, 1, t * P:(t + 1) * P], start=(tt == 0), stop=(tt == TS - 1), **free)
                    ins.then_inc(s["b_out"], 1)
                    pe.wait_ge(s["c_in"], 1)
                    for b in range(NSEQ):
                        ins = tr(PS[:, 6, b * P:(b + 1) * P], en[:, b, :], w("ident"))
                    ins.then_inc(s["c_out"], 1)
                    pe.wait_ge(s["d_in"], 1)
                    pe.wait_ge(s["v_ready"], 1)
                    for b in range(NSEQ):
                        ins = mm(PS[:, 7, b * S:(b + 1) * S], aT[:, b, :], vT[:, b * S:(b + 1) * S],
                                 start=(b == 0), stop=True, **free)
                    ins.then_inc(s["d_out"], 1)
                    pe.wait_ge(s["e_in"], 1)
                    for t in range(T):
                        ins = mm(PS[:, 0, t * P:(t + 1) * P], oT[:, t * P:(t + 1) * P], w("L2a_out"),
                                 start=(t == 0), stop=True, **free)
                    ins.then_inc(s["y_psum"], 1)
                    end_pass(core, pe, "go_pe")

            @block.scalar
            def _(act):
                a = nc.scalar.activation
                with act.Fori(0, NPASS) as it:
                    step = Step(act, s["act_step"])
                    step(a(et[:, :], w("L2a_temp"), ACT.Exp))
                    act_layernorm(core, act, step, L)
                    act_layernorm(core, act, step, L, n=1)
                    act.wait_ge(s["xT_psum"], 1)
                    a(L["xT"][:, :], PS[:, 7, :], ACT.Copy, scale=w("L2a_norm")).then_inc(s["xT_ready"], 1)
                    for n in range(2):
                        act.wait_ge(s["q_psum"], n + 1)
                        for b in range(NSEQ):
                            step.mark(a(junk[:, :], PS[:, n, b * S:(b + 1) * S], ACT.Square,
                                        accum_out=ss[:, n, b:b + 1]))
                            act.wait_ge(s["act_step"], step.n)
                    a(junk[:, 0:1], et[:, :], ACT.Copy).then_inc(s["f_in"], 1)
                    act_copy(core, act, vT[:, :], PS[:, 2, :], s["q_psum"], 3, s["v_ready"])
                    act.wait_ge(s["f_out"], 1)
                    step(a(lns[:, :, :], us[:, :, :], ACT.Ln, scale=UP))
                    a(rs[:, :, :], lns[:, :, :], ACT.Exp, scale=-0.5).then_inc(s["f_in"], 1)
                    act_copy(core, act, qkt[:, 0, :], PS[:, 3, :], s["a_out"], 1, s["b_in"])
                    act_copy(core, act, qkt[:, 1, :], PS[:, 4, :], s["a_out"], 2, s["b_in"])
                    act.wait_ge(s["gexp_in"], 1)
                    a(ex[:, :, :], sm[:, :, :], ACT.Exp).then_inc(s["gexp_out"], 1)
                    act_copy(core, act, aT[:, :, :].rearrange("p b i -> p (b i)"), PS[:, 6, 0:NSEQ * P],
                             s["c_out"], 1, s["d_in"])
                    act_copy(core, act, oT[:, :], PS[:, 7, :], s["d_out"], 1, s["e_in"])
                    end_pass(core, act, "go_act")

            @block.vector
            def _(dve):
                v = nc.vector
                with dve.Fori(0, NPASS) as it:
                    step = Step(dve, s["dve_step"])
                    dve_layernorm(core, dve, step, L, lambda t: tile_of(core, it, t), L["xn"], s["xn_ready"])
                    dve.wait_ge(s["xn_ready"], T)
                    dve_layernorm(core, dve, step, L, lambda t: L["xn"][:, t, :], f2, s["xh_ready"], n=1,
                                  rms=True, eps=1e-6)
                    dve.wait_ge(s["f_in"], 1)
                    v.tensor_scalar(us[:, :, :], ss[:, :, :], TINY, None, ALU.max).then_inc(s["f_out"], 1)
                    dve.wait_ge(s["f_in"], 2)
                    step(v.tensor_scalar(rs[:, :, :], rs[:, :, :], UP ** 0.5, None, ALU.mult))
                    dve.wait_ge(s["f_out"], 1)
                    step(v.tensor_tensor(us[:, :, :], us[:, :, :], rs[:, :, :], ALU.mult))
                    step(v.tensor_tensor(us[:, :, :], us[:, :, :], rs[:, :, :], ALU.mult))
                    step(v.tensor_scalar(us[:, :, :], us[:, :, :], -0.5, 1.5, ALU.mult, ALU.add))
                    step(v.tensor_tensor(rs[:, :, :], rs[:, :, :], us[:, :, :], ALU.mult))
                    step(v.tensor_scalar(rs[:, 0, :], rs[:, 0, :], et[:, :], None, ALU.mult))
                    for n in range(2):
                        for b in range(NSEQ):
                            v.tensor_scalar(qk[:, n, b * S:(b + 1) * S], PS[:, n, b * S:(b + 1) * S],
                                            rs[:, n, b:b + 1], None, ALU.mult).then_inc(s["a_in"], 1)
                    dve.wait_ge(s["b_out"], 1)
                    step(v.tensor_tensor(sm[:, :, :], PS[:, 5, 0:NSEQ * P].rearrange("p (b j) -> p b j", b=NSEQ),
                                         w("block_diag").unsqueeze(1).broadcast_to([P, NSEQ, P]), ALU.add))
                    step(v.tensor_reduce(rm[:, :], sm[:, :, :], AX, ALU.max))
                    v.tensor_tensor(sm[:, :, :], sm[:, :, :], rm[:, :].unsqueeze(2).broadcast_to([P, NSEQ, P]),
                                    ALU.subtract).then_inc(s["gexp_in"], 1)
                    dve.wait_ge(s["gexp_out"], 1)
                    step(v.tensor_reduce(rd[:, :], ex[:, :, :], AX, ALU.add))
                    step(v.reciprocal(rd[:, :], rd[:, :]))
                    v.tensor_tensor(en[:, :, :], ex[:, :, :], rd[:, :].unsqueeze(2).broadcast_to([P, NSEQ, P]),
                                    ALU.mult).then_inc(s["c_in"], 1)
                    dve_residual(core, dve, it, PS[:, 0, :], s["y_psum"])
                    end_pass(core, dve, "go_dve")


def retention(core):
    nc, s, PS, w = core.nc, core.sem, core.PS, core.w
    with ExitStack() as c:
        sb = core.buffers(c)
        L = ln_buffers(core, c)
        kvT = sb("kvT", [P, NT])
        t1, t2, rot = (sb(n, [P, 2, NT]) for n in ("t1", "t2", "rot"))
        V = sb("V", [P, T, D])
        D0 = sb("D0", [P, NSEQ, S])
        D1 = sb("D1", [P, NSEQ, P])
        with nc.Block() as block:

            @block.sync
            def _(sp):
                load_next_weights(core, sp)
                with sp.Fori(0, NPASS) as it:
                    end_pass_sync(core, sp)
                await_next_weights(core, sp)

            @block.gpsimd
            def _(pool):
                with pool.Fori(0, NPASS) as it:
                    nc.gpsimd.tensor_copy(kvT[:, :], core.ctxT[:, bass.ds(it * NT, NT)]).then_inc(s["kv_ready"], 1)
                    end_pass(core, pool, "go_pool")

            @block.tensor
            def _(pe):
                mm = nc.tensor.matmul
                free = dict(skip_group_check=True)
                with pe.Fori(0, NPASS) as it:
                    pe.wait_ge(s["kv_ready"], 1)
                    mm(PS[:, 2, :], w("L2x_k"), kvT[:, :], start=True, stop=True)
                    mm(PS[:, 3, :], w("L2x_ks"), kvT[:, :], start=True, stop=True).then_inc(s["k_psum"], 1)
                    for t in range(T):
                        ins = mm(PS[:, 4, t * P:(t + 1) * P], kvT[:, t * P:(t + 1) * P], w("L2x_v"),
                                 start=(t == 0), stop=True, **free)
                    ins.then_inc(s["v_psum"], 1)
                    pe_turn(core, pe, L["xn"], 7, s["xn_ready"], s["xT_psum"])
                    pe.wait_ge(s["xT_ready"], 1)
                    mm(PS[:, 0, :], w("L2x_q"), L["xT"][:, :], start=True, stop=True)
                    mm(PS[:, 1, :], w("L2x_qs"), L["xT"][:, :], start=True, stop=True).then_inc(s["q_psum"], 1)
                    pe.wait_ge(s["a_in"], 2)
                    for b in range(NSEQ):
                        q0 = b * S
                        mm(PS[:, 5, q0:q0 + S], rot[:, 1, q0:q0 + P], rot[:, 0, q0:q0 + S],
                           start=(b == 0), stop=True, **free)
                        ins = mm(PS[:, 6, b * P:(b + 1) * P], rot[:, 1, q0 + P:q0 + S], rot[:, 0, q0 + P:q0 + S],
                                 start=(b == 0), stop=True, **free)
                    ins.then_inc(s["a_out"], 1)
                    pe.wait_ge(s["b_in"], 2)
                    pe.wait_ge(s["v_ready"], 1)
                    for b in range(NSEQ):
                        for tt in range(TS):
                            t = b * TS + tt
                            o = PS[:, 7, t * P:(t + 1) * P]
                            ins = mm(o, D0[:, b, tt * P:(tt + 1) * P], V[:, b * TS, :], start=(t == 0),
                                     stop=(tt == 0), **free)
                            if tt == 1:
                                ins = mm(o, D1[:, b, :], V[:, b * TS + 1, :], start=False, stop=True, **free)
                    ins.then_inc(s["y_psum"], 1)
                    end_pass(core, pe, "go_pe")

            @block.scalar
            def _(act):
                with act.Fori(0, NPASS) as it:
                    step = Step(act, s["act_step"])
                    act_copy(core, act, V[:, :, :].rearrange("p t d -> p (t d)"), PS[:, 4, :], s["v_psum"], 1, s["v_ready"])
                    act_layernorm(core, act, step, L)
                    act_copy(core, act, L["xT"][:, :], PS[:, 7, :], s["xT_psum"], 1, s["xT_ready"])
                    end_pass(core, act, "go_act")

            @block.vector
            def _(dve):
                v = nc.vector
                two = lambda ap: ap.rearrange("p (b t) -> p b t", b=NSEQ)
                tab = lambda n: w(n).unsqueeze(1).broadcast_to([P, NSEQ, S])
                with dve.Fori(0, NPASS) as it:
                    step = Step(dve, s["dve_step"])
                    dve_layernorm(core, dve, step, L, lambda t: tile_of(core, it, t), L["xn"], s["xn_ready"])
                    for n, what in ((1, "k"), (0, "q")):
                        dve.wait_ge(s[what + "_psum"], 1)
                        step.mark(v.tensor_tensor(two(t1[:, n, :]), two(PS[:, 2 * n, :]), tab(f"x{what}_cos"), ALU.mult))
                        step(v.tensor_tensor(two(t2[:, n, :]), two(PS[:, 2 * n + 1, :]), tab(f"x{what}_sin"), ALU.mult))
                        v.tensor_tensor(rot[:, n, :], t1[:, n, :], t2[:, n, :], ALU.add).then_inc(s["a_in"], 1)
                    dve.wait_ge(s["a_out"], 1)
                    v.tensor_tensor(D0[:, :, :], two(PS[:, 5, :]), tab("decay0"), ALU.mult).then_inc(s["b_in"], 1)
                    v.tensor_tensor(D1[:, :, :], PS[:, 6, 0:NSEQ * P].rearrange("p (b t) -> p b t", b=NSEQ),
                                    w("decay0")[:, 0:P].unsqueeze(1).broadcast_to([P, NSEQ, P]), ALU.mult)\
                        .then_inc(s["b_in"], 1)
                    dve_residual(core, dve, it, PS[:, 7, :], s["y_psum"])
                    end_pass(core, dve, "go_dve")


def state_space(core):
    nc, s, PS, w = core.nc, core.sem, core.PS, core.w
    NH = 2
    PAD = TAPS - 1
    QW = S + P
    with ExitStack() as c:
        sb = core.buffers(c)
        L = ln_buffers(core, c)
        xTp = sb("xTp", [P, NSEQ, PAD + S])
        Wx = sb("Wx", [P, TAPS, NH * P])
        Wbc = sb("Wbc", [P, 2, TAPS, 64])
        xs = sb("xs", [P, NH, NT])
        BC = sb("BC", [64, 2, NT])
        zs = sb("zs", [P, NH, NT])
        Xt = sb("Xt", [P, NH, T, P])
        An = sb("An", [P, NH])
        dt, nv, av, u, w1, dd, ez, q1, dA = (sb(n, [P, T, NH]) for n in
                                             ("dt", "nv", "av", "u", "w1", "dd", "ez", "q1", "dA"))
        dAb = sb("dAb", [P, T, NH, P])
        cs = sb("cs", [P, T, NH])
        Ld = sb("Ld", [P, NSEQ, NH, QW])
        Lx = sb("Lx", [P, NSEQ, NH, QW])
        Gm0, Gm1 = sb("Gm0", [P, NSEQ, S]), sb("Gm1", [P, NSEQ, P])
        Wk = sb("Wk", [P, NSEQ, NH, QW])
        y2 = sb("y2", [P, NH, NT])
        y3 = sb("y3", [P, NH, NT])
        tri2 = core.W[:, COLS["tri"][0]:COLS["tri"][0] + S]
        core.n_setup += 4
        with nc.Block() as block:

            @block.sync
            def _(sp):
                load_next_weights(core, sp)
                with sp.Fori(0, NPASS) as it:
                    end_pass_sync(core, sp)
                await_next_weights(core, sp)

            @block.gpsimd
            def _(pool):
                g = nc.gpsimd
                g.memset(xTp[:, :, 0:PAD], 0.0).then_inc(s["setup"], 1)
                g.tensor_tensor(Wx[:, :, :], w("L3a_xs").unsqueeze(1).broadcast_to([P, TAPS, NH * P]),
                                w("L3a_taps_xs").rearrange("p (k c) -> p k c", k=TAPS), ALU.mult).then_inc(s["setup"], 1)
                for n, name in enumerate("bc"):
                    g.tensor_tensor(Wbc[:, n], w(f"L3a_{name}").unsqueeze(1).broadcast_to([P, TAPS, 64]),
                                    w(f"L3a_taps_{name}").rearrange("p (k c) -> p k c", k=TAPS), ALU.mult)\
                        .then_inc(s["setup"], 1)
                with pool.Fori(0, NPASS) as it:
                    pool.wait_ge(s["b_in"], 1)
                    g.tensor_copy(dAb[:, :, :, :], dA[:, :, :].unsqueeze(3).broadcast_to([P, T, NH, P]))\
                        .then_inc(s["b_out"], 1)
                    end_pass(core, pool, "go_pool")

            @block.tensor
            def _(pe):
                mm, tr = nc.tensor.matmul, nc.tensor.transpose
                free = dict(skip_group_check=True)
                pe.wait_ge(s["setup"], core.n_setup)
                with pe.Fori(0, NPASS) as it:
                    pe_turn(core, pe, L["xn"], 7, s["xn_ready"], s["xT_psum"])
                    pe.wait_ge(s["xT_ready"], 1)
                    for t in range(T):
                        q0 = PAD + (t % TS) * P
                        ins = mm(PS[:, 6, t * NH:(t + 1) * NH], xTp[:, t // TS, q0:q0 + P], w("L3a_dt"),
                                 start=(t == 0), stop=True, **free)
                    ins.then_inc(s["a_out"], 1)
                    for n in range(2):
                        for k in range(TAPS):
                            ins = mm(PS[0:64, 2 + n, :].rearrange("p (b t) -> p b t", b=NSEQ), Wbc[:, n, k, :],
                                     xTp[:, :, k:k + S], start=(k == 0), stop=(k == PAD))
                        ins.then_inc(s["z_psum"], 1)
                    for n in range(NH):
                        for k in range(TAPS):
                            ins = mm(PS[:, n, :].rearrange("p (b t) -> p b t", b=NSEQ), Wx[:, k, n * P:(n + 1) * P],
                                     xTp[:, :, k:k + S], start=(k == 0), stop=(k == PAD))
                        ins.then_inc(s["z_psum"], 1)
                    for n in range(NH):
                        mm(PS[:, 4 + n, :].rearrange("p (b t) -> p b t", b=NSEQ), w("L3a_z")[:, n * P:(n + 1) * P],
                           xTp[:, :, PAD:PAD + S], start=True, stop=True).then_inc(s["z_psum"], 1)
                    pe.wait_ge(s["b_in"], 1)
                    for t in range(T):
                        o = PS[:, 6, 64 + t * NH:64 + (t + 1) * NH]
                        ins = mm(o, w("tri"), dA[:, t, :], start=(t == 0), stop=True, **free)
                        if t % TS:
                            ins = mm(o, w("ones"), dA[:, t - 1, :], start=False, stop=True, **free)
                    ins.then_inc(s["c_out"], 1)
                    pe.wait_ge(s["b_out"], 1)
                    pe.wait_ge(s["h_raw"], 6)
                    for b in range(NSEQ):
                        bank = (7, 0)[b]
                        for h in range(NH):
                            mm(PS[:, bank, h * S:(h + 1) * S], dAb[:, b * TS, h, :], tri2, start=(h == 0), stop=True, **free)
                            ins = mm(PS[:, bank, h * S + P:(h + 1) * S], dAb[:, b * TS + 1, h, :], w("tri"),
                                     start=False, stop=True, **free)
                        ins.then_inc(s["d_out"], 1)
                    for b in range(NSEQ):
                        q0 = b * S
                        mm(PS[:, 2, q0:q0 + S], BC[:, 0, q0:q0 + P], BC[:, 1, q0:q0 + S], start=(b == 0), stop=True, **free)
                        ins = mm(PS[:, 3, b * P:(b + 1) * P], BC[:, 0, q0 + P:q0 + S], BC[:, 1, q0 + P:q0 + S],
                                 start=(b == 0), stop=True, **free)
                    ins.then_inc(s["e_out"], 1)
                    for h in range(NH):
                        for t in range(T):
                            ins = tr(PS[:, 4 + h, t * P:(t + 1) * P], xs[:, h, t * P:(t + 1) * P], w("ident"))
                        ins.then_inc(s["tr_psum"], 1)
                    pe.wait_ge(s["h_ready"], 2 * NSEQ * NH)
                    pe.wait_ge(s["v_ready"], NH)
                    for h in range(NH):
                        for b in range(NSEQ):
                            mm(PS[:, 1 - h, b * S:(b + 1) * S], Xt[:, h, b * TS, :], Wk[:, b, h, 0:S],
                               start=(b == 0), stop=True, **free)
                            ins = mm(PS[:, 1 - h, b * S + P:(b + 1) * S], Xt[:, h, b * TS + 1, :], Wk[:, b, h, S:QW],
                                     start=False, stop=True, **free)
                        ins.then_inc(s["f_out"], 1)
                    pe.wait_ge(s["f_in"], NH)
                    for t in range(T):
                        for h in range(NH):
                            ins = mm(PS[:, 2, t * P:(t + 1) * P], y3[:, h, t * P:(t + 1) * P],
                                     w("L3a_out")[:, h * P:(h + 1) * P], start=(t == 0 and h == 0), stop=True, **free)
                    ins.then_inc(s["y_psum"], 1)
                    end_pass(core, pe, "go_pe")

            @block.scalar
            def _(act):
                a = nc.scalar.activation
                act.wait_ge(s["setup"], core.n_setup)
                with act.Fori(0, NPASS) as it:
                    step = Step(act, s["act_step"])
                    a(An[:, :], w("L3a_alog"), ACT.Exp).then_inc(s["a_in"], 1)
                    act_layernorm(core, act, step, L)
                    act.wait_ge(s["xT_psum"], 1)
                    a(xTp[:, :, PAD:PAD + S], PS[:, 7, :].rearrange("p (b t) -> p b t", b=NSEQ), ACT.Copy)\
                        .then_inc(s["xT_ready"], 1)
                    act.wait_ge(s["gexp_in"], 1)
                    a(u[:, :, :], av[:, :, :], ACT.Exp, scale=-1.0).then_inc(s["gexp_out"], 1)
                    act.wait_ge(s["gexp_in"], 2)
                    a(q1[:, :, :], w1[:, :, :], ACT.Ln).then_inc(s["gexp_out"], 1)
                    for n in range(2):
                        act.wait_ge(s["z_psum"], n + 1)
                        a(BC[:, n, :], PS[0:64, 2 + n, :], ACT.Silu, bias=w(f"L3a_bias_{'bc'[n]}", 64))\
                            .then_inc(s["h_raw"], 1)
                    for n in range(NH):
                        act.wait_ge(s["z_psum"], 3 + n)
                        a(xs[:, n, :], PS[:, n, :], ACT.Silu, bias=w("L3a_bias_xs")[:, n:n + 1]).then_inc(s["h_raw"], 1)
                    for n in range(NH):
                        act.wait_ge(s["z_psum"], 5 + n)
                        a(zs[:, n, :], PS[:, 4 + n, :], ACT.Silu).then_inc(s["h_raw"], 1)
                    for b in range(NSEQ):
                        act.wait_ge(s["c_in"], b + 1)
                        a(Lx[:, b], Ld[:, b], ACT.Exp).then_inc(s["d_in"], 1)
                    for h in range(NH):
                        act_copy(core, act, Xt[:, h].rearrange("p t c -> p (t c)"), PS[:, 4 + h, :], s["tr_psum"], h + 1,
                                 s["v_ready"])
                    end_pass(core, act, "go_act")

            @block.vector
            def _(dve):
                v = nc.vector
                with dve.Fori(0, NPASS) as it:
                    step = Step(dve, s["dve_step"])
                    dve_layernorm(core, dve, step, L, lambda t: tile_of(core, it, t), L["xn"], s["xn_ready"])
                    dve.wait_ge(s["a_out"], 1)
                    step(v.tensor_tensor(dt[:, :, :], PS[:, 6, 0:T * NH].rearrange("p (t h) -> p t h", t=T),
                                         w("L3a_dtb").unsqueeze(1).broadcast_to([P, T, NH]), ALU.add))
                    step(v.tensor_scalar(nv[:, :, :], dt[:, :, :], -1.0, None, ALU.mult))
                    v.tensor_tensor(av[:, :, :], dt[:, :, :], nv[:, :, :], ALU.max).then_inc(s["gexp_in"], 1)
                    dve.wait_ge(s["gexp_out"], 1)
                    v.tensor_scalar(w1[:, :, :], u[:, :, :], 1.0, None, ALU.add).then_inc(s["gexp_in"], 1)
                    dve.wait_ge(s["gexp_in"], 2)
                    step(v.tensor_scalar(dd[:, :, :], w1[:, :, :], 1.0, None, ALU.subtract))
                    step(v.tensor_scalar(ez[:, :, :], dd[:, :, :], 0.0, None, ALU.is_equal))
                    step(v.tensor_tensor(dd[:, :, :], dd[:, :, :], ez[:, :, :], ALU.add))
                    step(v.reciprocal(dd[:, :, :], dd[:, :, :]))
                    dve.wait_ge(s["gexp_out"], 2)
                    step(v.tensor_tensor(dd[:, :, :], dd[:, :, :], q1[:, :, :], ALU.mult))
                    step(v.tensor_tensor(dd[:, :, :], dd[:, :, :], ez[:, :, :], ALU.add))
                    step(v.tensor_tensor(dd[:, :, :], dd[:, :, :], u[:, :, :], ALU.mult))
                    step(v.tensor_scalar(dt[:, :, :], dt[:, :, :], 0.0, None, ALU.max))
                    step(v.tensor_tensor(dt[:, :, :], dt[:, :, :], dd[:, :, :], ALU.add))
                    dve.wait_ge(s["a_in"], 1)
                    step(v.tensor_tensor(dd[:, :, :], dt[:, :, :], An[:, :].unsqueeze(1).broadcast_to([P, T, NH]), ALU.mult))
                    v.tensor_scalar(dA[:, :, :], dd[:, :, :], -1.0, None, ALU.mult).then_inc(s["b_in"], 1)
                    dve.wait_ge(s["c_out"], 1)
                    step(v.tensor_copy(cs[:, :, :], PS[:, 6, 64:64 + T * NH].rearrange("p (t h) -> p t h", t=T)))
                    for b in range(NSEQ):
                        dve.wait_ge(s["d_out"], b + 1)
                        bank = (7, 0)[b]
                        for h in range(NH):
                            v.tensor_scalar(Ld[:, b, h, 0:S], PS[:, bank, h * S:(h + 1) * S], cs[:, b * TS, h:h + 1], 0.0,
                                            ALU.subtract, ALU.min)
                            ins = v.tensor_scalar(Ld[:, b, h, S:QW], PS[:, bank, h * S + P:(h + 1) * S],
                                                  cs[:, b * TS + 1, h:h + 1], 0.0, ALU.subtract, ALU.min)
                        ins.then_inc(s["c_in"], 1)
                    dve.wait_ge(s["e_out"], 1)
                    step.mark(v.tensor_tensor(Gm0[:, :, :], PS[:, 2, :].rearrange("p (b t) -> p b t", b=NSEQ),
                                              tri2.unsqueeze(1).broadcast_to([P, NSEQ, S]), ALU.mult))
                    step(v.tensor_tensor(Gm1[:, :, :], PS[:, 3, 0:NSEQ * P].rearrange("p (b t) -> p b t", b=NSEQ),
                                         w("tri").unsqueeze(1).broadcast_to([P, NSEQ, P]), ALU.mult))
                    for b in range(NSEQ):
                        dve.wait_ge(s["d_in"], b + 1)
                        for h in range(NH):
                            v.scalar_tensor_tensor(Wk[:, b, h, 0:S], Lx[:, b, h, 0:S], dt[:, b * TS, h:h + 1],
                                                   Gm0[:, b, :], ALU.mult, ALU.mult).then_inc(s["h_ready"], 1)
                            v.scalar_tensor_tensor(Wk[:, b, h, S:QW], Lx[:, b, h, S:QW], dt[:, b * TS + 1, h:h + 1],
                                                   Gm1[:, b, :], ALU.mult, ALU.mult).then_inc(s["h_ready"], 1)
                    for h in range(NH):
                        dve.wait_ge(s["f_out"], h + 1)
                        step(v.scalar_tensor_tensor(y2[:, h, :], xs[:, h, :], w("L3a_skip")[:, h:h + 1], PS[:, 1 - h, :],
                                                    ALU.mult, ALU.add))
                        v.tensor_tensor(y3[:, h, :], y2[:, h, :], zs[:, h, :], ALU.mult).then_inc(s["f_in"], 1)
                    dve_residual(core, dve, it, PS[:, 2, :], s["y_psum"])
                    end_pass(core, dve, "go_dve")


def latent_experts(core):
    nc, s, PS, w = core.nc, core.sem, core.PS, core.w
    NR = 4
    NK = NR + 4
    RING = 3
    with ExitStack() as c:
        sb = core.buffers(c)
        L = ln_buffers(core, c)
        sg, sf, oh, eq, sc, wt, o2 = (sb(n, [P, T, E]) for n in ("sg", "sf", "oh", "eq", "sc", "wt", "o2"))
        pairs = sb("pairs", [P, T, 2, 6])
        gs, keep = sb("gs", [P, T, 2]), sb("keep", [P, T, 2])
        mx, mc = sb("mx", [P, T]), sb("mc", [P, T])
        wT = sb("wT", [P, NT])
        lat = sb("lat", [P, NT])
        comb = sb("comb", [P, NT])
        hs, hm, ht = (sb(n, [P, RING, NT]) for n in ("hs", "hm", "ht"))
        YT = sb("YT", [P, NT])
        core.n_setup += 1
        with nc.Block() as block:

            @block.sync
            def _(sp):
                load_next_weights(core, sp)
                with sp.Fori(0, NPASS) as it:
                    end_pass_sync(core, sp)
                await_next_weights(core, sp)

            @block.gpsimd
            def _(pool):
                nc.gpsimd.memset(wT[:, :], 0.0).then_inc(s["setup"], 1)
                with pool.Fori(0, NPASS) as it:
                    end_pass(core, pool, "go_pool")

            @block.tensor
            def _(pe):
                mm, tr = nc.tensor.matmul, nc.tensor.transpose
                free = dict(skip_group_check=True)
                pe.wait_ge(s["setup"], core.n_setup)
                with pe.Fori(0, NPASS) as it:
                    pe_turn(core, pe, L["xn"], 7, s["xn_ready"], s["xT_psum"])
                    pe.wait_ge(s["xT_ready"], 1)
                    for t in range(T):
                        ins = mm(PS[:, 6, t * E:(t + 1) * E], L["xT"][:, t * P:(t + 1) * P], w("L3f_gate"),
                                 start=(t == 0), stop=True, **free)
                    ins.then_inc(s["gate_psum"], 1)
                    mm(PS[:, 4, :], w("L3f_fc1"), L["xT"][:, :], start=True, stop=True, **free).then_inc(s["a_out"], 1)

                    def second(i):
                        k = ORDER[i]
                        pe.wait_ge(s["h_ready"], i + 1)
                        if k >= NR:
                            ins = mm(PS[:, 7, :], w("L3f_down")[:, (k - NR) * P:(k - NR + 1) * P], hm[:, i % RING, :],
                                     start=(k == NR), stop=False, **free)
                        else:
                            ins = mm(PS[:, 3, :], w("L3f_w2")[:, k * P:(k + 1) * P], hm[:, i % RING, :],
                                     start=(k == 0), stop=(k == NR - 1), **free)
                        ins.then_inc(s["h_used"], 1)

                    for i, k in enumerate(ORDER):
                        if i >= RING:
                            pe.wait_ge(s["h_raw"], i - RING + 1)
                        if k < NR:
                            if k == 0:
                                pe.wait_ge(s["gate_mask"], 1)
                                for t in range(T):
                                    ins = tr(PS[0:E, 6, t * P:(t + 1) * P], wt[:, t, :], w("ident"))
                                ins.then_inc(s["maskT_psum"], 1)
                                pe.wait_ge(s["maskT_ready"], 1)
                                pe.wait_ge(s["a_in"], 1)
                            if k >= 2:
                                pe.wait_ge(s["h_ready"], i - 1)
                            mm(PS[:, 4 + k % 2, :], w("pick_pairs")[:, k * P:(k + 1) * P], wT[:, :], start=True, stop=True, **free)\
                                .then_inc(s["g_psum"], 1)
                            mm(PS[:, i % RING, :], w("L3f_w1")[:, k * P:(k + 1) * P], lat[:, :],
                               start=True, stop=True, **free).then_inc(s["z_psum"], 1)
                        else:
                            mm(PS[:, i % RING, :], w("L3f_up")[:, (k - NR) * P:(k - NR + 1) * P], L["xT"][:, :],
                               start=True, stop=True, **free).then_inc(s["z_psum"], 1)
                        if i >= 2:
                            second(i - 2)
                    second(NK - 2)
                    second(NK - 1)
                    pe.wait_ge(s["b_in"], 1)
                    mm(PS[:, 7, :], w("L3f_fc2"), comb[:, :], start=False, stop=True, **free).then_inc(s["b_out"], 1)
                    pe.wait_ge(s["yT_ready"], 1)
                    for t in range(T):
                        ins = tr(PS[:, 0, t * P:(t + 1) * P], YT[:, t * P:(t + 1) * P], w("ident"))
                    ins.then_inc(s["y_psum"], 1)
                    end_pass(core, pe, "go_pe")

            @block.scalar
            def _(act):
                a = nc.scalar.activation
                act.wait_ge(s["setup"], core.n_setup)
                with act.Fori(0, NPASS) as it:
                    step = Step(act, s["act_step"])
                    act_layernorm(core, act, step, L)
                    act_copy(core, act, L["xT"][:, :], PS[:, 7, :], s["xT_psum"], 1, s["xT_ready"])
                    act_copy(core, act, lat[:, :], PS[:, 4, :], s["a_out"], 1, s["a_in"])
                    act.wait_ge(s["gexp_in"], 1)
                    a(sg[:, :, :], sf[:, :, :], ACT.Exp, scale=-1.0).then_inc(s["gexp_out"], 1)
                    for i, k in enumerate(ORDER):
                        if k == 0:
                            act.wait_ge(s["maskT_psum"], 1)
                            a(wT[0:E, :], PS[0:E, 6, :], ACT.Copy).then_inc(s["maskT_ready"], 1)
                        act.wait_ge(s["z_psum"], i + 1)
                        if i >= RING:
                            act.wait_ge(s["h_ready"], i - RING + 1)
                        a(hs[:, i % RING, :], PS[:, i % RING, :], ACT.Relu).then_inc(s["h_raw"], 1)
                    act_copy(core, act, comb[:, :], PS[:, 3, :], s["h_used"], NK, s["b_in"])
                    act_copy(core, act, YT[:, :], PS[:, 7, :], s["b_out"], 1, s["yT_ready"])
                    end_pass(core, act, "go_act")

            @block.vector
            def _(dve):
                v = nc.vector
                bc = lambda ap: ap.unsqueeze(2).broadcast_to([P, T, E])
                bt = lambda ap: ap.unsqueeze(1).broadcast_to([P, T, E])

                def hidden(dve, i):
                    k = ORDER[i]
                    dve.wait_ge(s["h_raw"], i + 1)
                    if i >= RING:
                        dve.wait_ge(s["h_used"], i - RING + 1)
                    if k < NR:
                        dve.wait_ge(s["g_psum"], k + 1)
                        v.tensor_tensor(ht[:, i % RING, :], hs[:, i % RING, :], PS[:, 4 + k % 2, :], ALU.mult)\
                            .then_inc(s["c_in"], 1)
                        dve.wait_ge(s["c_in"], k + 1)
                    other = ht if k < NR else hs
                    v.tensor_tensor(hm[:, i % RING, :], hs[:, i % RING, :], other[:, i % RING, :], ALU.mult)\
                        .then_inc(s["h_ready"], 1)

                with dve.Fori(0, NPASS) as it:
                    step = Step(dve, s["dve_step"])

                    def first_largest(values, out):
                        step(v.tensor_reduce(mx[:, :], values, AX, ALU.max))
                        step(v.tensor_tensor(eq[:, :, :], values, bc(mx[:, :]), ALU.is_equal))
                        step(v.tensor_tensor(sc[:, :, :], eq[:, :, :], bt(w("countdown")), ALU.mult))
                        step(v.tensor_reduce(mc[:, :], sc[:, :, :], AX, ALU.max))
                        step(v.tensor_tensor(out, sc[:, :, :], bc(mc[:, :]), ALU.is_equal))

                    dve_layernorm(core, dve, step, L, lambda t: tile_of(core, it, t), L["xn"], s["xn_ready"])
                    dve.wait_ge(s["gate_psum"], 1)
                    v.tensor_scalar(sf[:, :, :], PS[:, 6, 0:T * E].rearrange("p (t e) -> p t e", t=T), -80.0, None, ALU.max)\
                        .then_inc(s["gexp_in"], 1)
                    dve.wait_ge(s["gexp_out"], 1)
                    step(v.tensor_scalar(sg[:, :, :], sg[:, :, :], 1.0, None, ALU.add))
                    step(v.reciprocal(sg[:, :, :], sg[:, :, :]))
                    step(v.tensor_tensor(sf[:, :, :], sg[:, :, :], bt(w("L3f_corr")), ALU.add))
                    sv = sf[:, :, :].rearrange("p t (g e) -> p t g e", g=2)
                    for at, gap in ((0, 1), (3, 2), (5, 3)):
                        step.mark(v.tensor_tensor(pairs[:, :, :, at:at + 4 - gap], sv[:, :, :, 0:4 - gap],
                                                  sv[:, :, :, gap:4], ALU.add))
                    dve.wait_ge(s["dve_step"], step.n)
                    step(v.tensor_reduce(gs[:, :, :], pairs[:, :, :, :], AX, ALU.max))
                    step.mark(v.tensor_tensor(keep[:, :, 0:1], gs[:, :, 0:1], gs[:, :, 1:2], ALU.is_ge))
                    step(v.tensor_tensor(keep[:, :, 1:2], gs[:, :, 0:1], gs[:, :, 1:2], ALU.is_lt))
                    step(v.tensor_tensor(sv, sv, keep[:, :, :].unsqueeze(3).broadcast_to([P, T, 2, 4]), ALU.mult))
                    first_largest(sf[:, :, :], oh[:, :, :])
                    step(v.tensor_scalar(o2[:, :, :], oh[:, :, :], -BIG, None, ALU.mult))
                    step(v.tensor_tensor(sf[:, :, :], sf[:, :, :], o2[:, :, :], ALU.add))
                    first_largest(sf[:, :, :], o2[:, :, :])
                    step(v.tensor_tensor(oh[:, :, :], oh[:, :, :], o2[:, :, :], ALU.add))
                    step(v.tensor_tensor(oh[:, :, :], oh[:, :, :], sg[:, :, :], ALU.mult))
                    step(v.tensor_reduce(mx[:, :], oh[:, :, :], AX, ALU.add))
                    step(v.tensor_scalar(mx[:, :], mx[:, :], 1e-20, None, ALU.add))
                    step(v.reciprocal(mx[:, :], mx[:, :]))
                    v.tensor_tensor(wt[:, :, :], oh[:, :, :], bc(mx[:, :]), ALU.mult).then_inc(s["gate_mask"], 1)
                    for i in range(NK):
                        hidden(dve, i)
                    dve_residual(core, dve, it, PS[:, 0, :], s["y_psum"])
                    end_pass(core, dve, "go_dve")


ORDER = (4, 5, 6, 7, 0, 1, 2, 3)


def start(core):
    nc, s, PS, w = core.nc, core.sem, core.PS, core.w
    with ExitStack() as c:
        ctx_tok = c.enter_context(nc.sbuf_tensor("ctx_tok_", [P, B * TS, D], F32))
        pick = c.enter_context(nc.sbuf_tensor("pick32", [P, E * P], F32))
        with nc.Block() as block:

            @block.sync
            def _(sp):
                sp.dma_start(core.W[:, :], core.dram["small_common"]).then_inc(s["w_in"], 16)
                sp.dma_start(pick[:, :], core.dram["pick_rows"]).then_inc(s["w_in"], 16)
                sp.dma_start(core.stage_W[0][:, 0:width(WEIGHTS[STAGES[0]])], core.dram[f"small_{STAGES[0]}"])\
                    .then_inc(s["stage_w"], 16)
                sp.dma_start(ctx_tok[:, :, :], core.dram["ctx"].rearrange("(t p) d -> p t d", p=P)).then_inc(s["ctx_tok"], 16)
                sp.dma_start(core.X[:, :, :], core.dram["x"].rearrange("(t p) d -> p t d", p=P)).then_inc(s["x_in"], 16)
                sp.wait_ge(s["x_in"], 16)
                sp.wait_ge(s["stage_w"], 16)
                load_ffn(core, sp, "L0", 0)

            @block.tensor
            def _(pe):
                pe.wait_ge(s["w_in"], 32)
                pe.wait_ge(s["ctx_tok"], 16)
                for k in range(4):
                    for t in range(4):
                        ins = nc.tensor.transpose(PS[:, k, t * P:(t + 1) * P], ctx_tok[:, 4 * k + t, :], w("ident"))
                    ins.then_inc(s["ctx_psum"], 1)

            @block.scalar
            def _(act):
                nc.scalar.preload_act_table_set("natural_log_exp_and_others")
                act.wait_ge(s["w_in"], 32)
                for k in range(4):
                    act_copy(core, act, core.ctxT[:, k * 512:(k + 1) * 512], PS[:, k, :], s["ctx_psum"], k + 1, s["ctx_done"])

            @block.vector
            def _(dve):
                v = nc.vector
                dve.wait_ge(s["w_in"], 32)
                v.tensor_copy(core.ident_b[:, :], w("ident"))
                v.tensor_copy(core.neg_q[:, :], w("neg_q"))
                v.tensor_copy(core.neg_k[:, :], w("neg_k"))
                v.tensor_copy(core.pick[:, :], pick[:, :]).then_inc(s["ctx_done"], 1)
                dve.wait_ge(s["ctx_done"], 5)


def finish(core):
    nc, s = core.nc, core.sem
    with nc.Block() as block:

        @block.sync
        def _(sp):
            sp.dma_start(core.dram["out"].rearrange("(t p) d -> p t d", p=P), core.X[:, :, :]).then_inc(s["out_done"], 16)
            sp.wait_ge(s["out_done"], 16)


def program(nc, dram):
    with ExitStack() as ctx:
        core = Core(nc, ctx, dram)
        start(core)
        for core.at, st in enumerate(STAGES):
            if st in ATTN:
                attention(core, st)
            elif st in ("L0f", "L1f", "L2f"):
                experts(core, st)
            else:
                {"L2a": channel_attention, "L2x": retention, "L3a": state_space, "L3f": latent_experts}[st](core)
        finish(core)


def tables():
    f = np.float32
    t = {"ident": np.eye(P, dtype=f), "ones": np.ones((P, P), f)}
    r, c = np.arange(P)[:, None], np.arange(P)[None, :]
    t["tri"] = (r <= c).astype(f)
    t["neg_q"] = np.where(c > r, f(-BIG), f(0))
    t["neg_k"] = np.where(r > c, f(-BIG), f(0))
    t["block_diag"] = np.where(r // 16 == c // 16, f(0), f(-BIG))
    t["pick"] = np.zeros((P, E, P), f)
    t["pick"][np.arange(E), np.arange(E), :] = 1
    t["pick"] = t["pick"].reshape(P, E * P)
    t["pick_pairs"] = np.zeros((P, E, 64), f)
    t["pick_pairs"][np.arange(E), np.arange(E), :] = 1
    t["pick_pairs"] = t["pick_pairs"].reshape(P, E * 64)
    t["countdown"] = np.tile(np.arange(E, 0, -1, dtype=f), (P, 1))
    d = np.arange(P) % 64 // DH
    inv = f(1) / np.power(f(10000), np.arange(0, DH, 2, dtype=f) / f(DH))
    ang = (np.arange(S, dtype=f)[None, :] * inv[d // 2][:, None]).astype(f)
    t["rope_cos"] = np.cos(ang).astype(f)
    t["rope_sin"] = np.where(d[:, None] % 2 == 0, -np.sin(ang), np.sin(ang)).astype(f)
    ch = np.arange(P)
    half = D // 2
    sv = (np.arange(0, D, 2, dtype=f) + f(0.4 * D)) / f(1.4 * D)
    pos = np.arange(S, dtype=f)
    scale = np.power(sv[None, :], (pos / f(512))[:, None]).astype(f)
    freqs = f(1) / np.power(f(10000), np.arange(half, dtype=f) / f(half))
    ang = (pos[:, None] * freqs[None, :]).astype(f)
    for q, sc in (("q", scale), ("k", f(1) / scale)):
        co = (np.cos(ang) * sc).astype(f)[:, ch // 2].T
        si = (np.sin(ang) * sc).astype(f)[:, ch // 2].T
        t[f"x{q}_cos"] = co
        t[f"x{q}_sin"] = np.where(ch[:, None] % 2 == 0, -si, si)
    diff = np.arange(S, dtype=f)[None, :] - np.arange(P, dtype=f)[:, None]
    t["decay0"] = np.where(diff >= 0, np.power(f(0.96875), np.maximum(diff, 0)), f(0)).astype(f)
    return t


def lay_out(i):
    f = np.float32
    a = {k: np.asarray(v) for k, v in i.items()}
    col = dict(tables())

    def stack_order(wt, swap=False):
        x = wt.reshape(wt.shape[:-1] + (H // 2, 2, DH // 2, 2))
        if swap:
            x = x[..., ::-1]
        n = x.ndim
        x = x.transpose(tuple(range(n - 4)) + (n - 3, n - 2, n - 1, n - 4))
        return x.reshape(wt.shape)

    spread = lambda x: np.broadcast_to(x.reshape(1, -1), (P, x.size))
    rows = lambda x: np.concatenate([x, np.zeros((P - x.shape[0],) + x.shape[1:], f)], axis=0)
    wide = lambda x: np.concatenate([x, np.zeros(x.shape[:-1] + (P - x.shape[-1],), f)], axis=-1)
    zero = np.zeros(P, f)
    att = {
        "L0a": (a["L0_attn_Wq"].T, a["L0_attn_bq"], a["L0_attn_Wk"].T, a["L0_attn_bk"], a["L0_attn_Wv"].T,
                a["L0_attn_bv"], a["L0_attn_Wo"].T, a["L0_attn_bo"]),
        "L0x": (a["L0_xattn_wq_k"], a["L0_xattn_wq_b"], a["L0_xattn_wk_k"], a["L0_xattn_wk_b"], a["L0_xattn_wv_k"],
                a["L0_xattn_wv_b"], a["L0_xattn_wo_k"], a["L0_xattn_wo_b"]),
        "L1a": (a["L1_attn_W_q"].T, zero, a["L1_attn_W_k"].T, zero, a["L1_attn_W_v"].T, zero, a["L1_attn_W_o"].T, zero),
        "L1x": (a["L1_xattn_WQ"], a["L1_xattn_bQ"], a["L1_xattn_WK"], a["L1_xattn_bK"], a["L1_xattn_WV"],
                a["L1_xattn_bV"], a["L1_xattn_WO"], a["L1_xattn_bO"]),
        "L3x": (a["L3_xattn_Wq"].T, a["L3_xattn_bq"], a["L3_xattn_Wk"].T, a["L3_xattn_bk"], a["L3_xattn_Wv"].T,
                a["L3_xattn_bv"], a["L3_xattn_Wo"].T, a["L3_xattn_bo"]),
    }
    for st, (wq, bq, wk, bk, wv, bv, wo, bo) in att.items():
        for n, wt, b in (("q", wq, bq), ("k", wk, bk)):
            col[f"{st}_w{n}"], col[f"{st}_w{n}s"] = stack_order(wt), stack_order(wt, True)
            col[f"{st}_b{n}"], col[f"{st}_b{n}s"] = stack_order(b)[:, None], stack_order(b, True)[:, None]
        col[f"{st}_wv"], col[f"{st}_wo"] = wv, wo
        col[f"{st}_bv"], col[f"{st}_bo"] = spread(bv), spread(bo)
    chunked = lambda b: b.reshape(E, FC, P).transpose(2, 0, 1).reshape(P, E * FC)
    col["L0_gate"], col["L0_b1"], col["L0_b2"] = a["L0_ffn_centroids"].T, chunked(a["L0_ffn_b1"]), rows(a["L0_ffn_b2"])
    col["L0_gamma"], col["L0_beta"] = a["L0_ffn_gamma"].T, a["L0_ffn_beta"].T
    col["L1_gate"], col["L1_gate_bias"] = a["L1_ffn_w_gate"], spread(a["L1_ffn_b_gate"])
    col["L1_b1"], col["L1_b2"] = chunked(a["L1_ffn_b1"]), rows(a["L1_ffn_b2"])
    col["L2_gate"], col["L2_gate_bias"] = a["L2_ffn_Wr"].T, spread(a["L2_ffn_br"])
    col["L2_b1"], col["L2_b2"] = chunked(a["L2_ffn_b1"]), rows(a["L2_ffn_b2"])
    col["L2a_qkv"], col["L2a_out"] = a["L2_attn_w_qkv"].T, a["L2_attn_w_out"].T
    col["L2a_norm"] = a["L2_attn_norm_weight"][:, None]
    col["L2a_temp"] = np.repeat(a["L2_attn_temperature"].reshape(-1), 16)[:, None]
    swap = lambda x: x.reshape(D, D // 2, 2)[:, :, ::-1].reshape(D, D)
    for n in "qkv":
        col[f"L2x_{n}"] = a[f"L2_xattn_W{n}"]
        if n != "v":
            col[f"L2x_{n}s"] = swap(a[f"L2_xattn_W{n}"])
    win = a["L3_attn_W_in"].T
    taps = a["L3_attn_conv_w"][:, 0, :].T
    cb = a["L3_attn_conv_b"]
    col["L3a_z"], col["L3a_xs"], col["L3a_b"], col["L3a_c"], col["L3a_dt"] = (
        win[:, 0:256], win[:, 256:512], win[:, 512:576], win[:, 576:640], win[:, 640:642])
    col["L3a_taps_xs"], col["L3a_taps_b"], col["L3a_taps_c"] = (
        spread(taps[:, 0:256]), spread(taps[:, 256:320]), spread(taps[:, 320:384]))
    col["L3a_bias_xs"] = cb[0:256].reshape(2, P).T
    col["L3a_bias_b"], col["L3a_bias_c"] = rows(cb[256:320, None]), rows(cb[320:384, None])
    col["L3a_alog"], col["L3a_dtb"], col["L3a_skip"] = (
        spread(a["L3_attn_A_log"]), spread(a["L3_attn_dt_bias"]), spread(a["L3_attn_D_skip"]))
    col["L3a_out"] = a["L3_attn_W_out"].T.reshape(2, P, D).transpose(1, 0, 2).reshape(P, 2 * D)
    col["L3f_gate"], col["L3f_corr"] = a["L3_ffn_gate"].T, spread(a["L3_ffn_corr_bias"])
    col["L3f_fc1"] = wide(a["L3_ffn_fc1_w"].T)
    col["L3f_w1"] = rows(a["L3_ffn_w1"].transpose(2, 0, 1).reshape(64, E * 64))
    col["L3f_w2"] = wide(a["L3_ffn_w2"].transpose(0, 2, 1).reshape(4, P, 64)).transpose(1, 0, 2).reshape(P, 4 * P)
    col["L3f_fc2"] = rows(a["L3_ffn_fc2_w"].T)
    col["L3f_up"] = a["L3_ffn_up_w"].T
    col["L3f_down"] = a["L3_ffn_down_w"].T.reshape(4, P, D).transpose(1, 0, 2).reshape(P, 4 * D)
    packs = {f"small_{st}": np.concatenate([col[n] for n, _ in pairs], axis=1).astype(f, copy=False)
             for st, pairs in {"common": COMMON, **WEIGHTS}.items()}

    first = lambda x: np.ascontiguousarray(x.transpose(1, 0, 2).reshape(P, E * F))
    second = lambda x: np.ascontiguousarray(x.reshape(E, FC, P, D).transpose(2, 0, 1, 3).reshape(P, E * F))
    return {
        **packs, "pick_rows": col["pick"],
        "x": a["x"].reshape(B * S, D), "ctx": a["ctx_1024"].reshape(B * S, D),
        "mask0q": a["mask_BxSxS2_ik1"], "mask0k": np.ascontiguousarray(a["mask_BxSxS2_ik1"].transpose(0, 2, 1)),
        "mask1q": np.ascontiguousarray(a["mask_Bx1xSxS2_ik1"][:, 0]),
        "mask1k": np.ascontiguousarray(a["mask_Bx1xSxS2_ik1"][:, 0].transpose(0, 2, 1)),
        "gate_prob": np.ascontiguousarray(a["fside_BxSxS2_0"].transpose(0, 2, 1)),
        "L0_ffn1": first(a["L0_ffn_w1"]), "L0_ffn2": second(a["L0_ffn_w2"]),
        "L1_ffn1": first(a["L1_ffn_W1"]), "L1_ffn2": second(a["L1_ffn_W2"]),
        "L2_ffn1": first(a["L2_ffn_W1"].transpose(0, 2, 1)), "L2_ffn2": second(a["L2_ffn_W2"].transpose(0, 2, 1)),
    }


def kernel(**inputs):
    import concourse.bacc as bacc
    from concourse.bass_utils import run_bass_kernel_spmd

    nc = bacc.Bacc("TRN2", target_bir_lowering=False, num_devices=1)
    arrays = lay_out(inputs)
    dram = {n: nc.dram_tensor(n, a.shape, mybir.dt.from_np(a.dtype), kind="ExternalInput").ap()
            for n, a in arrays.items()}
    dram["out"] = nc.dram_tensor("out", (B * S, D), F32, kind="ExternalOutput").ap()
    for n in "qk":
        dram[f"{n}_bounce"] = nc.dram_tensor(f"{n}_bounce", (2, len(Q_PARTS), 64, NT), BF16, kind="Internal").ap()
    dram["m_bounce"] = nc.dram_tensor("m_bounce", (NMAX * H, NT), BF16, kind="Internal").ap()
    program(nc, dram)
    r = run_bass_kernel_spmd(nc, [arrays], core_ids=[0])
    return r.results[0]["out"].reshape(B, S, D)
```

```python
from contextlib import ExitStack

import concourse.bass as bass
import numpy as np
from concourse import mybir

F32 = mybir.dt.float32
BF16 = mybir.dt.bfloat16
I32 = mybir.dt.int32
ALU = mybir.AluOpType
ACT = mybir.ActivationFunctionType
AX = mybir.AxisListType.X

P = 128
B, S, D = 8, 256, 128
NSEQ = 2
NPASS = B // NSEQ
NT = NSEQ * S
T = NT // P
TS = S // P
H, DH = 16, 8
HP = H // 2
DEPTH = 3
E, F = 8, 512
FC = F // P
TAPS = 4
EPS = 1e-5
BIG = 2.0 ** 100

SLOT = {"q": (0, 1, 2), "k": (1, 2, 0)}
MAX_ROW = 32
PAIR_ROW = 40
NMAX = 3


ATTN = ("L0a", "L0x", "L1a", "L1x", "L3x")
STAGES = ("L0a", "L0x", "L0f", "L1a", "L1x", "L1f", "L2a", "L2x", "L2f", "L3a", "L3x", "L3f")

COMMON = [("ident", P), ("neg_q", P), ("neg_k", P), ("rope_cos", S), ("rope_sin", S), ("tri", P), ("ones", P),
          ("countdown", E)]
WEIGHTS = {st: [(f"{st}_{n}", k) for n, k in (
    ("wq", P), ("wqs", P), ("wk", P), ("wks", P), ("wv", P), ("wo", P),
    ("bq", 1), ("bqs", 1), ("bk", 1), ("bks", 1), ("bv", P), ("bo", P))] for st in ATTN}
WEIGHTS["L0f"] = [("L0_gate", E), ("L0_b1", E * FC), ("L0_b2", P), ("L0_gamma", E), ("L0_beta", E)]
WEIGHTS["L1f"] = [("L1_gate", E), ("L1_gate_bias", E), ("L1_b1", E * FC), ("L1_b2", P)]
WEIGHTS["L2f"] = [("L2_gate", E), ("L2_gate_bias", E), ("L2_b1", E * FC), ("L2_b2", P)]
WEIGHTS["L2a"] = [("L2a_qkv", 3 * P), ("L2a_out", P), ("L2a_norm", 1), ("L2a_temp", 1), ("block_diag", P)]
WEIGHTS["L2x"] = [("L2x_q", P), ("L2x_qs", P), ("L2x_k", P), ("L2x_ks", P), ("L2x_v", P),
                  ("xq_cos", S), ("xq_sin", S), ("xk_cos", S), ("xk_sin", S), ("decay0", S)]
WEIGHTS["L3a"] = [("L3a_z", 2 * P), ("L3a_xs", 2 * P), ("L3a_b", 64), ("L3a_c", 64), ("L3a_dt", 2),
                  ("L3a_taps_xs", TAPS * 2 * P), ("L3a_taps_b", TAPS * 64), ("L3a_taps_c", TAPS * 64),
                  ("L3a_bias_xs", 2), ("L3a_bias_b", 1), ("L3a_bias_c", 1), ("L3a_alog", 2), ("L3a_dtb", 2),
                  ("L3a_skip", 2), ("L3a_out", 2 * P)]
WEIGHTS["L3f"] = [("L3f_gate", E), ("L3f_corr", E), ("L3f_fc1", P), ("L3f_w1", E * 64), ("L3f_w2", 4 * P),
                  ("L3f_fc2", P), ("L3f_up", 4 * P), ("L3f_down", 4 * P), ("pick_pairs", 4 * P)]


def ranges(pairs):
    out, at = {}, 0
    for name, n in pairs:
        out[name] = (at, at + n)
        at += n
    return out


COLS = {}
for _pairs in (COMMON, *WEIGHTS.values()):
    COLS.update(ranges(_pairs))
width = lambda pairs: sum(n for _, n in pairs)
STAGE_COLS = max(width(pairs) for pairs in WEIGHTS.values())

KEEP = """x_in w_in stage_w ffn_w0 ffn_w1 ffn_w2 ctx_tok ctx_psum ctx_done setup out_done
go_pe go_act go_dve go_pool q_stack0 q_stack1 q_stack2 k_stack0 k_stack1 k_stack2 m_stack""".split()
ALL_STAGES = "iter_done dve_step act_step pool_step ln_mv ln_r0 xn_ready xT_psum xT_ready y_psum".split()
PASS_SEMS = {
    "attention": """kv_ready q_psum k_psum v_psum v_ready q_p1 q_rest q_p2 q_p3 q_full k_p1 k_rest k_p2 k_p3 k_full
        zero_max x_done q_bounce k_bounce m_bounce mask_in mask_ready gp_in s_psum s_max m_parts mT_psum mT_ready
        st_psum p_ready pg_ready pv_done o_ready tr_psum a_ready aT_psum aT_ready xb_ready""".split(),
    "experts": """xh_ready xhT_psum xhT_ready gate_psum gate_mask maskT_psum maskT_ready gexp_in gexp_out he_ready
        z_psum h_raw g_psum h_ready h_used yT_ready""".split(),
    "channel_attention": """xh_ready q_psum v_ready gexp_in gexp_out a_in a_out b_in b_out c_in c_out d_in d_out
        e_in f_in f_out""".split(),
    "retention": "kv_ready q_psum k_psum v_psum v_ready a_in a_out b_in".split(),
    "state_space": """v_ready tr_psum gexp_in gexp_out z_psum h_raw h_ready a_in a_out b_in b_out c_in c_out
        d_in d_out e_out f_in f_out""".split(),
    "latent_experts": """gate_psum gate_mask maskT_psum maskT_ready gexp_in gexp_out z_psum h_raw g_psum h_ready
        h_used yT_ready a_in a_out b_in b_out c_in""".split(),
}
SEMS = list(dict.fromkeys(KEEP + ALL_STAGES + sum(PASS_SEMS.values(), [])))


class Step:

    def __init__(self, eng, sem):
        self.eng, self.sem, self.n = eng, sem, 0

    def mark(self, ins):
        self.n += 1
        return ins.then_inc(self.sem, 1)

    def __call__(self, ins):
        self.mark(ins)
        self.eng.wait_ge(self.sem, self.n)


class Core:

    def __init__(self, nc, ctx, dram):
        self.nc, self.dram = nc, dram
        self.sem = {n: ctx.enter_context(nc.semaphore(n)) for n in SEMS}
        sb = lambda name, shape, dt=F32: ctx.enter_context(nc.sbuf_tensor(name, shape, dt))
        self.X = sb("X", [P, B * TS, D])
        self.ctxT = sb("ctxT", [P, B * S])
        self.W = sb("W", [P, width(COMMON)])
        self.stage_W = [sb(f"stage_W{k}", [P, STAGE_COLS]) for k in range(2)]
        self.at = 0
        self.ffn = [sb(f"ffn_w{n}_", [P, E * F]) for n in (1, 2)]
        self.ident_b = sb("ident_b", [P, P], BF16)
        self.neg_q = sb("neg_q", [P, P], BF16)
        self.neg_k = sb("neg_k", [P, P], BF16)
        self.pick = sb("pick", [P, E * P], BF16)
        self.Qm = sb("Qm", [P, DEPTH, 2, HP, S], BF16)
        self.Kst = sb("Kst", [P, DEPTH, HP, S], BF16)
        self.vaug = sb("vaug", [P, DEPTH, TS, H, 32])
        self.n_setup = 0
        self.PS = ctx.enter_context(nc.psum_tensor("PS", [P, 8, 512], F32))

    def buffers(self, stack):
        st = STAGES[self.at]
        return lambda name, shape, dt=F32: stack.enter_context(self.nc.sbuf_tensor(f"{st}_{name}", shape, dt))

    def w(self, name, rows=P):
        a, b = COLS[name]
        src = self.W if name in dict(COMMON) else self.stage_W[self.at % 2]
        return src[0:rows, a:b]


def load_next_weights(core, sp):
    if core.at + 1 < len(STAGES):
        st = STAGES[core.at + 1]
        sp.dma_start(core.stage_W[(core.at + 1) % 2][:, 0:width(WEIGHTS[st])], core.dram[f"small_{st}"])\
            .then_inc(core.sem["stage_w"], 16)


def await_next_weights(core, sp):
    if core.at + 1 < len(STAGES):
        sp.wait_ge(core.sem["stage_w"], 16 * (core.at + 2))


def end_pass(core, eng, go):
    eng.drain().then_inc(core.sem["iter_done"], 1)
    eng.wait_ge(core.sem[go], 1)
    eng.sem_clear(core.sem[go])


def end_pass_sync(core, sp, kind):
    sp.wait_ge(core.sem["iter_done"], 4)
    for name in ALL_STAGES + PASS_SEMS[kind]:
        sp.sem_clear(core.sem[name])
    for go in ("go_pe", "go_act", "go_dve", "go_pool"):
        sp.sem_inc(core.sem[go], 1)


def ln_buffers(core, c, tiles=T):
    sb = core.buffers(c)
    return dict(st=sb("ln_st", [P, tiles, 6]), mv=sb("ln_mv_", [P, 2, tiles, 2]), lnv=sb("ln_lnv", [P, 2, tiles]),
                r0=sb("ln_r0_", [P, 2, tiles]), sq=sb("ln_sq", [P, 2, tiles]), w=sb("ln_w", [P, 2, tiles]),
                r=sb("ln_r", [P, 2, tiles]), xn=sb("xn", [P, tiles, D]), xT=sb("xT", [P, tiles * P]))


def tokens_of(core, it):
    return core.X[:, bass.ds(it * T, T), :]


def tile_of(core, it, t):
    return core.X[:, bass.ds(it * T + t, 1), :].rearrange("p a d -> p (a d)")


def dve_norm_stats(core, dve, step, L, src, n, tiles, slot=0, rms=False, eps=EPS):
    v, s = core.nc.vector, core.sem
    mv, u = L["mv"][:, slot], L["sq"][:, slot]
    for t in range(tiles):
        step.mark(v.bn_stats(L["st"][:, t, :], src(t)))
    dve.wait_ge(s["dve_step"], step.n)
    for t in range(tiles):
        step.mark(v.bn_aggr(mv[:, t, :], L["st"][:, t, :]))
    dve.wait_ge(s["dve_step"], step.n)
    if rms:
        step(v.tensor_tensor(u, mv[:, :, 0], mv[:, :, 0], ALU.mult))
        step(v.tensor_tensor(mv[:, :, 1], mv[:, :, 1], u, ALU.add))
    v.tensor_scalar(L["w"][:, slot], mv[:, :, 1], eps, None, ALU.add).then_inc(s["ln_mv"], 1)


def dve_norm_apply(core, dve, step, L, src, dst, ready, n, tiles, slot=0, rms=False):
    v, s = core.nc.vector, core.sem
    mv, u = L["mv"][:, slot], L["sq"][:, slot]
    dve.wait_ge(s["ln_mv"], n + 1)
    dve.wait_ge(s["ln_r0"], n + 1)
    step(v.tensor_tensor(u, L["r0"][:, slot], L["r0"][:, slot], ALU.mult))
    step(v.tensor_tensor(u, u, L["w"][:, slot], ALU.mult))
    step(v.tensor_scalar(u, u, -0.5, 1.5, ALU.mult, ALU.add))
    step(v.tensor_tensor(L["r"][:, slot], L["r0"][:, slot], u, ALU.mult))
    for t in range(tiles):
        r = L["r"][:, slot, t:t + 1]
        ops = (r, None, ALU.mult) if rms else (mv[:, t, 0:1], r, ALU.subtract, ALU.mult)
        v.tensor_scalar(dst[:, t, :], src(t), *ops).then_inc(ready, 1)


def dve_layernorm(core, dve, step, L, src, dst, ready, n=0, rms=False, eps=EPS):
    dve_norm_stats(core, dve, step, L, src, n, T, n, rms, eps)
    dve_norm_apply(core, dve, step, L, src, dst, ready, n, T, n, rms)


def act_layernorm(core, act, step, L, n=0, slot=None):
    a, s = core.nc.scalar, core.sem
    slot = n if slot is None else slot
    act.wait_ge(s["ln_mv"], n + 1)
    step(a.activation(L["lnv"][:, slot], L["w"][:, slot], ACT.Ln))
    a.activation(L["r0"][:, slot], L["lnv"][:, slot], ACT.Exp, scale=-0.5).then_inc(s["ln_r0"], 1)


def pe_turn(core, pe, src, bank, ready, done, tiles=T):
    for t in range(tiles):
        pe.wait_ge(ready, t + 1)
        ins = core.nc.tensor.transpose(core.PS[:, bank, t * P:(t + 1) * P], src[:, t, :], core.w("ident"))
    ins.then_inc(done, 1)


def act_copy(core, act, out, src, wait, n, done):
    act.wait_ge(wait, n)
    core.nc.scalar.activation(out, src, ACT.Copy).then_inc(done, 1)


def dve_residual(core, dve, it, add, wait, base=None):
    dve.wait_ge(wait, 1)
    x = tokens_of(core, it)
    core.nc.vector.tensor_tensor(x, add.rearrange("p (t d) -> p t d", t=T), x if base is None else base, ALU.add)


def attention(core, st):
    nc, s, PS, w = core.nc, core.sem, core.PS, core.w
    rope = st in ("L0a", "L1a")
    causal = rope
    masked = st in ("L0x", "L1x")
    gated = st == "L0x"
    cross = not rope
    bias = st != "L1a"
    SCALE = float(1.0 / np.sqrt(np.float32(DH)))
    NG = H // 4
    UNITS = [(t, g) for t in range(TS) for g in range(NG)]
    NU = len(UNITS)
    LEAD = 2
    S_BANK, T_BANK, O_BANK, FRONT = 0, 2, 4, 6

    with ExitStack() as c:
        sb = core.buffers(c)
        L = ln_buffers(core, c, TS)
        Qm, Kst, vaug = core.Qm, core.Kst, core.vaug
        Pr = sb("Pr", [P, 2, 4 * S])
        Osb = sb("Osb", [P, NG, S])
        part = {n: sb(f"{n}part", [P, 3, S], BF16) for n in "qk"}
        rest = {n: sb(f"{n}rest", [P, S]) for n in "qk"}
        rot = {n: sb(f"{n}rot", [P, 3, S]) for n in "qk"} if rope else None
        mx = sb("mx", [P, TS, H])
        mrest = sb("mrest", [P, TS, H])
        mpart = sb("mpart", [P, TS, NMAX, H], BF16)
        mT = sb("mT", [NMAX * H, S], BF16)
        rden = sb("rden", [P, TS, H])
        A, AT = sb("A", [P, TS, D]), sb("AT", [P, S])
        Xb = sb("Xb", [P, TS, D]) if bias else None
        kvT = sb("kvT", [P, S]) if cross else L["xT"]
        if masked:
            msk = sb("msk", [P, 2, TS, S], I32)
            neg = sb("neg", [P, DEPTH, 2, TS, S], BF16)
        if gated:
            G = sb("G", [P, DEPTH, TS, S])
            PG = sb("PG", [P, 2, 4 * S])
            den = sb("den", [P, 32])
        first = core.at == 0
        set_ready = core.n_setup
        core.n_setup += (7 if first else 0) + (2 if gated else 1)
        bank_of = {"k": FRONT + 1, "q": FRONT}

        def stages_of(run_step, segment_end, loop, first_norm=lambda p: None):
            first_norm(0)
            run_step((0, 0, 0), None, None, None, norm=(1, 1))
            run_step((1, 1, 1), None, None, None)
            run_step(None, (0, 0, 0), None, None)
            segment_end()
            with loop(0, (B - 2) // DEPTH) as it:
                first_norm(it * DEPTH + 2)
                for k in range(DEPTH):
                    p = it * DEPTH + k
                    run_step((p + 2, k, (k + 2) % DEPTH), (p + 1, k, (k + 1) % DEPTH), (p, k, k),
                             (p - 1, k - 1) if k > 0 else None,
                             norm=(p + 3, k + 1) if k + 1 < DEPTH else None)
                run_step(None, None, None, (it * DEPTH + DEPTH - 1, DEPTH - 1))
                segment_end()
            run_step(None, (B - 1, 0, (B - 1) % DEPTH), (B - 2, 0, (B - 2) % DEPTH), None)
            run_step(None, None, (B - 1, 1, (B - 1) % DEPTH), (B - 2, 0))
            run_step(None, None, None, (B - 1, 1))
            segment_end()

        in_loop = [False]
        tok = lambda p, t: core.X[:, bass.ds(p * TS + t, 1), :].rearrange("p a d -> p (a d)")

        with nc.Block() as block:

            @block.sync
            def _(sp):
                load_next_weights(core, sp)
                if st == "L1a":
                    load_ffn(core, sp, "L1")
                name = "mask0" if st == "L0x" else "mask1"

                def run_step(front, maxima, output, tail, norm=None):
                    if front and masked:
                        p, i, buf = front
                        if i > 0:
                            sp.wait_ge(s["mask_ready"], 2 * i)
                        for k in range(2):
                            sp.dma_start(msk[:, k, :, :], core.dram[name + "qk"[k]][bass.ds(p, 1)]
                                         .rearrange("b (t p) k -> p (b t) k", p=P)).then_inc(s["mask_in"], 16)
                    if front and gated:
                        if output and i > 0:
                            sp.wait_ge(s["pg_ready"], NU * i)
                        sp.dma_start(G[:, buf], core.dram["gate_prob"][bass.ds(p, 1)]
                                     .rearrange("b (t p) k -> p (b t) k", p=P)).then_inc(s["gp_in"], 16)
                    if front:
                        p, i, buf = front
                        for what in "kq":
                            sp.wait_ge(s[what + "_p2"], i + 1)
                            sp.wait_ge(s[what + "_p3"], i + 1)
                            for par in range(2):
                                sp.dma_start(core.dram[what + "_bounce"][buf, par].rearrange("c r t -> r c t"),
                                             part[what][64 * par:64 * par + 64]).then_inc(s[what + "_bounce"], 16)
                        if output and i > 0:
                            sp.wait_ge(s["st_psum"], NU * i)
                        if first:
                            sp.wait_ge(s["setup"], core.n_setup if output else set_ready + 2 * (i + 1))
                        for what in "kq":
                            sp.wait_ge(s[what + "_bounce"], 32 * (i + 1))
                            for par in range(2):
                                slots = core.dram[what + "_bounce"][buf, par].rearrange("c (d p) t -> (c d) (p t)", p=HP)
                                stack = Kst[:, buf] if what == "k" else Qm[:, buf, par]
                                twice = lambda rows, n: rows.unsqueeze(0).broadcast_to([2, n, HP * S])
                                if what == "k":
                                    runs = ((0, 4, twice(slots[DH:3 * DH], 2 * DH)), (PAIR_ROW, 2, slots[0:2 * DH]))
                                else:
                                    pair = slots.rearrange("(c d) x -> c d x", d=DH)[0:3:2]
                                    runs = ((0, 2, twice(slots[0:DH], DH)), (2 * DH, 2, twice(slots[DH:2 * DH], DH)),
                                            (PAIR_ROW, 2, pair))
                                for row, blocks, src in runs:
                                    sp.dma_start(stack[64 * par + row:64 * par + row + blocks * DH], src)\
                                        .then_inc(s[f"{what}_stack{buf}"], 16)
                    if maxima:
                        p, i, buf = maxima
                        sp.wait_ge(s["mT_ready"], i + 1)
                        sp.dma_start(core.dram["m_bounce"], mT[:, :]).then_inc(s["m_bounce"], 16)
                        sp.wait_ge(s["m_bounce"], 16 * (i + 1))
                        for par in range(2):
                            sp.dma_start(Qm[64 * par + MAX_ROW:64 * par + MAX_ROW + NMAX, buf, par],
                                         core.dram["m_bounce"].rearrange("(c r p) t -> r c p t", c=NMAX, r=2)[par])\
                                .then_inc(s["m_stack"], 16)

                stages_of(run_step, lambda: end_pass_sync(core, sp, "attention"), sp.Fori)
                await_next_weights(core, sp)

            @block.gpsimd
            def _(pool):
                g = nc.gpsimd
                def set_up(k):
                    g.memset(Kst[:, k], -1.0).then_inc(s["setup"], 1)
                    g.memset(Qm[:, k], 0.0).then_inc(s["setup"], 1)

                def run_step(front, maxima, output, tail, norm=None):
                    if front:
                        p, i, buf = front
                        if cross:
                            if i > 0:
                                pool.wait_ge(s["v_psum"], i)
                            g.tensor_copy(kvT[:, :], core.ctxT[:, bass.ds(p * S, S)]).then_inc(s["kv_ready"], 1)
                        if masked:
                            pool.wait_ge(s["mask_in"], 32 * (i + 1))
                            if output and i > 0:
                                pool.wait_ge(s["st_psum"], NU * i)
                            for k in range(2):
                                if st == "L1x":
                                    ops = (0.0, -BIG, ALU.is_equal, ALU.mult)
                                else:
                                    ops = (2.0 ** 31, -2.0 ** 31, ALU.mult, ALU.add)
                                g.tensor_scalar(neg[:, buf, k], msk[:, k], *ops).then_inc(s["mask_ready"], 1)
                    if tail and bias:
                        p, i = tail
                        if i > 0:
                            pool.wait_ge(s["x_done"], i)
                        for t in range(TS):
                            g.tensor_tensor(Xb[:, t, :], tok(p, t), w(f"{st}_bo"), ALU.add).then_inc(s["xb_ready"], 1)

                    if first and front and not output:
                        set_up(front[2])
                    if maxima and not output:
                        if first:
                            set_up(DEPTH - 1)
                            g.memset(vaug[:, :, :, :, DH + 1:32], 0.0).then_inc(s["setup"], 1)
                        g.memset(vaug[:, :, :, :, DH:DH + 1], 0.0 if gated else 1.0).then_inc(s["setup"], 1)
                        if gated:
                            g.tensor_scalar(den[:, :], w("ones")[:, 0:32], 0.0, None, ALU.mult)\
                                .then_inc(s["pool_step"], 1)
                            pool.wait_ge(s["pool_step"], 1)
                            g.memset(den[:, DH:DH + 1], 1.0).then_inc(s["setup"], 1)

                stages_of(run_step, lambda: end_pass(core, pool, "go_pool"), pool.Fori)

            @block.tensor
            def _(pe):
                mm, tr = nc.tensor.matmul, nc.tensor.transpose
                free = dict(skip_group_check=True)

                def turn_norm(i):
                    for t in range(TS):
                        pe.wait_ge(s["xn_ready"], TS * i + t + 1)
                        ins = tr(PS[:, FRONT, t * P:(t + 1) * P], L["xn"][:, t, :], w("ident"))
                    ins.then_inc(s["xT_psum"], 1)

                def project(i):
                    if cross:
                        pe.wait_ge(s["kv_ready"], i + 1)
                    pe.wait_ge(s["xT_ready"], i + 1)
                    for what, src in (("k", kvT), ("q", L["xT"])):
                        if rope:
                            mm(PS[:, bank_of[what], S:2 * S], w(f"{st}_w{what}s"), src[:, :], start=True, stop=True, **free)
                        mm(PS[:, bank_of[what], 0:S], w(f"{st}_w{what}"), src[:, :], start=not rope, stop=True, **free)\
                            .then_inc(s[what + "_psum"], 1)

                def project_v(i):
                    pe.wait_ge(s["k_full" if rope else "k_rest"], i + 1)
                    for t in range(TS):
                        ins = mm(PS[:, FRONT + 1, t * P:(t + 1) * P], kvT[:, t * P:(t + 1) * P], w(f"{st}_wv"),
                                 start=(t == 0), stop=True, **free)
                    ins.then_inc(s["v_psum"], 1)

                def scores(i, buf, u, front_here):
                    tt, g = UNITS[u]
                    if u == 0:
                        for what, dmas in ((f"k_stack{buf}", 4), (f"q_stack{buf}", 6)):
                            pe.wait_ge(s[what], 16 * dmas)
                            pe.sem_clear(s[what])
                    if u == 0 and i > 0:
                        pe.wait_ge(s["mT_ready"], i)
                    if u == 0 and front_here:
                        if i > 0 or not first:
                            pe.wait_ge(s["zero_max"], 2 * max(i, 1))
                        if masked:
                            pe.wait_ge(s["mask_ready"], 2 * max(i, 1))
                    if u > 0:
                        pe.wait_ge(s["s_max"], NU * i + u)
                    nk = (tt + 1) * P if causal else S
                    for pp in range(2):
                        for par in range(2):
                            mm(PS[:, S_BANK + par, pp * S:pp * S + nk], Qm[:, buf, par, 2 * g + pp, tt * P:(tt + 1) * P],
                               Kst[:, buf, 2 * g + pp, 0:nk], start=(pp == 0), stop=True, **free)\
                                if not (pp == 1 and par == 1 and not (causal or masked)) else\
                                mm(PS[:, S_BANK + par, pp * S:pp * S + nk], Qm[:, buf, par, 2 * g + pp, tt * P:(tt + 1) * P],
                                   Kst[:, buf, 2 * g + pp, 0:nk], start=False, stop=True, **free).then_inc(s["s_psum"], 1)
                    for par in range(2):
                        o = PS[:, S_BANK + par, :].rearrange("p (a k) -> p a k", a=2)
                        if causal:
                            ins = mm(o[:, :, tt * P:tt * P + P], core.ident_b[:, :],
                                     core.neg_q[:, :].unsqueeze(1).broadcast_to([P, 2, P]), start=False, stop=True, **free)
                        if masked:
                            ins = mm(o, core.ident_b[:, :], neg[:, buf, 0, tt].unsqueeze(1).broadcast_to([P, 2, S]),
                                     start=False, stop=True, **free)
                    if causal or masked:
                        ins.then_inc(s["s_psum"], 1)

                def turn_max(i):
                    pe.wait_ge(s["m_parts"], i + 1)
                    for tt in range(TS):
                        ins = tr(PS[0:NMAX * H, S_BANK, tt * 64:tt * 64 + 64].bitcast(BF16),
                                 mpart[:, tt].rearrange("p c h -> p (c h)"), core.ident_b[:, :])
                    ins.then_inc(s["mT_psum"], 1)

                def keyed_scores(i, buf, v):
                    kt, g = UNITS[v]
                    if v == 0:
                        pe.wait_ge(s["m_stack"], 32)
                        pe.sem_clear(s["m_stack"])
                    if NU * i + v > 0:
                        pe.wait_ge(s["p_ready"], NU * i + v)
                    q0 = kt * P if causal else 0
                    nq = S - q0
                    for pp in range(2):
                        o = PS[:, T_BANK + pp, 0:2 * nq].rearrange("p (a q) -> p a q", a=2)
                        ins = mm(o, Kst[:, buf, 2 * g + pp, kt * P:(kt + 1) * P], Qm[:, buf, :, 2 * g + pp, q0:S],
                                 start=True, stop=True, **free)
                        if causal:
                            ins = mm(o[:, :, 0:P], core.ident_b[:, :],
                                     core.neg_k[:, :].unsqueeze(1).broadcast_to([P, 2, P]), start=False, stop=True, **free)
                        if masked:
                            ins = mm(o, core.ident_b[:, :], neg[:, buf, 1, kt].unsqueeze(1).broadcast_to([P, 2, S]),
                                     start=False, stop=True, **free)
                    ins.then_inc(s["st_psum"], 1)

                def times_v(i, buf, v):
                    kt, g = UNITS[v]
                    pe.wait_ge(s["p_ready"], NU * i + v + 1)
                    if gated:
                        pe.wait_ge(s["pg_ready"], NU * i + v + 1)
                    if v == 0:
                        pe.wait_ge(s["setup"], core.n_setup)
                    if v == 0 and i > 0:
                        pe.wait_ge(s["o_ready"], i)
                    q0 = kt * P if causal else 0
                    nq = S - q0
                    for j in range(4):
                        o = PS[32 * j:32 * j + 32, O_BANK + g // 2, (g % 2) * S + q0:(g % 2) * S + S]
                        opening = kt == 0 and g % 2 == 0
                        probs = Pr[:, v % 2, j * nq:(j + 1) * nq]
                        if gated:
                            ins = mm(o, vaug[:, buf, kt, 4 * g + j, :], PG[:, v % 2, j * nq:(j + 1) * nq],
                                     start=opening, stop=True, **free)
                            ins = mm(o, den[:, :], probs, start=False, stop=True, **free)
                        else:
                            ins = mm(o, vaug[:, buf, kt, 4 * g + j, :], probs, start=opening, stop=True, **free)
                    ins.then_inc(s["pv_done"], 1)

                def turn_heads(i, front):
                    pe.wait_ge(s["o_ready"], i + 1)
                    for t in range(TS):
                        if front and t == 0:
                            pe.wait_ge(s["q_full" if rope else "q_rest"], front[1] + 1)
                        if front and t == 1:
                            pe.wait_ge(s["v_ready"], front[1] + 1)
                        for g in range(NG):
                            ins = tr(PS[:, FRONT + t, g * P:(g + 1) * P], Osb[:, g, t * P:(t + 1) * P], w("ident"))
                        ins.then_inc(s["tr_psum"], 1)

                def turn_context(i):
                    pe.wait_ge(s["a_ready"], TS * (i + 1))
                    for t in range(TS):
                        ins = tr(PS[:, FRONT, t * P:(t + 1) * P], A[:, t, :], w("ident"))
                    ins.then_inc(s["aT_psum"], 1)

                def times_wo(i):
                    pe.wait_ge(s["aT_ready"], i + 1)
                    for t in range(TS):
                        ins = mm(PS[:, FRONT + 1, t * P:(t + 1) * P], AT[:, t * P:(t + 1) * P], w(f"{st}_wo"),
                                 start=(t == 0), stop=True, **free)
                    ins.then_inc(s["y_psum"], 1)

                def run_step(front, maxima, output, tail, norm=None):
                    if front and output and output[1] > 1:
                        pe.wait_ge(s["x_done"], output[1] - 1)
                    for u in range(NU + LEAD):
                        if maxima and u < NU:
                            scores(maxima[1], maxima[2], u, maxima[1] > 0 or not output)
                        if output and u >= LEAD:
                            keyed_scores(output[1], output[2], u - LEAD)
                        if output and u > LEAD:
                            times_v(output[1], output[2], u - LEAD - 1)
                        if front and u == 0:
                            turn_norm(front[1])
                        if front and u == 1:
                            project(front[1])
                        if front and u == 3:
                            project_v(front[1])
                        if tail and u == 6:
                            turn_heads(tail[1], front)
                        if maxima and u == NU:
                            turn_max(maxima[1])
                        if tail and u == 9:
                            turn_context(tail[1])
                    if output:
                        times_v(output[1], output[2], NU - 1)
                    if tail:
                        times_wo(tail[1])

                stages_of(run_step, lambda: end_pass(core, pe, "go_pe"), pe.Fori)

            @block.scalar
            def _(act):
                a = nc.scalar.activation
                step = Step(act, s["act_step"])

                def cut_first(what, i):
                    if rope:
                        act.wait_ge(s[what + "_full"], i + 1)
                        src = dict(in_=rot[what][:, 2, :], func=ACT.Copy)
                    else:
                        act.wait_ge(s[what + "_psum"], i + 1)
                        src = dict(in_=PS[:, bank_of[what], 0:S], func=ACT.Identity, bias=w(f"{st}_b{what}"))
                    if i > 0:
                        act.wait_ge(s[what + "_bounce"], 32 * i)
                    a(part[what][:, SLOT[what][0], :], **src).then_inc(s[what + "_p1"], 1)

                def cut_second(what, i):
                    act.wait_ge(s[what + "_rest"], i + 1)
                    a(part[what][:, SLOT[what][1], :], rest[what][:, :], ACT.Copy).then_inc(s[what + "_p2"], 1)

                def exponentials(i, u):
                    kt, g = UNITS[u]
                    act.wait_ge(s["st_psum"], NU * i + u + 1)
                    if NU * i + u >= 2:
                        act.wait_ge(s["pv_done"], NU * i + u - 1)
                    nq = S - kt * P if causal else S
                    a(Pr[:, u % 2, 0:4 * nq].rearrange("p (a k) -> p a k", a=2),
                      PS[:, T_BANK:T_BANK + 2, 0:2 * nq], ACT.Exp, scale=SCALE).then_inc(s["p_ready"], 1)

                def run_step(front, maxima, output, tail, norm=None):
                    for u in range(NU + LEAD):
                        if output and u >= LEAD:
                            exponentials(output[1], u - LEAD)
                        if front and u == 0:
                            act_copy(core, act, L["xT"][:, :], PS[:, FRONT, 0:S], s["xT_psum"], front[1] + 1, s["xT_ready"])
                        if front and u == 2:
                            cut_first("k", front[1])
                        if front and u == 3:
                            cut_first("q", front[1])
                        if front and u == 4:
                            cut_second("k", front[1])
                            cut_second("q", front[1])
                        if maxima and u == NU:
                            i = maxima[1]
                            act.wait_ge(s["mT_psum"], i + 1)
                            if i > 0:
                                act.wait_ge(s["m_bounce"], 16 * i)
                            a(mT[:, :], PS[0:NMAX * H, S_BANK, 0:P].bitcast(BF16), ACT.Copy).then_inc(s["mT_ready"], 1)
                        if norm and u == NU:
                            act_layernorm(core, act, step, L, n=norm[1], slot=0)
                    if tail:
                        act_copy(core, act, AT[:, :], PS[:, FRONT, 0:S], s["aT_psum"], tail[1] + 1, s["aT_ready"])

                def segment_end():
                    end_pass(core, act, "go_act")
                    step.n = 0

                stages_of(run_step, segment_end, act.Fori, lambda p: act_layernorm(core, act, step, L, n=0, slot=0))

            @block.vector
            def _(dve):
                v = nc.vector
                step = Step(dve, s["dve_step"])

                def apply_norm(p, i):
                    if i > 0:
                        dve.wait_ge(s["xT_psum"], i)
                    dve_norm_apply(core, dve, step, L, lambda t: tok(p, t), L["xn"], s["xn_ready"], i, TS)

                def first_norm(p):
                    dve_norm_stats(core, dve, step, L, lambda t: tok(p, t), 0, TS)
                    apply_norm(p, 0)

                def rotate(what, i):
                    b = bank_of[what]
                    dve.wait_ge(s[what + "_psum"], i + 1)
                    for n, (tab, sw) in enumerate((("rope_cos", ""), ("rope_sin", "s"))):
                        step.mark(v.scalar_tensor_tensor(rot[what][:, n, :], PS[:, b, n * S:(n + 1) * S],
                                                         w(f"{st}_b{what}{sw}"), w(tab), ALU.add, ALU.mult))
                    dve.wait_ge(s["dve_step"], step.n)
                    v.tensor_tensor(rot[what][:, 2, :], rot[what][:, 0, :], rot[what][:, 1, :], ALU.add)\
                        .then_inc(s[what + "_full"], 1)

                def cut_rest(what, i):
                    dve.wait_ge(s[what + "_p1"], i + 1)
                    if rope:
                        v.tensor_tensor(rest[what][:, :], rot[what][:, 2, :], part[what][:, SLOT[what][0], :], ALU.subtract)\
                            .then_inc(s[what + "_rest"], 1)
                    else:
                        v.scalar_tensor_tensor(rest[what][:, :], PS[:, bank_of[what], 0:S], w(f"{st}_b{what}"),
                                               part[what][:, SLOT[what][0], :], ALU.add, ALU.subtract)\
                            .then_inc(s[what + "_rest"], 1)

                def cut_third(i):
                    for what in "kq":
                        dve.wait_ge(s[what + "_p2"], i + 1)
                        v.tensor_tensor(part[what][:, SLOT[what][2], :], rest[what][:, :], part[what][:, SLOT[what][1], :],
                                        ALU.subtract)\
                            .then_inc(s[what + "_p3"], 1)

                def take_v(i, buf):
                    dve.wait_ge(s["v_psum"], i + 1)
                    for t in range(TS):
                        ins = v.tensor_tensor(vaug[:, buf, t, :, 0:DH],
                                              PS[:, FRONT + 1, t * P:(t + 1) * P].rearrange("p (h d) -> p h d", h=H),
                                              w(f"{st}_bv").rearrange("p (h d) -> p h d", h=H), ALU.add)
                    ins.then_inc(s["v_ready"], 1)

                def row_max(i, u):
                    tt, g = UNITS[u]
                    dve.wait_ge(s["s_psum"], NU * i + u + 1)
                    nk = (tt + 1) * P if causal else S
                    o = mx[:, tt, :].rearrange("p (r a) -> p r a", r=2)[:, :, 2 * g:2 * g + 2]
                    src = PS[:, S_BANK:S_BANK + 2, :].rearrange("p r (a k) -> p r a k", a=2)[:, :, :, 0:nk]
                    v.tensor_reduce(o, src, AX, ALU.max).then_inc(s["s_max"], 1)

                def cut_max(i):
                    dve.wait_ge(s["s_max"], NU * (i + 1))
                    if i > 0:
                        dve.wait_ge(s["mT_psum"], i)
                    step(v.tensor_copy(mpart[:, :, 0, :], mx[:, :, :]))
                    step(v.tensor_tensor(mrest[:, :, :], mx[:, :, :], mpart[:, :, 0, :], ALU.subtract))
                    step(v.tensor_copy(mpart[:, :, 1, :], mrest[:, :, :]))
                    v.tensor_tensor(mpart[:, :, 2, :], mrest[:, :, :], mpart[:, :, 1, :], ALU.subtract)\
                        .then_inc(s["m_parts"], 1)

                def gate(i, buf, u):
                    dve.wait_ge(s["p_ready"], NU * i + u + 1)
                    if NU * i + u >= 2:
                        dve.wait_ge(s["pv_done"], NU * i + u - 1)
                    v.tensor_tensor(PG[:, u % 2, :].rearrange("p (h q) -> p h q", h=4),
                                    Pr[:, u % 2, :].rearrange("p (h q) -> p h q", h=4),
                                    G[:, buf, UNITS[u][0], :].unsqueeze(1).broadcast_to([P, 4, S]), ALU.mult)\
                        .then_inc(s["pg_ready"], 1)

                def divide(i):
                    for t in range(TS):
                        dve.wait_ge(s["tr_psum"], TS * i + t + 1)
                        o = PS[:, FRONT + t, :].rearrange("p (h r) -> p h r", r=32)
                        step(v.reciprocal(rden[:, t, :].unsqueeze(2), o[:, :, DH:DH + 1]))
                        v.tensor_tensor(A[:, t, :].rearrange("p (h d) -> p h d", h=H), o[:, :, 0:DH],
                                        rden[:, t, :].unsqueeze(2).broadcast_to([P, H, DH]), ALU.mult)\
                            .then_inc(s["a_ready"], 1)

                def residual(p, i):
                    if bias:
                        dve.wait_ge(s["xb_ready"], TS * (i + 1))
                    dve.wait_ge(s["y_psum"], i + 1)
                    x = core.X[:, bass.ds(p * TS, TS), :]
                    v.tensor_tensor(x, PS[:, FRONT + 1, 0:S].rearrange("p (t d) -> p t d", t=TS),
                                    Xb[:, :, :] if bias else x, ALU.add).then_inc(s["x_done"], 1)

                def run_step(front, maxima, output, tail, norm=None):
                    if front:
                        p, i, buf = front
                    for u in range(NU + LEAD):
                        if maxima and u < NU:
                            row_max(maxima[1], u)
                        if front and u == 2:
                            (rotate if rope else cut_rest)("k", i)
                        if front and u == 3:
                            (rotate if rope else cut_rest)("q", i)
                        if front and u == 4:
                            take_v(i, buf)
                            if rope:
                                cut_rest("k", i)
                                cut_rest("q", i)
                        if front and u == 5:
                            cut_third(i)
                        if front and (output or not first) and u == 6:
                            if first:
                                dve.wait_ge(s["setup"], core.n_setup)
                            for par in range(2):
                                v.memset(Qm[64 * par + MAX_ROW:64 * par + MAX_ROW + NMAX, buf, par], 0.0)\
                                    .then_inc(s["zero_max"], 1)
                        if norm and u == NU - 1:
                            dve_norm_stats(core, dve, step, L, lambda t: tok(norm[0], t), norm[1], TS)
                        if maxima and u == NU - 1:
                            cut_max(maxima[1])
                        if output and gated and u >= LEAD:
                            if u == LEAD and output[1] >= 2:
                                dve.wait_ge(s["gp_in"], 16 * (output[1] - 1))
                            gate(output[1], output[2], u - LEAD)
                        if tail and u == NU - 1:
                            divide(tail[1])
                        if norm and u == NU:
                            apply_norm(*norm)
                    if tail:
                        residual(*tail)
                    if output:
                        dve.wait_ge(s["pv_done"], NU * (output[1] + 1))
                        v.tensor_copy(Osb[:, :, :].rearrange("p g q -> p (g q)"),
                                      PS[:, O_BANK:O_BANK + 2, :].rearrange("p a q -> p (a q)"))\
                            .then_inc(s["o_ready"], 1)

                def segment_end():
                    end_pass(core, dve, "go_dve")
                    step.n = 0

                stages_of(run_step, segment_end, dve.Fori, first_norm)


def experts(core, st):
    nc, s, PS, w = core.nc, core.sem, core.PS, core.w
    ly = st[:2]
    W1 = core.ffn[0][:, :].rearrange("p (e f) -> p e f", e=E)
    W2 = core.ffn[1][:, :].rearrange("p (e c d) -> p e c d", e=E, c=FC)
    two_norms = st == "L0f"
    NK = E * FC
    RING = 3

    with ExitStack() as c:
        sb = core.buffers(c)
        L = ln_buffers(core, c)
        xh = sb("xh", [P, T, D]) if two_norms else None
        xhT = sb("xhT", [P, NT]) if two_norms else L["xT"]
        he = sb("he", [P, 2, NT]) if two_norms else None
        lg, eq, sc, msk = (sb(n, [P, T, E]) for n in ("lg", "eq", "sc", "msk"))
        mx, mc, gain = (sb(n, [P, T]) for n in ("mx", "mc", "gain"))
        mT = sb("mT", [P, NT])
        mTb = sb("mTb", [P, NT], BF16)
        b2 = sb("b2", [P, P])
        hs = sb("hs", [P, RING, NT])
        hm = sb("hm", [P, RING, NT])
        YT = sb("YT", [P, NT])
        core.n_setup += 2

        with nc.Block() as block:

            @block.sync
            def _(sp):
                load_next_weights(core, sp)
                with sp.Fori(0, NPASS) as it:
                    end_pass_sync(core, sp, "experts")
                await_next_weights(core, sp)

            @block.gpsimd
            def _(pool):
                nc.gpsimd.memset(mT[:, :], 0.0).then_inc(s["setup"], 1)
                nc.gpsimd.memset(mTb[:, :], 0.0).then_inc(s["setup"], 1)
                with pool.Fori(0, NPASS) as it:
                    if two_norms:
                        pool.wait_ge(s["xhT_ready"], 1)
                        for e in range(E):
                            if e >= 2:
                                pool.wait_ge(s["z_psum"], FC * (e - 1))
                            nc.gpsimd.tensor_scalar(he[:, e % 2, :], xhT[:, :], w("L0_gamma")[:, e:e + 1],
                                                    w("L0_beta")[:, e:e + 1], ALU.mult, ALU.add)\
                                .then_inc(s["he_ready"], 1)
                    end_pass(core, pool, "go_pool")

            @block.tensor
            def _(pe):
                mm, tr = nc.tensor.matmul, nc.tensor.transpose
                free = dict(skip_group_check=True)
                pe.wait_ge(s["setup"], core.n_setup)
                pe.wait_ge(s[f"ffn_w{ly[1]}"], 32)
                with pe.Fori(0, NPASS) as it:
                    pe_turn(core, pe, L["xn"], 7, s["xn_ready"], s["xT_psum"])
                    pe.wait_ge(s["xT_ready"], 1)
                    for t in range(T):
                        ins = mm(PS[:, 6, t * E:(t + 1) * E], L["xT"][:, t * P:(t + 1) * P], w(f"{ly}_gate"),
                                 start=(t == 0), stop=True, **free)
                    ins.then_inc(s["gate_psum"], 1)
                    if two_norms:
                        pe_turn(core, pe, xh, 5, s["xh_ready"], s["xhT_psum"])
                    pe.wait_ge(s["gate_mask"], 1)
                    for t in range(T):
                        ins = tr(PS[0:E, 4, t * P:(t + 1) * P], msk[:, t, :], w("ident"))
                    ins.then_inc(s["maskT_psum"], 1)
                    pe.wait_ge(s["maskT_ready"], 2)
                    mm(PS[:, 3, :], w(f"{ly}_b2"), mT[:, :], start=True, stop=False, **free)
                    if two_norms:
                        pe.wait_ge(s["xhT_ready"], 1)

                    def second(k):
                        pe.wait_ge(s["h_ready"], k + 1)
                        ins = mm(PS[:, 3, :], W2[:, k // FC, k % FC, :], hm[:, k % RING, :],
                                 start=False, stop=(k == NK - 1), **free)
                        ins.then_inc(s["h_used"], 1)

                    for k in range(NK):
                        e, ch = k // FC, k % FC
                        if ch == 0:
                            if e >= 2:
                                pe.wait_ge(s["h_ready"], FC * (e - 1))
                            mm(PS[:, 4 + e % 2, :], core.pick[:, e * P:(e + 1) * P], mTb[:, :],
                               start=True, stop=True, **free).then_inc(s["g_psum"], 1)
                            if two_norms:
                                pe.wait_ge(s["he_ready"], e + 1)
                        if k >= RING:
                            pe.wait_ge(s["h_raw"], k - RING + 1)
                        rhs = he[:, e % 2, :] if two_norms else xhT[:, :]
                        mm(PS[:, k % RING, :], W1[:, e, ch * P:(ch + 1) * P], rhs, start=True, stop=True, **free)\
                            .then_inc(s["z_psum"], 1)
                        if k >= 2:
                            second(k - 2)
                    second(NK - 2)
                    second(NK - 1)
                    pe.wait_ge(s["yT_ready"], 1)
                    for t in range(T):
                        ins = tr(PS[:, 7, t * P:(t + 1) * P], YT[:, t * P:(t + 1) * P], w("ident"))
                    ins.then_inc(s["y_psum"], 1)
                    end_pass(core, pe, "go_pe")

            @block.scalar
            def _(act):
                a = nc.scalar.activation
                act.wait_ge(s["setup"], core.n_setup)
                with act.Fori(0, NPASS) as it:
                    step = Step(act, s["act_step"])
                    act_layernorm(core, act, step, L)
                    act_copy(core, act, L["xT"][:, :], PS[:, 7, :], s["xT_psum"], 1, s["xT_ready"])
                    if two_norms:
                        act_layernorm(core, act, step, L, n=1)
                    if st == "L1f":
                        act.wait_ge(s["gexp_in"], 1)
                        a(sc[:, :, :], eq[:, :, :], ACT.Exp).then_inc(s["gexp_out"], 1)
                    if st == "L0f":
                        act.wait_ge(s["gexp_in"], 1)
                        a(gain[:, :], mx[:, :], ACT.Exp, scale=-1.0).then_inc(s["gexp_out"], 1)
                        act_copy(core, act, xhT[:, :], PS[:, 5, :], s["xhT_psum"], 1, s["xhT_ready"])
                    act.wait_ge(s["maskT_psum"], 1)
                    a(mT[0:E, :], PS[0:E, 4, :], ACT.Copy).then_inc(s["maskT_ready"], 1)
                    a(mTb[0:E, :], PS[0:E, 4, :], ACT.Copy).then_inc(s["maskT_ready"], 1)
                    for k in range(NK):
                        act.wait_ge(s["z_psum"], k + 1)
                        if k >= RING:
                            act.wait_ge(s["h_ready"], k - RING + 1)
                        a(hs[:, k % RING, :], PS[:, k % RING, :], ACT.Relu, bias=w(f"{ly}_b1")[:, k:k + 1])\
                            .then_inc(s["h_raw"], 1)
                    act_copy(core, act, YT[:, :], PS[:, 3, :], s["h_used"], NK, s["yT_ready"])
                    end_pass(core, act, "go_act")

            @block.vector
            def _(dve):
                v = nc.vector
                bc = lambda ap: ap.unsqueeze(2).broadcast_to([P, T, E])
                bt = lambda ap: ap.unsqueeze(1).broadcast_to([P, T, E])
                with dve.Fori(0, NPASS) as it:
                    step = Step(dve, s["dve_step"])
                    dve_layernorm(core, dve, step, L, lambda t: tile_of(core, it, t), L["xn"], s["xn_ready"])
                    if two_norms:
                        dve.wait_ge(s["xn_ready"], T)
                        dve_layernorm(core, dve, step, L, lambda t: L["xn"][:, t, :], xh, s["xh_ready"], n=1)
                    dve.wait_ge(s["gate_psum"], 1)
                    logits = PS[:, 6, 0:T * E].rearrange("p (t e) -> p t e", t=T)
                    if ly == "L0":
                        step(v.tensor_copy(lg[:, :, :], logits))
                    else:
                        step(v.tensor_tensor(lg[:, :, :], logits, bt(w(f"{ly}_gate_bias")), ALU.add))
                    step(v.tensor_reduce(mx[:, :], lg[:, :, :], AX, ALU.max))
                    step(v.tensor_tensor(eq[:, :, :], lg[:, :, :], bc(mx[:, :]), ALU.is_equal))
                    step(v.tensor_tensor(sc[:, :, :], eq[:, :, :], bt(w("countdown")), ALU.mult))
                    step(v.tensor_reduce(mc[:, :], sc[:, :, :], AX, ALU.max))
                    v.tensor_tensor(msk[:, :, :], sc[:, :, :], bc(mc[:, :]), ALU.is_equal).then_inc(s["gate_mask"], 1)
                    dve.wait_ge(s["gate_mask"], 1)
                    if st == "L0f":
                        step(v.tensor_scalar(mx[:, :], mx[:, :], -80.0, None, ALU.max))
                        v.tensor_copy(mc[:, :], mx[:, :]).then_inc(s["gexp_in"], 1)
                        dve.wait_ge(s["gexp_out"], 1)
                        dve.wait_ge(s["gexp_in"], 1)
                        step(v.tensor_scalar(gain[:, :], gain[:, :], 1.0, None, ALU.add))
                        step(v.reciprocal(gain[:, :], gain[:, :]))
                    if st == "L1f":
                        v.tensor_tensor(eq[:, :, :], lg[:, :, :], bc(mx[:, :]), ALU.subtract).then_inc(s["gexp_in"], 1)
                        dve.wait_ge(s["gexp_out"], 1)
                        step(v.tensor_reduce(gain[:, :], sc[:, :, :], AX, ALU.add))
                        step(v.reciprocal(gain[:, :], gain[:, :]))
                    for k in range(NK):
                        dve.wait_ge(s["h_raw"], k + 1)
                        dve.wait_ge(s["g_psum"], k // FC + 1)
                        if k >= RING:
                            dve.wait_ge(s["h_used"], k - RING + 1)
                        v.tensor_tensor(hm[:, k % RING, :], hs[:, k % RING, :], PS[:, 4 + (k // FC) % 2, :], ALU.mult)\
                            .then_inc(s["h_ready"], 1)
                    dve.wait_ge(s["y_psum"], 1)
                    if st == "L2f":
                        dve_residual(core, dve, it, PS[:, 7, :], s["y_psum"])
                    for t in range(T):
                        y = PS[:, 7, t * P:(t + 1) * P]
                        if st == "L1f":
                            v.scalar_tensor_tensor(tile_of(core, it, t), y, gain[:, t:t + 1], tile_of(core, it, t),
                                                   ALU.mult, ALU.add)
                        if st == "L0f":
                            step.mark(v.scalar_tensor_tensor(xh[:, t, :], y, gain[:, t:t + 1], L["xn"][:, t, :],
                                                             ALU.mult, ALU.add))
                    if st == "L0f":
                        dve.wait_ge(s["dve_step"], step.n)
                        v.tensor_tensor(tokens_of(core, it), tokens_of(core, it), xh[:, :, :], ALU.add)
                    end_pass(core, dve, "go_dve")


def load_ffn(core, eng, ly):
    for n in (0, 1):
        eng.dma_start(core.ffn[n][:, :], core.dram[f"{ly}_ffn{n + 1}"]).then_inc(core.sem[f"ffn_w{ly[1]}"], 16)


def channel_attention(core):
    nc, s, PS, w = core.nc, core.sem, core.PS, core.w
    with ExitStack() as c:
        sb = core.buffers(c)
        L = ln_buffers(core, c)
        f2 = sb("f2", [P, T, D])
        et = sb("et", [P, 1])
        junk = sb("junk", [P, S])
        ss, lns, rs, us = (sb(n, [P, 2, NSEQ]) for n in ("ss", "lns", "rs", "us"))
        qk = sb("qk", [P, 2, NT])
        qkt = sb("qkt", [P, 2, NT])
        vT = sb("vT", [P, NT])
        sm, ex, en = (sb(n, [P, NSEQ, P]) for n in ("sm", "ex", "en"))
        rm, rd = sb("rm", [P, NSEQ]), sb("rd", [P, NSEQ])
        aT = sb("aT", [P, NSEQ, P])
        oT = sb("oT", [P, NT])
        TINY, UP = 1e-24, 2.0 ** 20
        with nc.Block() as block:

            @block.sync
            def _(sp):
                load_next_weights(core, sp)
                load_ffn(core, sp, "L2")
                with sp.Fori(0, NPASS) as it:
                    end_pass_sync(core, sp, "channel_attention")
                await_next_weights(core, sp)

            @block.gpsimd
            def _(pool):
                with pool.Fori(0, NPASS) as it:
                    end_pass(core, pool, "go_pool")

            @block.tensor
            def _(pe):
                mm, tr = nc.tensor.matmul, nc.tensor.transpose
                free = dict(skip_group_check=True)
                with pe.Fori(0, NPASS) as it:
                    pe_turn(core, pe, f2, 7, s["xh_ready"], s["xT_psum"])
                    pe.wait_ge(s["xT_ready"], 1)
                    for n in range(3):
                        mm(PS[:, n, :], w("L2a_qkv")[:, n * P:(n + 1) * P], L["xT"][:, :], start=True, stop=True)\
                            .then_inc(s["q_psum"], 1)
                    for n in range(2):
                        pe.wait_ge(s["a_in"], 2 * n + 2)
                        for t in range(T):
                            ins = tr(PS[:, 3 + n, t * P:(t + 1) * P], qk[:, n, t * P:(t + 1) * P], w("ident"))
                        ins.then_inc(s["a_out"], 1)
                    pe.wait_ge(s["b_in"], 2)
                    for b in range(NSEQ):
                        for tt in range(TS):
                            t = b * TS + tt
                            ins = mm(PS[:, 5, b * P:(b + 1) * P], qkt[:, 0, t * P:(t + 1) * P],
                                     qkt[:, 1, t * P:(t + 1) * P], start=(tt == 0), stop=(tt == TS - 1), **free)
                    ins.then_inc(s["b_out"], 1)
                    pe.wait_ge(s["c_in"], 1)
                    for b in range(NSEQ):
                        ins = tr(PS[:, 6, b * P:(b + 1) * P], en[:, b, :], w("ident"))
                    ins.then_inc(s["c_out"], 1)
                    pe.wait_ge(s["d_in"], 1)
                    pe.wait_ge(s["v_ready"], 1)
                    for b in range(NSEQ):
                        ins = mm(PS[:, 7, b * S:(b + 1) * S], aT[:, b, :], vT[:, b * S:(b + 1) * S],
                                 start=(b == 0), stop=True, **free)
                    ins.then_inc(s["d_out"], 1)
                    pe.wait_ge(s["e_in"], 1)
                    for t in range(T):
                        ins = mm(PS[:, 0, t * P:(t + 1) * P], oT[:, t * P:(t + 1) * P], w("L2a_out"),
                                 start=(t == 0), stop=True, **free)
                    ins.then_inc(s["y_psum"], 1)
                    end_pass(core, pe, "go_pe")

            @block.scalar
            def _(act):
                a = nc.scalar.activation
                with act.Fori(0, NPASS) as it:
                    step = Step(act, s["act_step"])
                    step(a(et[:, :], w("L2a_temp"), ACT.Exp))
                    act_layernorm(core, act, step, L)
                    act_layernorm(core, act, step, L, n=1)
                    act.wait_ge(s["xT_psum"], 1)
                    a(L["xT"][:, :], PS[:, 7, :], ACT.Copy, scale=w("L2a_norm")).then_inc(s["xT_ready"], 1)
                    for n in range(2):
                        act.wait_ge(s["q_psum"], n + 1)
                        for b in range(NSEQ):
                            step.mark(a(junk[:, :], PS[:, n, b * S:(b + 1) * S], ACT.Square,
                                        accum_out=ss[:, n, b:b + 1]))
                            act.wait_ge(s["act_step"], step.n)
                    a(junk[:, 0:1], et[:, :], ACT.Copy).then_inc(s["f_in"], 1)
                    act_copy(core, act, vT[:, :], PS[:, 2, :], s["q_psum"], 3, s["v_ready"])
                    act.wait_ge(s["f_out"], 1)
                    step(a(lns[:, :, :], us[:, :, :], ACT.Ln, scale=UP))
                    a(rs[:, :, :], lns[:, :, :], ACT.Exp, scale=-0.5).then_inc(s["f_in"], 1)
                    act_copy(core, act, qkt[:, 0, :], PS[:, 3, :], s["a_out"], 1, s["b_in"])
                    act_copy(core, act, qkt[:, 1, :], PS[:, 4, :], s["a_out"], 2, s["b_in"])
                    act.wait_ge(s["gexp_in"], 1)
                    a(ex[:, :, :], sm[:, :, :], ACT.Exp).then_inc(s["gexp_out"], 1)
                    act_copy(core, act, aT[:, :, :].rearrange("p b i -> p (b i)"), PS[:, 6, 0:NSEQ * P],
                             s["c_out"], 1, s["d_in"])
                    act_copy(core, act, oT[:, :], PS[:, 7, :], s["d_out"], 1, s["e_in"])
                    end_pass(core, act, "go_act")

            @block.vector
            def _(dve):
                v = nc.vector
                with dve.Fori(0, NPASS) as it:
                    step = Step(dve, s["dve_step"])
                    dve_layernorm(core, dve, step, L, lambda t: tile_of(core, it, t), L["xn"], s["xn_ready"])
                    dve.wait_ge(s["xn_ready"], T)
                    dve_layernorm(core, dve, step, L, lambda t: L["xn"][:, t, :], f2, s["xh_ready"], n=1,
                                  rms=True, eps=1e-6)
                    dve.wait_ge(s["f_in"], 1)
                    v.tensor_scalar(us[:, :, :], ss[:, :, :], TINY, None, ALU.max).then_inc(s["f_out"], 1)
                    dve.wait_ge(s["f_in"], 2)
                    step(v.tensor_scalar(rs[:, :, :], rs[:, :, :], UP ** 0.5, None, ALU.mult))
                    dve.wait_ge(s["f_out"], 1)
                    step(v.tensor_tensor(us[:, :, :], us[:, :, :], rs[:, :, :], ALU.mult))
                    step(v.tensor_tensor(us[:, :, :], us[:, :, :], rs[:, :, :], ALU.mult))
                    step(v.tensor_scalar(us[:, :, :], us[:, :, :], -0.5, 1.5, ALU.mult, ALU.add))
                    step(v.tensor_tensor(rs[:, :, :], rs[:, :, :], us[:, :, :], ALU.mult))
                    step(v.tensor_scalar(rs[:, 0, :], rs[:, 0, :], et[:, :], None, ALU.mult))
                    for n in range(2):
                        for b in range(NSEQ):
                            v.tensor_scalar(qk[:, n, b * S:(b + 1) * S], PS[:, n, b * S:(b + 1) * S],
                                            rs[:, n, b:b + 1], None, ALU.mult).then_inc(s["a_in"], 1)
                    dve.wait_ge(s["b_out"], 1)
                    step(v.tensor_tensor(sm[:, :, :], PS[:, 5, 0:NSEQ * P].rearrange("p (b j) -> p b j", b=NSEQ),
                                         w("block_diag").unsqueeze(1).broadcast_to([P, NSEQ, P]), ALU.add))
                    step(v.tensor_reduce(rm[:, :], sm[:, :, :], AX, ALU.max))
                    v.tensor_tensor(sm[:, :, :], sm[:, :, :], rm[:, :].unsqueeze(2).broadcast_to([P, NSEQ, P]),
                                    ALU.subtract).then_inc(s["gexp_in"], 1)
                    dve.wait_ge(s["gexp_out"], 1)
                    step(v.tensor_reduce(rd[:, :], ex[:, :, :], AX, ALU.add))
                    step(v.reciprocal(rd[:, :], rd[:, :]))
                    v.tensor_tensor(en[:, :, :], ex[:, :, :], rd[:, :].unsqueeze(2).broadcast_to([P, NSEQ, P]),
                                    ALU.mult).then_inc(s["c_in"], 1)
                    dve_residual(core, dve, it, PS[:, 0, :], s["y_psum"])
                    end_pass(core, dve, "go_dve")


def retention(core):
    nc, s, PS, w = core.nc, core.sem, core.PS, core.w
    with ExitStack() as c:
        sb = core.buffers(c)
        L = ln_buffers(core, c)
        kvT = sb("kvT", [P, NT])
        t1, t2, rot = (sb(n, [P, 2, NT]) for n in ("t1", "t2", "rot"))
        V = sb("V", [P, T, D])
        D0 = sb("D0", [P, NSEQ, S])
        D1 = sb("D1", [P, NSEQ, P])
        with nc.Block() as block:

            @block.sync
            def _(sp):
                load_next_weights(core, sp)
                with sp.Fori(0, NPASS) as it:
                    end_pass_sync(core, sp, "retention")
                await_next_weights(core, sp)

            @block.gpsimd
            def _(pool):
                with pool.Fori(0, NPASS) as it:
                    nc.gpsimd.tensor_copy(kvT[:, :], core.ctxT[:, bass.ds(it * NT, NT)]).then_inc(s["kv_ready"], 1)
                    end_pass(core, pool, "go_pool")

            @block.tensor
            def _(pe):
                mm = nc.tensor.matmul
                free = dict(skip_group_check=True)
                with pe.Fori(0, NPASS) as it:
                    pe.wait_ge(s["kv_ready"], 1)
                    mm(PS[:, 2, :], w("L2x_k"), kvT[:, :], start=True, stop=True)
                    mm(PS[:, 3, :], w("L2x_ks"), kvT[:, :], start=True, stop=True).then_inc(s["k_psum"], 1)
                    for t in range(T):
                        ins = mm(PS[:, 4, t * P:(t + 1) * P], kvT[:, t * P:(t + 1) * P], w("L2x_v"),
                                 start=(t == 0), stop=True, **free)
                    ins.then_inc(s["v_psum"], 1)
                    pe_turn(core, pe, L["xn"], 7, s["xn_ready"], s["xT_psum"])
                    pe.wait_ge(s["xT_ready"], 1)
                    mm(PS[:, 0, :], w("L2x_q"), L["xT"][:, :], start=True, stop=True)
                    mm(PS[:, 1, :], w("L2x_qs"), L["xT"][:, :], start=True, stop=True).then_inc(s["q_psum"], 1)
                    pe.wait_ge(s["a_in"], 2)
                    for b in range(NSEQ):
                        q0 = b * S
                        mm(PS[:, 5, q0:q0 + S], rot[:, 1, q0:q0 + P], rot[:, 0, q0:q0 + S],
                           start=(b == 0), stop=True, **free)
                        ins = mm(PS[:, 6, b * P:(b + 1) * P], rot[:, 1, q0 + P:q0 + S], rot[:, 0, q0 + P:q0 + S],
                                 start=(b == 0), stop=True, **free)
                    ins.then_inc(s["a_out"], 1)
                    pe.wait_ge(s["b_in"], 2)
                    pe.wait_ge(s["v_ready"], 1)
                    for b in range(NSEQ):
                        for tt in range(TS):
                            t = b * TS + tt
                            o = PS[:, 7, t * P:(t + 1) * P]
                            ins = mm(o, D0[:, b, tt * P:(tt + 1) * P], V[:, b * TS, :], start=(t == 0),
                                     stop=(tt == 0), **free)
                            if tt == 1:
                                ins = mm(o, D1[:, b, :], V[:, b * TS + 1, :], start=False, stop=True, **free)
                    ins.then_inc(s["y_psum"], 1)
                    end_pass(core, pe, "go_pe")

            @block.scalar
            def _(act):
                with act.Fori(0, NPASS) as it:
                    step = Step(act, s["act_step"])
                    act_copy(core, act, V[:, :, :].rearrange("p t d -> p (t d)"), PS[:, 4, :], s["v_psum"], 1, s["v_ready"])
                    act_layernorm(core, act, step, L)
                    act_copy(core, act, L["xT"][:, :], PS[:, 7, :], s["xT_psum"], 1, s["xT_ready"])
                    end_pass(core, act, "go_act")

            @block.vector
            def _(dve):
                v = nc.vector
                two = lambda ap: ap.rearrange("p (b t) -> p b t", b=NSEQ)
                tab = lambda n: w(n).unsqueeze(1).broadcast_to([P, NSEQ, S])
                with dve.Fori(0, NPASS) as it:
                    step = Step(dve, s["dve_step"])
                    dve_layernorm(core, dve, step, L, lambda t: tile_of(core, it, t), L["xn"], s["xn_ready"])
                    for n, what in ((1, "k"), (0, "q")):
                        dve.wait_ge(s[what + "_psum"], 1)
                        step.mark(v.tensor_tensor(two(t1[:, n, :]), two(PS[:, 2 * n, :]), tab(f"x{what}_cos"), ALU.mult))
                        step(v.tensor_tensor(two(t2[:, n, :]), two(PS[:, 2 * n + 1, :]), tab(f"x{what}_sin"), ALU.mult))
                        v.tensor_tensor(rot[:, n, :], t1[:, n, :], t2[:, n, :], ALU.add).then_inc(s["a_in"], 1)
                    dve.wait_ge(s["a_out"], 1)
                    v.tensor_tensor(D0[:, :, :], two(PS[:, 5, :]), tab("decay0"), ALU.mult).then_inc(s["b_in"], 1)
                    v.tensor_tensor(D1[:, :, :], PS[:, 6, 0:NSEQ * P].rearrange("p (b t) -> p b t", b=NSEQ),
                                    w("decay0")[:, 0:P].unsqueeze(1).broadcast_to([P, NSEQ, P]), ALU.mult)\
                        .then_inc(s["b_in"], 1)
                    dve_residual(core, dve, it, PS[:, 7, :], s["y_psum"])
                    end_pass(core, dve, "go_dve")


def state_space(core):
    nc, s, PS, w = core.nc, core.sem, core.PS, core.w
    NH = 2
    PAD = TAPS - 1
    QW = S + P
    with ExitStack() as c:
        sb = core.buffers(c)
        L = ln_buffers(core, c)
        xTp = sb("xTp", [P, NSEQ, PAD + S])
        Wx = sb("Wx", [P, TAPS, NH * P])
        Wbc = sb("Wbc", [P, 2, TAPS, 64])
        xs = sb("xs", [P, NH, NT])
        BC = sb("BC", [64, 2, NT])
        zs = sb("zs", [P, NH, NT])
        Xt = sb("Xt", [P, NH, T, P])
        An = sb("An", [P, NH])
        dt, nv, av, u, w1, dd, ez, q1, dA = (sb(n, [P, T, NH]) for n in
                                             ("dt", "nv", "av", "u", "w1", "dd", "ez", "q1", "dA"))
        dAb = sb("dAb", [P, T, NH, P])
        cs = sb("cs", [P, T, NH])
        Ld = sb("Ld", [P, NSEQ, NH, QW])
        Lx = sb("Lx", [P, NSEQ, NH, QW])
        Gm0, Gm1 = sb("Gm0", [P, NSEQ, S]), sb("Gm1", [P, NSEQ, P])
        Wk = sb("Wk", [P, NSEQ, NH, QW])
        y2 = sb("y2", [P, NH, NT])
        y3 = sb("y3", [P, NH, NT])
        tri2 = core.W[:, COLS["tri"][0]:COLS["tri"][0] + S]
        core.n_setup += 4
        with nc.Block() as block:

            @block.sync
            def _(sp):
                load_next_weights(core, sp)
                with sp.Fori(0, NPASS) as it:
                    end_pass_sync(core, sp, "state_space")
                await_next_weights(core, sp)

            @block.gpsimd
            def _(pool):
                g = nc.gpsimd
                g.memset(xTp[:, :, 0:PAD], 0.0).then_inc(s["setup"], 1)
                g.tensor_tensor(Wx[:, :, :], w("L3a_xs").unsqueeze(1).broadcast_to([P, TAPS, NH * P]),
                                w("L3a_taps_xs").rearrange("p (k c) -> p k c", k=TAPS), ALU.mult).then_inc(s["setup"], 1)
                for n, name in enumerate("bc"):
                    g.tensor_tensor(Wbc[:, n], w(f"L3a_{name}").unsqueeze(1).broadcast_to([P, TAPS, 64]),
                                    w(f"L3a_taps_{name}").rearrange("p (k c) -> p k c", k=TAPS), ALU.mult)\
                        .then_inc(s["setup"], 1)
                with pool.Fori(0, NPASS) as it:
                    pool.wait_ge(s["b_in"], 1)
                    g.tensor_copy(dAb[:, :, :, :], dA[:, :, :].unsqueeze(3).broadcast_to([P, T, NH, P]))\
                        .then_inc(s["b_out"], 1)
                    end_pass(core, pool, "go_pool")

            @block.tensor
            def _(pe):
                mm, tr = nc.tensor.matmul, nc.tensor.transpose
                free = dict(skip_group_check=True)
                pe.wait_ge(s["setup"], core.n_setup)
                with pe.Fori(0, NPASS) as it:
                    pe_turn(core, pe, L["xn"], 7, s["xn_ready"], s["xT_psum"])
                    pe.wait_ge(s["xT_ready"], 1)
                    for t in range(T):
                        q0 = PAD + (t % TS) * P
                        ins = mm(PS[:, 6, t * NH:(t + 1) * NH], xTp[:, t // TS, q0:q0 + P], w("L3a_dt"),
                                 start=(t == 0), stop=True, **free)
                    ins.then_inc(s["a_out"], 1)
                    for n in range(2):
                        for k in range(TAPS):
                            ins = mm(PS[0:64, 2 + n, :].rearrange("p (b t) -> p b t", b=NSEQ), Wbc[:, n, k, :],
                                     xTp[:, :, k:k + S], start=(k == 0), stop=(k == PAD))
                        ins.then_inc(s["z_psum"], 1)
                    for n in range(NH):
                        for k in range(TAPS):
                            ins = mm(PS[:, n, :].rearrange("p (b t) -> p b t", b=NSEQ), Wx[:, k, n * P:(n + 1) * P],
                                     xTp[:, :, k:k + S], start=(k == 0), stop=(k == PAD))
                        ins.then_inc(s["z_psum"], 1)
                    for n in range(NH):
                        mm(PS[:, 4 + n, :].rearrange("p (b t) -> p b t", b=NSEQ), w("L3a_z")[:, n * P:(n + 1) * P],
                           xTp[:, :, PAD:PAD + S], start=True, stop=True).then_inc(s["z_psum"], 1)
                    pe.wait_ge(s["b_in"], 1)
                    for t in range(T):
                        o = PS[:, 6, 64 + t * NH:64 + (t + 1) * NH]
                        ins = mm(o, w("tri"), dA[:, t, :], start=(t == 0), stop=True, **free)
                        if t % TS:
                            ins = mm(o, w("ones"), dA[:, t - 1, :], start=False, stop=True, **free)
                    ins.then_inc(s["c_out"], 1)
                    pe.wait_ge(s["b_out"], 1)
                    pe.wait_ge(s["h_raw"], 6)
                    for b in range(NSEQ):
                        bank = (7, 0)[b]
                        for h in range(NH):
                            mm(PS[:, bank, h * S:(h + 1) * S], dAb[:, b * TS, h, :], tri2, start=(h == 0), stop=True, **free)
                            ins = mm(PS[:, bank, h * S + P:(h + 1) * S], dAb[:, b * TS + 1, h, :], w("tri"),
                                     start=False, stop=True, **free)
                        ins.then_inc(s["d_out"], 1)
                    for b in range(NSEQ):
                        q0 = b * S
                        mm(PS[:, 2, q0:q0 + S], BC[:, 0, q0:q0 + P], BC[:, 1, q0:q0 + S], start=(b == 0), stop=True, **free)
                        ins = mm(PS[:, 3, b * P:(b + 1) * P], BC[:, 0, q0 + P:q0 + S], BC[:, 1, q0 + P:q0 + S],
                                 start=(b == 0), stop=True, **free)
                    ins.then_inc(s["e_out"], 1)
                    for h in range(NH):
                        for t in range(T):
                            ins = tr(PS[:, 4 + h, t * P:(t + 1) * P], xs[:, h, t * P:(t + 1) * P], w("ident"))
                        ins.then_inc(s["tr_psum"], 1)
                    pe.wait_ge(s["h_ready"], 2 * NSEQ * NH)
                    pe.wait_ge(s["v_ready"], NH)
                    for h in range(NH):
                        for b in range(NSEQ):
                            mm(PS[:, 1 - h, b * S:(b + 1) * S], Xt[:, h, b * TS, :], Wk[:, b, h, 0:S],
                               start=(b == 0), stop=True, **free)
                            ins = mm(PS[:, 1 - h, b * S + P:(b + 1) * S], Xt[:, h, b * TS + 1, :], Wk[:, b, h, S:QW],
                                     start=False, stop=True, **free)
                        ins.then_inc(s["f_out"], 1)
                    pe.wait_ge(s["f_in"], NH)
                    for t in range(T):
                        for h in range(NH):
                            ins = mm(PS[:, 2, t * P:(t + 1) * P], y3[:, h, t * P:(t + 1) * P],
                                     w("L3a_out")[:, h * P:(h + 1) * P], start=(t == 0 and h == 0), stop=True, **free)
                    ins.then_inc(s["y_psum"], 1)
                    end_pass(core, pe, "go_pe")

            @block.scalar
            def _(act):
                a = nc.scalar.activation
                act.wait_ge(s["setup"], core.n_setup)
                with act.Fori(0, NPASS) as it:
                    step = Step(act, s["act_step"])
                    a(An[:, :], w("L3a_alog"), ACT.Exp).then_inc(s["a_in"], 1)
                    act_layernorm(core, act, step, L)
                    act.wait_ge(s["xT_psum"], 1)
                    a(xTp[:, :, PAD:PAD + S], PS[:, 7, :].rearrange("p (b t) -> p b t", b=NSEQ), ACT.Copy)\
                        .then_inc(s["xT_ready"], 1)
                    act.wait_ge(s["gexp_in"], 1)
                    a(u[:, :, :], av[:, :, :], ACT.Exp, scale=-1.0).then_inc(s["gexp_out"], 1)
                    act.wait_ge(s["gexp_in"], 2)
                    a(q1[:, :, :], w1[:, :, :], ACT.Ln).then_inc(s["gexp_out"], 1)
                    for n in range(2):
                        act.wait_ge(s["z_psum"], n + 1)
                        a(BC[:, n, :], PS[0:64, 2 + n, :], ACT.Silu, bias=w(f"L3a_bias_{'bc'[n]}", 64))\
                            .then_inc(s["h_raw"], 1)
                    for n in range(NH):
                        act.wait_ge(s["z_psum"], 3 + n)
                        a(xs[:, n, :], PS[:, n, :], ACT.Silu, bias=w("L3a_bias_xs")[:, n:n + 1]).then_inc(s["h_raw"], 1)
                    for n in range(NH):
                        act.wait_ge(s["z_psum"], 5 + n)
                        a(zs[:, n, :], PS[:, 4 + n, :], ACT.Silu).then_inc(s["h_raw"], 1)
                    for b in range(NSEQ):
                        act.wait_ge(s["c_in"], b + 1)
                        a(Lx[:, b], Ld[:, b], ACT.Exp).then_inc(s["d_in"], 1)
                    for h in range(NH):
                        act_copy(core, act, Xt[:, h].rearrange("p t c -> p (t c)"), PS[:, 4 + h, :], s["tr_psum"], h + 1,
                                 s["v_ready"])
                    end_pass(core, act, "go_act")

            @block.vector
            def _(dve):
                v = nc.vector
                with dve.Fori(0, NPASS) as it:
                    step = Step(dve, s["dve_step"])
                    dve_layernorm(core, dve, step, L, lambda t: tile_of(core, it, t), L["xn"], s["xn_ready"])
                    dve.wait_ge(s["a_out"], 1)
                    step(v.tensor_tensor(dt[:, :, :], PS[:, 6, 0:T * NH].rearrange("p (t h) -> p t h", t=T),
                                         w("L3a_dtb").unsqueeze(1).broadcast_to([P, T, NH]), ALU.add))
                    step(v.tensor_scalar(nv[:, :, :], dt[:, :, :], -1.0, None, ALU.mult))
                    v.tensor_tensor(av[:, :, :], dt[:, :, :], nv[:, :, :], ALU.max).then_inc(s["gexp_in"], 1)
                    dve.wait_ge(s["gexp_out"], 1)
                    v.tensor_scalar(w1[:, :, :], u[:, :, :], 1.0, None, ALU.add).then_inc(s["gexp_in"], 1)
                    dve.wait_ge(s["gexp_in"], 2)
                    step(v.tensor_scalar(dd[:, :, :], w1[:, :, :], 1.0, None, ALU.subtract))
                    step(v.tensor_scalar(ez[:, :, :], dd[:, :, :], 0.0, None, ALU.is_equal))
                    step(v.tensor_tensor(dd[:, :, :], dd[:, :, :], ez[:, :, :], ALU.add))
                    step(v.reciprocal(dd[:, :, :], dd[:, :, :]))
                    dve.wait_ge(s["gexp_out"], 2)
                    step(v.tensor_tensor(dd[:, :, :], dd[:, :, :], q1[:, :, :], ALU.mult))
                    step(v.tensor_tensor(dd[:, :, :], dd[:, :, :], ez[:, :, :], ALU.add))
                    step(v.tensor_tensor(dd[:, :, :], dd[:, :, :], u[:, :, :], ALU.mult))
                    step(v.tensor_scalar(dt[:, :, :], dt[:, :, :], 0.0, None, ALU.max))
                    step(v.tensor_tensor(dt[:, :, :], dt[:, :, :], dd[:, :, :], ALU.add))
                    dve.wait_ge(s["a_in"], 1)
                    step(v.tensor_tensor(dd[:, :, :], dt[:, :, :], An[:, :].unsqueeze(1).broadcast_to([P, T, NH]), ALU.mult))
                    v.tensor_scalar(dA[:, :, :], dd[:, :, :], -1.0, None, ALU.mult).then_inc(s["b_in"], 1)
                    dve.wait_ge(s["c_out"], 1)
                    step(v.tensor_copy(cs[:, :, :], PS[:, 6, 64:64 + T * NH].rearrange("p (t h) -> p t h", t=T)))
                    for b in range(NSEQ):
                        dve.wait_ge(s["d_out"], b + 1)
                        bank = (7, 0)[b]
                        for h in range(NH):
                            v.tensor_scalar(Ld[:, b, h, 0:S], PS[:, bank, h * S:(h + 1) * S], cs[:, b * TS, h:h + 1], 0.0,
                                            ALU.subtract, ALU.min)
                            ins = v.tensor_scalar(Ld[:, b, h, S:QW], PS[:, bank, h * S + P:(h + 1) * S],
                                                  cs[:, b * TS + 1, h:h + 1], 0.0, ALU.subtract, ALU.min)
                        ins.then_inc(s["c_in"], 1)
                    dve.wait_ge(s["e_out"], 1)
                    step.mark(v.tensor_tensor(Gm0[:, :, :], PS[:, 2, :].rearrange("p (b t) -> p b t", b=NSEQ),
                                              tri2.unsqueeze(1).broadcast_to([P, NSEQ, S]), ALU.mult))
                    step(v.tensor_tensor(Gm1[:, :, :], PS[:, 3, 0:NSEQ * P].rearrange("p (b t) -> p b t", b=NSEQ),
                                         w("tri").unsqueeze(1).broadcast_to([P, NSEQ, P]), ALU.mult))
                    for b in range(NSEQ):
                        dve.wait_ge(s["d_in"], b + 1)
                        for h in range(NH):
                            v.scalar_tensor_tensor(Wk[:, b, h, 0:S], Lx[:, b, h, 0:S], dt[:, b * TS, h:h + 1],
                                                   Gm0[:, b, :], ALU.mult, ALU.mult).then_inc(s["h_ready"], 1)
                            v.scalar_tensor_tensor(Wk[:, b, h, S:QW], Lx[:, b, h, S:QW], dt[:, b * TS + 1, h:h + 1],
                                                   Gm1[:, b, :], ALU.mult, ALU.mult).then_inc(s["h_ready"], 1)
                    for h in range(NH):
                        dve.wait_ge(s["f_out"], h + 1)
                        step(v.scalar_tensor_tensor(y2[:, h, :], xs[:, h, :], w("L3a_skip")[:, h:h + 1], PS[:, 1 - h, :],
                                                    ALU.mult, ALU.add))
                        v.tensor_tensor(y3[:, h, :], y2[:, h, :], zs[:, h, :], ALU.mult).then_inc(s["f_in"], 1)
                    dve_residual(core, dve, it, PS[:, 2, :], s["y_psum"])
                    end_pass(core, dve, "go_dve")


def latent_experts(core):
    nc, s, PS, w = core.nc, core.sem, core.PS, core.w
    NR = 4
    NK = NR + 4
    RING = 3
    with ExitStack() as c:
        sb = core.buffers(c)
        L = ln_buffers(core, c)
        sg, sf, oh, eq, sc, wt, o2 = (sb(n, [P, T, E]) for n in ("sg", "sf", "oh", "eq", "sc", "wt", "o2"))
        pairs = sb("pairs", [P, T, 2, 6])
        gs, keep = sb("gs", [P, T, 2]), sb("keep", [P, T, 2])
        mx, mc = sb("mx", [P, T]), sb("mc", [P, T])
        wT = sb("wT", [P, NT])
        lat = sb("lat", [P, NT])
        comb = sb("comb", [P, NT])
        hs, hm, ht = (sb(n, [P, RING, NT]) for n in ("hs", "hm", "ht"))
        YT = sb("YT", [P, NT])
        core.n_setup += 1
        with nc.Block() as block:

            @block.sync
            def _(sp):
                load_next_weights(core, sp)
                with sp.Fori(0, NPASS) as it:
                    end_pass_sync(core, sp, "latent_experts")
                await_next_weights(core, sp)

            @block.gpsimd
            def _(pool):
                nc.gpsimd.memset(wT[:, :], 0.0).then_inc(s["setup"], 1)
                with pool.Fori(0, NPASS) as it:
                    end_pass(core, pool, "go_pool")

            @block.tensor
            def _(pe):
                mm, tr = nc.tensor.matmul, nc.tensor.transpose
                free = dict(skip_group_check=True)
                pe.wait_ge(s["setup"], core.n_setup)
                with pe.Fori(0, NPASS) as it:
                    pe_turn(core, pe, L["xn"], 7, s["xn_ready"], s["xT_psum"])
                    pe.wait_ge(s["xT_ready"], 1)
                    for t in range(T):
                        ins = mm(PS[:, 6, t * E:(t + 1) * E], L["xT"][:, t * P:(t + 1) * P], w("L3f_gate"),
                                 start=(t == 0), stop=True, **free)
                    ins.then_inc(s["gate_psum"], 1)
                    mm(PS[:, 4, :], w("L3f_fc1"), L["xT"][:, :], start=True, stop=True, **free).then_inc(s["a_out"], 1)

                    def second(i):
                        k = ORDER[i]
                        pe.wait_ge(s["h_ready"], i + 1)
                        if k >= NR:
                            ins = mm(PS[:, 7, :], w("L3f_down")[:, (k - NR) * P:(k - NR + 1) * P], hm[:, i % RING, :],
                                     start=(k == NR), stop=False, **free)
                        else:
                            ins = mm(PS[:, 3, :], w("L3f_w2")[:, k * P:(k + 1) * P], hm[:, i % RING, :],
                                     start=(k == 0), stop=(k == NR - 1), **free)
                        ins.then_inc(s["h_used"], 1)

                    for i, k in enumerate(ORDER):
                        if i >= RING:
                            pe.wait_ge(s["h_raw"], i - RING + 1)
                        if k < NR:
                            if k == 0:
                                pe.wait_ge(s["gate_mask"], 1)
                                for t in range(T):
                                    ins = tr(PS[0:E, 6, t * P:(t + 1) * P], wt[:, t, :], w("ident"))
                                ins.then_inc(s["maskT_psum"], 1)
                                pe.wait_ge(s["maskT_ready"], 1)
                                pe.wait_ge(s["a_in"], 1)
                            if k >= 2:
                                pe.wait_ge(s["h_ready"], i - 1)
                            mm(PS[:, 4 + k % 2, :], w("pick_pairs")[:, k * P:(k + 1) * P], wT[:, :], start=True, stop=True, **free)\
                                .then_inc(s["g_psum"], 1)
                            mm(PS[:, i % RING, :], w("L3f_w1")[:, k * P:(k + 1) * P], lat[:, :],
                               start=True, stop=True, **free).then_inc(s["z_psum"], 1)
                        else:
                            mm(PS[:, i % RING, :], w("L3f_up")[:, (k - NR) * P:(k - NR + 1) * P], L["xT"][:, :],
                               start=True, stop=True, **free).then_inc(s["z_psum"], 1)
                        if i >= 2:
                            second(i - 2)
                    second(NK - 2)
                    second(NK - 1)
                    pe.wait_ge(s["b_in"], 1)
                    mm(PS[:, 7, :], w("L3f_fc2"), comb[:, :], start=False, stop=True, **free).then_inc(s["b_out"], 1)
                    pe.wait_ge(s["yT_ready"], 1)
                    for t in range(T):
                        ins = tr(PS[:, 0, t * P:(t + 1) * P], YT[:, t * P:(t + 1) * P], w("ident"))
                    ins.then_inc(s["y_psum"], 1)
                    end_pass(core, pe, "go_pe")

            @block.scalar
            def _(act):
                a = nc.scalar.activation
                act.wait_ge(s["setup"], core.n_setup)
                with act.Fori(0, NPASS) as it:
                    step = Step(act, s["act_step"])
                    act_layernorm(core, act, step, L)
                    act_copy(core, act, L["xT"][:, :], PS[:, 7, :], s["xT_psum"], 1, s["xT_ready"])
                    act_copy(core, act, lat[:, :], PS[:, 4, :], s["a_out"], 1, s["a_in"])
                    act.wait_ge(s["gexp_in"], 1)
                    a(sg[:, :, :], sf[:, :, :], ACT.Exp, scale=-1.0).then_inc(s["gexp_out"], 1)
                    for i, k in enumerate(ORDER):
                        if k == 0:
                            act.wait_ge(s["maskT_psum"], 1)
                            a(wT[0:E, :], PS[0:E, 6, :], ACT.Copy).then_inc(s["maskT_ready"], 1)
                        act.wait_ge(s["z_psum"], i + 1)
                        if i >= RING:
                            act.wait_ge(s["h_ready"], i - RING + 1)
                        a(hs[:, i % RING, :], PS[:, i % RING, :], ACT.Relu).then_inc(s["h_raw"], 1)
                    act_copy(core, act, comb[:, :], PS[:, 3, :], s["h_used"], NK, s["b_in"])
                    act_copy(core, act, YT[:, :], PS[:, 7, :], s["b_out"], 1, s["yT_ready"])
                    end_pass(core, act, "go_act")

            @block.vector
            def _(dve):
                v = nc.vector
                bc = lambda ap: ap.unsqueeze(2).broadcast_to([P, T, E])
                bt = lambda ap: ap.unsqueeze(1).broadcast_to([P, T, E])

                def hidden(dve, i):
                    k = ORDER[i]
                    dve.wait_ge(s["h_raw"], i + 1)
                    if i >= RING:
                        dve.wait_ge(s["h_used"], i - RING + 1)
                    if k < NR:
                        dve.wait_ge(s["g_psum"], k + 1)
                        v.tensor_tensor(ht[:, i % RING, :], hs[:, i % RING, :], PS[:, 4 + k % 2, :], ALU.mult)\
                            .then_inc(s["c_in"], 1)
                        dve.wait_ge(s["c_in"], k + 1)
                    other = ht if k < NR else hs
                    v.tensor_tensor(hm[:, i % RING, :], hs[:, i % RING, :], other[:, i % RING, :], ALU.mult)\
                        .then_inc(s["h_ready"], 1)

                with dve.Fori(0, NPASS) as it:
                    step = Step(dve, s["dve_step"])

                    def first_largest(values, out):
                        step(v.tensor_reduce(mx[:, :], values, AX, ALU.max))
                        step(v.tensor_tensor(eq[:, :, :], values, bc(mx[:, :]), ALU.is_equal))
                        step(v.tensor_tensor(sc[:, :, :], eq[:, :, :], bt(w("countdown")), ALU.mult))
                        step(v.tensor_reduce(mc[:, :], sc[:, :, :], AX, ALU.max))
                        step(v.tensor_tensor(out, sc[:, :, :], bc(mc[:, :]), ALU.is_equal))

                    dve_layernorm(core, dve, step, L, lambda t: tile_of(core, it, t), L["xn"], s["xn_ready"])
                    dve.wait_ge(s["gate_psum"], 1)
                    v.tensor_scalar(sf[:, :, :], PS[:, 6, 0:T * E].rearrange("p (t e) -> p t e", t=T), -80.0, None, ALU.max)\
                        .then_inc(s["gexp_in"], 1)
                    dve.wait_ge(s["gexp_out"], 1)
                    step(v.tensor_scalar(sg[:, :, :], sg[:, :, :], 1.0, None, ALU.add))
                    step(v.reciprocal(sg[:, :, :], sg[:, :, :]))
                    step(v.tensor_tensor(sf[:, :, :], sg[:, :, :], bt(w("L3f_corr")), ALU.add))
                    sv = sf[:, :, :].rearrange("p t (g e) -> p t g e", g=2)
                    for at, gap in ((0, 1), (3, 2), (5, 3)):
                        step.mark(v.tensor_tensor(pairs[:, :, :, at:at + 4 - gap], sv[:, :, :, 0:4 - gap],
                                                  sv[:, :, :, gap:4], ALU.add))
                    dve.wait_ge(s["dve_step"], step.n)
                    step(v.tensor_reduce(gs[:, :, :], pairs[:, :, :, :], AX, ALU.max))
                    step.mark(v.tensor_tensor(keep[:, :, 0:1], gs[:, :, 0:1], gs[:, :, 1:2], ALU.is_ge))
                    step(v.tensor_tensor(keep[:, :, 1:2], gs[:, :, 0:1], gs[:, :, 1:2], ALU.is_lt))
                    step(v.tensor_tensor(sv, sv, keep[:, :, :].unsqueeze(3).broadcast_to([P, T, 2, 4]), ALU.mult))
                    first_largest(sf[:, :, :], oh[:, :, :])
                    step(v.tensor_scalar(o2[:, :, :], oh[:, :, :], -BIG, None, ALU.mult))
                    step(v.tensor_tensor(sf[:, :, :], sf[:, :, :], o2[:, :, :], ALU.add))
                    first_largest(sf[:, :, :], o2[:, :, :])
                    step(v.tensor_tensor(oh[:, :, :], oh[:, :, :], o2[:, :, :], ALU.add))
                    step(v.tensor_tensor(oh[:, :, :], oh[:, :, :], sg[:, :, :], ALU.mult))
                    step(v.tensor_reduce(mx[:, :], oh[:, :, :], AX, ALU.add))
                    step(v.tensor_scalar(mx[:, :], mx[:, :], 1e-20, None, ALU.add))
                    step(v.reciprocal(mx[:, :], mx[:, :]))
                    v.tensor_tensor(wt[:, :, :], oh[:, :, :], bc(mx[:, :]), ALU.mult).then_inc(s["gate_mask"], 1)
                    for i in range(NK):
                        hidden(dve, i)
                    dve_residual(core, dve, it, PS[:, 0, :], s["y_psum"])
                    end_pass(core, dve, "go_dve")


ORDER = (4, 5, 6, 7, 0, 1, 2, 3)


def start(core):
    nc, s, PS, w = core.nc, core.sem, core.PS, core.w
    with ExitStack() as c:
        ctx_tok = c.enter_context(nc.sbuf_tensor("ctx_tok_", [P, B * TS, D], F32))
        pick = c.enter_context(nc.sbuf_tensor("pick32", [P, E * P], F32))
        with nc.Block() as block:

            @block.sync
            def _(sp):
                sp.dma_start(core.W[:, :], core.dram["small_common"]).then_inc(s["w_in"], 16)
                sp.dma_start(pick[:, :], core.dram["pick_rows"]).then_inc(s["w_in"], 16)
                sp.dma_start(core.stage_W[0][:, 0:width(WEIGHTS[STAGES[0]])], core.dram[f"small_{STAGES[0]}"])\
                    .then_inc(s["stage_w"], 16)
                sp.dma_start(ctx_tok[:, :, :], core.dram["ctx"].rearrange("(t p) d -> p t d", p=P)).then_inc(s["ctx_tok"], 16)
                sp.dma_start(core.X[:, :, :], core.dram["x"].rearrange("(t p) d -> p t d", p=P)).then_inc(s["x_in"], 16)
                sp.wait_ge(s["x_in"], 16)
                sp.wait_ge(s["stage_w"], 16)
                load_ffn(core, sp, "L0")

            @block.tensor
            def _(pe):
                pe.wait_ge(s["w_in"], 32)
                pe.wait_ge(s["ctx_tok"], 16)
                for k in range(4):
                    for t in range(4):
                        ins = nc.tensor.transpose(PS[:, k, t * P:(t + 1) * P], ctx_tok[:, 4 * k + t, :], w("ident"))
                    ins.then_inc(s["ctx_psum"], 1)

            @block.scalar
            def _(act):
                nc.scalar.preload_act_table_set("natural_log_exp_and_others")
                act.wait_ge(s["w_in"], 32)
                for k in range(4):
                    act_copy(core, act, core.ctxT[:, k * 512:(k + 1) * 512], PS[:, k, :], s["ctx_psum"], k + 1, s["ctx_done"])

            @block.vector
            def _(dve):
                v = nc.vector
                dve.wait_ge(s["w_in"], 32)
                v.tensor_copy(core.ident_b[:, :], w("ident"))
                v.tensor_copy(core.neg_q[:, :], w("neg_q"))
                v.tensor_copy(core.neg_k[:, :], w("neg_k"))
                v.tensor_copy(core.pick[:, :], pick[:, :]).then_inc(s["ctx_done"], 1)
                dve.wait_ge(s["ctx_done"], 5)


def finish(core):
    nc, s = core.nc, core.sem
    with nc.Block() as block:

        @block.sync
        def _(sp):
            sp.dma_start(core.dram["out"].rearrange("(t p) d -> p t d", p=P), core.X[:, :, :]).then_inc(s["out_done"], 16)
            sp.wait_ge(s["out_done"], 16)


def program(nc, dram):
    with ExitStack() as ctx:
        core = Core(nc, ctx, dram)
        start(core)
        for core.at, st in enumerate(STAGES):
            if st in ATTN:
                attention(core, st)
            elif st in ("L0f", "L1f", "L2f"):
                experts(core, st)
            else:
                {"L2a": channel_attention, "L2x": retention, "L3a": state_space, "L3f": latent_experts}[st](core)
        finish(core)


def tables():
    f = np.float32
    t = {"ident": np.eye(P, dtype=f), "ones": np.ones((P, P), f)}
    r, c = np.arange(P)[:, None], np.arange(P)[None, :]
    t["tri"] = (r <= c).astype(f)
    t["neg_q"] = np.where(c > r, f(-BIG), f(0))
    t["neg_k"] = np.where(r > c, f(-BIG), f(0))
    t["block_diag"] = np.where(r // 16 == c // 16, f(0), f(-BIG))
    t["pick"] = np.zeros((P, E, P), f)
    t["pick"][np.arange(E), np.arange(E), :] = 1
    t["pick"] = t["pick"].reshape(P, E * P)
    t["pick_pairs"] = np.zeros((P, E, 64), f)
    t["pick_pairs"][np.arange(E), np.arange(E), :] = 1
    t["pick_pairs"] = t["pick_pairs"].reshape(P, E * 64)
    t["countdown"] = np.tile(np.arange(E, 0, -1, dtype=f), (P, 1))
    d = np.arange(P) % 64 // DH
    inv = f(1) / np.power(f(10000), np.arange(0, DH, 2, dtype=f) / f(DH))
    ang = (np.arange(S, dtype=f)[None, :] * inv[d // 2][:, None]).astype(f)
    t["rope_cos"] = np.cos(ang).astype(f)
    t["rope_sin"] = np.where(d[:, None] % 2 == 0, -np.sin(ang), np.sin(ang)).astype(f)
    ch = np.arange(P)
    half = D // 2
    sv = (np.arange(0, D, 2, dtype=f) + f(0.4 * D)) / f(1.4 * D)
    pos = np.arange(S, dtype=f)
    scale = np.power(sv[None, :], (pos / f(512))[:, None]).astype(f)
    freqs = f(1) / np.power(f(10000), np.arange(half, dtype=f) / f(half))
    ang = (pos[:, None] * freqs[None, :]).astype(f)
    for q, sc in (("q", scale), ("k", f(1) / scale)):
        co = (np.cos(ang) * sc).astype(f)[:, ch // 2].T
        si = (np.sin(ang) * sc).astype(f)[:, ch // 2].T
        t[f"x{q}_cos"] = co
        t[f"x{q}_sin"] = np.where(ch[:, None] % 2 == 0, -si, si)
    diff = np.arange(S, dtype=f)[None, :] - np.arange(P, dtype=f)[:, None]
    t["decay0"] = np.where(diff >= 0, np.power(f(0.96875), np.maximum(diff, 0)), f(0)).astype(f)
    return t


def lay_out(i):
    f = np.float32
    a = {k: np.asarray(v) for k, v in i.items()}
    col = dict(tables())

    def stack_order(wt, swap=False):
        x = wt.reshape(wt.shape[:-1] + (H // 2, 2, DH // 2, 2))
        if swap:
            x = x[..., ::-1]
        n = x.ndim
        x = x.transpose(tuple(range(n - 4)) + (n - 3, n - 2, n - 1, n - 4))
        return x.reshape(wt.shape)

    spread = lambda x: np.broadcast_to(x.reshape(1, -1), (P, x.size))
    rows = lambda x: np.concatenate([x, np.zeros((P - x.shape[0],) + x.shape[1:], f)], axis=0)
    wide = lambda x: np.concatenate([x, np.zeros(x.shape[:-1] + (P - x.shape[-1],), f)], axis=-1)
    zero = np.zeros(P, f)
    att = {
        "L0a": (a["L0_attn_Wq"].T, a["L0_attn_bq"], a["L0_attn_Wk"].T, a["L0_attn_bk"], a["L0_attn_Wv"].T,
                a["L0_attn_bv"], a["L0_attn_Wo"].T, a["L0_attn_bo"]),
        "L0x": (a["L0_xattn_wq_k"], a["L0_xattn_wq_b"], a["L0_xattn_wk_k"], a["L0_xattn_wk_b"], a["L0_xattn_wv_k"],
                a["L0_xattn_wv_b"], a["L0_xattn_wo_k"], a["L0_xattn_wo_b"]),
        "L1a": (a["L1_attn_W_q"].T, zero, a["L1_attn_W_k"].T, zero, a["L1_attn_W_v"].T, zero, a["L1_attn_W_o"].T, zero),
        "L1x": (a["L1_xattn_WQ"], a["L1_xattn_bQ"], a["L1_xattn_WK"], a["L1_xattn_bK"], a["L1_xattn_WV"],
                a["L1_xattn_bV"], a["L1_xattn_WO"], a["L1_xattn_bO"]),
        "L3x": (a["L3_xattn_Wq"].T, a["L3_xattn_bq"], a["L3_xattn_Wk"].T, a["L3_xattn_bk"], a["L3_xattn_Wv"].T,
                a["L3_xattn_bv"], a["L3_xattn_Wo"].T, a["L3_xattn_bo"]),
    }
    for st, (wq, bq, wk, bk, wv, bv, wo, bo) in att.items():
        for n, wt, b in (("q", wq, bq), ("k", wk, bk)):
            col[f"{st}_w{n}"], col[f"{st}_w{n}s"] = stack_order(wt), stack_order(wt, True)
            col[f"{st}_b{n}"], col[f"{st}_b{n}s"] = stack_order(b)[:, None], stack_order(b, True)[:, None]
        col[f"{st}_wv"], col[f"{st}_wo"] = wv, wo
        col[f"{st}_bv"], col[f"{st}_bo"] = spread(bv), spread(bo)
    chunked = lambda b: b.reshape(E, FC, P).transpose(2, 0, 1).reshape(P, E * FC)
    col["L0_gate"], col["L0_b1"], col["L0_b2"] = a["L0_ffn_centroids"].T, chunked(a["L0_ffn_b1"]), rows(a["L0_ffn_b2"])
    col["L0_gamma"], col["L0_beta"] = a["L0_ffn_gamma"].T, a["L0_ffn_beta"].T
    col["L1_gate"], col["L1_gate_bias"] = a["L1_ffn_w_gate"], spread(a["L1_ffn_b_gate"])
    col["L1_b1"], col["L1_b2"] = chunked(a["L1_ffn_b1"]), rows(a["L1_ffn_b2"])
    col["L2_gate"], col["L2_gate_bias"] = a["L2_ffn_Wr"].T, spread(a["L2_ffn_br"])
    col["L2_b1"], col["L2_b2"] = chunked(a["L2_ffn_b1"]), rows(a["L2_ffn_b2"])
    col["L2a_qkv"], col["L2a_out"] = a["L2_attn_w_qkv"].T, a["L2_attn_w_out"].T
    col["L2a_norm"] = a["L2_attn_norm_weight"][:, None]
    col["L2a_temp"] = np.repeat(a["L2_attn_temperature"].reshape(-1), 16)[:, None]
    swap = lambda x: x.reshape(D, D // 2, 2)[:, :, ::-1].reshape(D, D)
    for n in "qkv":
        col[f"L2x_{n}"] = a[f"L2_xattn_W{n}"]
        if n != "v":
            col[f"L2x_{n}s"] = swap(a[f"L2_xattn_W{n}"])
    win = a["L3_attn_W_in"].T
    taps = a["L3_attn_conv_w"][:, 0, :].T
    cb = a["L3_attn_conv_b"]
    col["L3a_z"], col["L3a_xs"], col["L3a_b"], col["L3a_c"], col["L3a_dt"] = (
        win[:, 0:256], win[:, 256:512], win[:, 512:576], win[:, 576:640], win[:, 640:642])
    col["L3a_taps_xs"], col["L3a_taps_b"], col["L3a_taps_c"] = (
        spread(taps[:, 0:256]), spread(taps[:, 256:320]), spread(taps[:, 320:384]))
    col["L3a_bias_xs"] = cb[0:256].reshape(2, P).T
    col["L3a_bias_b"], col["L3a_bias_c"] = rows(cb[256:320, None]), rows(cb[320:384, None])
    col["L3a_alog"], col["L3a_dtb"], col["L3a_skip"] = (
        spread(a["L3_attn_A_log"]), spread(a["L3_attn_dt_bias"]), spread(a["L3_attn_D_skip"]))
    col["L3a_out"] = a["L3_attn_W_out"].T.reshape(2, P, D).transpose(1, 0, 2).reshape(P, 2 * D)
    col["L3f_gate"], col["L3f_corr"] = a["L3_ffn_gate"].T, spread(a["L3_ffn_corr_bias"])
    col["L3f_fc1"] = wide(a["L3_ffn_fc1_w"].T)
    col["L3f_w1"] = rows(a["L3_ffn_w1"].transpose(2, 0, 1).reshape(64, E * 64))
    col["L3f_w2"] = wide(a["L3_ffn_w2"].transpose(0, 2, 1).reshape(4, P, 64)).transpose(1, 0, 2).reshape(P, 4 * P)
    col["L3f_fc2"] = rows(a["L3_ffn_fc2_w"].T)
    col["L3f_up"] = a["L3_ffn_up_w"].T
    col["L3f_down"] = a["L3_ffn_down_w"].T.reshape(4, P, D).transpose(1, 0, 2).reshape(P, 4 * D)
    packs = {f"small_{st}": np.concatenate([col[n] for n, _ in pairs], axis=1).astype(f, copy=False)
             for st, pairs in {"common": COMMON, **WEIGHTS}.items()}

    first = lambda x: np.ascontiguousarray(x.transpose(1, 0, 2).reshape(P, E * F))
    second = lambda x: np.ascontiguousarray(x.reshape(E, FC, P, D).transpose(2, 0, 1, 3).reshape(P, E * F))
    return {
        **packs, "pick_rows": col["pick"],
        "x": a["x"].reshape(B * S, D), "ctx": a["ctx_1024"].reshape(B * S, D),
        "mask0q": a["mask_BxSxS2_ik1"], "mask0k": np.ascontiguousarray(a["mask_BxSxS2_ik1"].transpose(0, 2, 1)),
        "mask1q": np.ascontiguousarray(a["mask_Bx1xSxS2_ik1"][:, 0]),
        "mask1k": np.ascontiguousarray(a["mask_Bx1xSxS2_ik1"][:, 0].transpose(0, 2, 1)),
        "gate_prob": np.ascontiguousarray(a["fside_BxSxS2_0"].transpose(0, 2, 1)),
        "L0_ffn1": first(a["L0_ffn_w1"]), "L0_ffn2": second(a["L0_ffn_w2"]),
        "L1_ffn1": first(a["L1_ffn_W1"]), "L1_ffn2": second(a["L1_ffn_W2"]),
        "L2_ffn1": first(a["L2_ffn_W1"].transpose(0, 2, 1)), "L2_ffn2": second(a["L2_ffn_W2"].transpose(0, 2, 1)),
    }


def kernel(**inputs):
    import concourse.bacc as bacc
    from concourse.bass_utils import run_bass_kernel_spmd

    nc = bacc.Bacc("TRN2", target_bir_lowering=False, num_devices=1)
    arrays = lay_out(inputs)
    dram = {n: nc.dram_tensor(n, a.shape, mybir.dt.from_np(a.dtype), kind="ExternalInput").ap()
            for n, a in arrays.items()}
    dram["out"] = nc.dram_tensor("out", (B * S, D), F32, kind="ExternalOutput").ap()
    for n in "qk":
        dram[f"{n}_bounce"] = nc.dram_tensor(f"{n}_bounce", (3, 2, 3, P // 2, S), BF16, kind="Internal").ap()
    dram["m_bounce"] = nc.dram_tensor("m_bounce", (NMAX * H, S), BF16, kind="Internal").ap()
    program(nc, dram)
    r = run_bass_kernel_spmd(nc, [arrays], core_ids=[0])
    return r.results[0]["out"].reshape(B, S, D)
```

```python
from contextlib import ExitStack

import concourse.bass as bass
import numpy as np
from concourse import mybir

F32 = mybir.dt.float32
BF16 = mybir.dt.bfloat16
I32 = mybir.dt.int32
ALU = mybir.AluOpType
ACT = mybir.ActivationFunctionType
ENGINE = mybir.EngineType
AX = mybir.AxisListType.X

P = 128
B, S, D = 8, 256, 128
NSEQ = 2
NPASS = B // NSEQ
NT = NSEQ * S
T = NT // P
TS = S // P
ALL_TILES = B * TS
H, DH = 16, 8
HP = H // 2
DEPTH = 3
E, F = 8, 512
FC = F // P
BLOCKS = 24
TAPS = 4
EPS = 1e-5
BIG = 2.0 ** 100

SLOT = {"q": (0, 1, 2), "k": (1, 2, 0)}
MAX_ROW = 32
PAIR_ROW = 40
NMAX = 3


ATTN = ("L0a", "L0x", "L1a", "L1x", "L3x")
STAGES = ("L0a", "L0x", "L0f", "L1a", "L1x", "L1f", "L2a", "L2x", "L2f", "L3a", "L3x", "L3f")

COMMON = [("ident", P), ("neg_q", P), ("neg_k", P), ("rope_cos", S), ("rope_sin", S), ("tri", P), ("ones", P),
          ("countdown", E), ("numbers", BLOCKS)]
WEIGHTS = {st: [(f"{st}_{n}", k) for n, k in (
    ("wq", P), ("wqs", P), ("wk", P), ("wks", P), ("wv", P), ("wo", P),
    ("bq", 1), ("bqs", 1), ("bk", 1), ("bks", 1), ("bv", P), ("bo", P))] for st in ATTN}
WEIGHTS["L0f"] = [("L0_gate", E), ("L0_b1", E * FC), ("L0_b2", E * P), ("L0_gamma", E), ("L0_beta", E)]
WEIGHTS["L1f"] = [("L1_gate", E), ("L1_gate_bias", E), ("L1_b1", E * FC), ("L1_b2", E * P)]
WEIGHTS["L2f"] = [("L2_gate", E), ("L2_gate_bias", E), ("L2_b1", E * FC), ("L2_b2", E * P)]
WEIGHTS["L2a"] = [("L2a_qkv", 3 * P), ("L2a_out", P), ("L2a_norm", 1), ("L2a_temp", 1), ("block_diag", P)]
WEIGHTS["L2x"] = [("L2x_q", P), ("L2x_qs", P), ("L2x_k", P), ("L2x_ks", P), ("L2x_v", P),
                  ("xq_cos", S), ("xq_sin", S), ("xk_cos", S), ("xk_sin", S), ("decay0", S)]
WEIGHTS["L3a"] = [("L3a_z", 2 * P), ("L3a_xs", 2 * P), ("L3a_b", 64), ("L3a_c", 64), ("L3a_dt", 2),
                  ("L3a_taps_xs", TAPS * 2 * P), ("L3a_taps_b", TAPS * 64), ("L3a_taps_c", TAPS * 64),
                  ("L3a_bias_xs", 2), ("L3a_bias_b", 1), ("L3a_bias_c", 1), ("L3a_alog", 2), ("L3a_dtb", 2),
                  ("L3a_skip", 2), ("L3a_out", 2 * P)]
WEIGHTS["L3f"] = [("L3f_gate", E), ("L3f_corr", E), ("L3f_fc1", P), ("L3f_w1", E * 64), ("L3f_w2", 4 * P),
                  ("L3f_fc2", P), ("L3f_up", 4 * P), ("L3f_down", 4 * P), ("pick_pairs", 4 * P)]


def ranges(pairs):
    out, at = {}, 0
    for name, n in pairs:
        out[name] = (at, at + n)
        at += n
    return out


COLS = {}
for _pairs in (COMMON, *WEIGHTS.values()):
    COLS.update(ranges(_pairs))
width = lambda pairs: sum(n for _, n in pairs)
STAGE_COLS = max(width(pairs) for pairs in WEIGHTS.values())

KEEP = """x_in w_in stage_w ffn_w0 ffn_w1 ffn_w2 ctx_tok ctx_psum ctx_done rows_zero setup out_done
go_pe go_act go_dve go_pool q_stack0 q_stack1 q_stack2 k_stack0 k_stack1 k_stack2 m_stack scattered xsT_ready y_out""".split()
KEEP += [f"gathered{t}" for t in range(B * TS)]
ALL_STAGES = "iter_done dve_step act_step pool_step ln_mv ln_r0 xn_ready xT_psum xT_ready y_psum".split()
PASS_SEMS = {
    "attention": """kv_ready q_psum k_psum v_psum v_ready q_p1 q_rest q_p2 q_p3 q_full k_p1 k_rest k_p2 k_p3 k_full
        zero_max x_done q_bounce k_bounce m_bounce mask_in mask_ready gp_in s_psum s_max m_parts mT_psum mT_ready
        st_psum p_ready pg_ready pv_done o_ready tr_psum a_ready aT_psum aT_ready xb_ready""".split(),
    "experts": """xh_ready gate_psum gate_mask gexp_in gexp_out pads cum_psum cum_used pos_ready plan_ready
        xsT_psum xb_ready z_psum h_raw hT_psum h_ready y_ready""".split()
        + [f"sorted_in{k}" for k in range(BLOCKS // 4)],
    "channel_attention": """xh_ready q_psum v_ready gexp_in gexp_out a_in a_out b_in b_out c_in c_out d_in d_out
        e_in f_in f_out""".split(),
    "retention": "q_psum k_psum v_psum v_ready a_in a_out b_in".split(),
    "state_space": """v_ready tr_psum gexp_in gexp_out z_psum h_raw h_ready a_in a_out b_in b_out c_in c_out
        d_in d_out e_out f_in f_out""".split(),
    "latent_experts": """gate_psum gate_mask maskT_psum maskT_ready gexp_in gexp_out z_psum h_raw g_psum h_ready
        h_used yT_ready a_in a_out b_in b_out c_in""".split(),
}
SEMS = list(dict.fromkeys(KEEP + ALL_STAGES + sum(PASS_SEMS.values(), [])))


class Step:

    def __init__(self, eng, sem):
        self.eng, self.sem, self.n = eng, sem, 0

    def mark(self, ins):
        self.n += 1
        return ins.then_inc(self.sem, 1)

    def __call__(self, ins):
        self.mark(ins)
        self.eng.wait_ge(self.sem, self.n)


class Core:

    def __init__(self, nc, ctx, dram):
        self.nc, self.dram = nc, dram
        self.sem = {n: ctx.enter_context(nc.semaphore(n)) for n in SEMS}
        sb = lambda name, shape, dt=F32: ctx.enter_context(nc.sbuf_tensor(name, shape, dt))
        self.X = sb("X", [P, B * TS, D])
        self.ctxT = sb("ctxT", [P, B * S])
        self.W = sb("W", [P, width(COMMON)])
        self.stage_W = [sb(f"stage_W{k}", [P, STAGE_COLS]) for k in range(2)]
        self.at = 0
        self.ffn = [sb(f"ffn_w{n}_", [P, E * F]) for n in (1, 2)]
        self.ident_b = sb("ident_b", [P, P], BF16)
        self.neg_q = sb("neg_q", [P, P], BF16)
        self.neg_k = sb("neg_k", [P, P], BF16)
        self.Qm = sb("Qm", [P, DEPTH, 2, HP, S], BF16)
        self.Kst = sb("Kst", [P, DEPTH, HP, S], BF16)
        self.vaug = sb("vaug", [P, DEPTH, TS, H, 32])
        self.n_experts = 0
        self.n_setup = 0
        self.PS = ctx.enter_context(nc.psum_tensor("PS", [P, 8, 512], F32))

    def buffers(self, stack):
        st = STAGES[self.at]
        return lambda name, shape, dt=F32: stack.enter_context(self.nc.sbuf_tensor(f"{st}_{name}", shape, dt))

    def w(self, name, rows=P):
        a, b = COLS[name]
        src = self.W if name in dict(COMMON) else self.stage_W[self.at % 2]
        return src[0:rows, a:b]


def load_next_weights(core, sp):
    if core.at + 1 < len(STAGES):
        st = STAGES[core.at + 1]
        sp.dma_start(core.stage_W[(core.at + 1) % 2][:, 0:width(WEIGHTS[st])], core.dram[f"small_{st}"])\
            .then_inc(core.sem["stage_w"], 16)


def await_next_weights(core, sp):
    if core.at + 1 < len(STAGES):
        sp.wait_ge(core.sem["stage_w"], 16 * (core.at + 2))


def end_pass(core, eng, go):
    eng.drain().then_inc(core.sem["iter_done"], 1)
    eng.wait_ge(core.sem[go], 1)
    eng.sem_clear(core.sem[go])


def end_pass_sync(core, sp, kind):
    sp.wait_ge(core.sem["iter_done"], 4)
    for name in ALL_STAGES + PASS_SEMS[kind]:
        sp.sem_clear(core.sem[name])
    for go in ("go_pe", "go_act", "go_dve", "go_pool"):
        sp.sem_inc(core.sem[go], 1)


def ln_buffers(core, c, tiles=T, turned=True):
    sb = core.buffers(c)
    return dict(st=sb("ln_st", [P, tiles, 6]), mv=sb("ln_mv_", [P, 2, tiles, 2]), lnv=sb("ln_lnv", [P, 2, tiles]),
                r0=sb("ln_r0_", [P, 2, tiles]), sq=sb("ln_sq", [P, 2, tiles]), w=sb("ln_w", [P, 2, tiles]),
                r=sb("ln_r", [P, 2, tiles]), xn=sb("xn", [P, tiles, D]),
                xT=sb("xT", [P, tiles * P]) if turned else None)


def tokens_of(core, it):
    return core.X[:, bass.ds(it * T, T), :]


def dve_norm_stats(core, dve, step, L, src, n, tiles, slot=0, rms=False, eps=EPS):
    v, s = core.nc.vector, core.sem
    mv, u = L["mv"][:, slot], L["sq"][:, slot]
    for t in range(tiles):
        step.mark(v.bn_stats(L["st"][:, t, :], src(t)))
    dve.wait_ge(s["dve_step"], step.n)
    for t in range(tiles):
        step.mark(v.bn_aggr(mv[:, t, :], L["st"][:, t, :]))
    dve.wait_ge(s["dve_step"], step.n)
    if rms:
        step(v.tensor_tensor(u, mv[:, :, 0], mv[:, :, 0], ALU.mult))
        step(v.tensor_tensor(mv[:, :, 1], mv[:, :, 1], u, ALU.add))
    v.tensor_scalar(L["w"][:, slot], mv[:, :, 1], eps, None, ALU.add).then_inc(s["ln_mv"], 1)


def dve_norm_apply(core, dve, step, L, src, dst, ready, n, tiles, slot=0, rms=False):
    v, s = core.nc.vector, core.sem
    mv, u = L["mv"][:, slot], L["sq"][:, slot]
    dve.wait_ge(s["ln_mv"], n + 1)
    dve.wait_ge(s["ln_r0"], n + 1)
    step(v.tensor_tensor(u, L["r0"][:, slot], L["r0"][:, slot], ALU.mult))
    step(v.tensor_tensor(u, u, L["w"][:, slot], ALU.mult))
    step(v.tensor_scalar(u, u, -0.5, 1.5, ALU.mult, ALU.add))
    step(v.tensor_tensor(L["r"][:, slot], L["r0"][:, slot], u, ALU.mult))
    for t in range(tiles):
        r = L["r"][:, slot, t:t + 1]
        ops = (r, None, ALU.mult) if rms else (mv[:, t, 0:1], r, ALU.subtract, ALU.mult)
        v.tensor_scalar(dst[:, t, :], src(t), *ops).then_inc(ready, 1)


def dve_layernorm(core, dve, step, L, src, dst, ready, n=0, rms=False, eps=EPS, tiles=T):
    dve_norm_stats(core, dve, step, L, src, n, tiles, n, rms, eps)
    dve_norm_apply(core, dve, step, L, src, dst, ready, n, tiles, n, rms)


def act_layernorm(core, act, step, L, n=0, slot=None):
    a, s = core.nc.scalar, core.sem
    slot = n if slot is None else slot
    act.wait_ge(s["ln_mv"], n + 1)
    step(a.activation(L["lnv"][:, slot], L["w"][:, slot], ACT.Ln))
    a.activation(L["r0"][:, slot], L["lnv"][:, slot], ACT.Exp, scale=-0.5).then_inc(s["ln_r0"], 1)


def pe_turn_all(core, pe, src, ready):
    s = core.sem
    for g in range(ALL_TILES // 4):
        for t in range(4 * g, 4 * g + 4):
            pe.wait_ge(s[ready], t + 1)
            ins = core.nc.tensor.transpose(core.PS[:, g, (t % 4) * P:(t % 4 + 1) * P], src[:, t, :], core.w("ident"))
        ins.then_inc(s["xT_psum"], 1)


def act_copy(core, act, out, src, wait, n, done):
    act.wait_ge(wait, n)
    core.nc.scalar.activation(out, src, ACT.Copy).then_inc(done, 1)


def dve_residual(core, dve, it, add, wait, base=None):
    dve.wait_ge(wait, 1)
    x = tokens_of(core, it)
    core.nc.vector.tensor_tensor(x, add.rearrange("p (t d) -> p t d", t=T), x if base is None else base, ALU.add)


def attention(core, st):
    nc, s, PS, w = core.nc, core.sem, core.PS, core.w
    rope = st in ("L0a", "L1a")
    causal = rope
    masked = st in ("L0x", "L1x")
    gated = st == "L0x"
    cross = not rope
    bias = st != "L1a"
    SCALE = float(1.0 / np.sqrt(np.float32(DH)))
    NG = H // 4
    UNITS = [(t, g) for t in range(TS) for g in range(NG)]
    NU = len(UNITS)
    LEAD = 2
    S_BANK, T_BANK, O_BANK, FRONT = 0, 2, 4, 6

    with ExitStack() as c:
        sb = core.buffers(c)
        L = ln_buffers(core, c, TS)
        Qm, Kst, vaug = core.Qm, core.Kst, core.vaug
        Pr = sb("Pr", [P, 2, 4 * S])
        Osb = sb("Osb", [P, NG, S])
        part = {n: sb(f"{n}part", [P, 3, S], BF16) for n in "qk"}
        rest = {n: sb(f"{n}rest", [P, S]) for n in "qk"}
        rot = {n: sb(f"{n}rot", [P, 3, S]) for n in "qk"} if rope else None
        mx = sb("mx", [P, TS, H])
        mrest = sb("mrest", [P, TS, H])
        mpart = sb("mpart", [P, TS, NMAX, H], BF16)
        mT = sb("mT", [NMAX * H, S], BF16)
        rden = sb("rden", [P, TS, H])
        A, AT = sb("A", [P, TS, D]), sb("AT", [P, S])
        Xb = sb("Xb", [P, TS, D]) if bias else None
        kvT = sb("kvT", [P, S]) if cross else L["xT"]
        if masked:
            msk = sb("msk", [P, 2, TS, S], I32)
            neg = sb("neg", [P, DEPTH, 2, TS, S], BF16)
        if gated:
            G = sb("G", [P, DEPTH, TS, S])
            PG = sb("PG", [P, 2, 4 * S])
            den = sb("den", [P, 32])
        first = core.at == 0
        set_ready = core.n_setup
        core.n_setup += (7 if first else 0) + (2 if gated else 1)
        bank_of = {"k": FRONT + 1, "q": FRONT}

        def s_bank(u, alone):
            return T_BANK if u == 1 or alone and u % 2 else S_BANK

        def t_bank(v, alone):
            return S_BANK if alone and v % 2 else T_BANK

        def stages_of(run_step, segment_end, loop, first_norm=lambda p: None):
            first_norm(0)
            run_step((0, 0, 0), None, None, None, norm=(1, 1))
            run_step((1, 1, 1), None, None, None)
            run_step(None, (0, 0, 0), None, None)
            segment_end()
            with loop(0, (B - 2) // DEPTH) as it:
                first_norm(it * DEPTH + 2)
                for k in range(DEPTH):
                    p = it * DEPTH + k
                    run_step((p + 2, k, (k + 2) % DEPTH), (p + 1, k, (k + 1) % DEPTH), (p, k, k),
                             (p - 1, k - 1) if k > 0 else None,
                             norm=(p + 3, k + 1) if k + 1 < DEPTH else None)
                run_step(None, None, None, (it * DEPTH + DEPTH - 1, DEPTH - 1))
                segment_end()
            run_step(None, (B - 1, 0, (B - 1) % DEPTH), (B - 2, 0, (B - 2) % DEPTH), None)
            run_step(None, None, (B - 1, 1, (B - 1) % DEPTH), (B - 2, 0))
            run_step(None, None, None, (B - 1, 1))
            segment_end()

        tok = lambda p, t: core.X[:, bass.ds(p * TS + t, 1), :].rearrange("p a d -> p (a d)")

        with nc.Block() as block:

            @block.sync
            def _(sp):
                load_next_weights(core, sp)
                if st == "L1a":
                    load_ffn(core, sp, "L1")
                name = "mask0" if st == "L0x" else "mask1"

                def run_step(front, maxima, output, tail, norm=None):
                    if front and masked:
                        p, i, buf = front
                        if i > 0:
                            sp.wait_ge(s["mask_ready"], 2 * i)
                        for k in range(2):
                            sp.dma_start(msk[:, k, :, :], core.dram[name + "qk"[k]][bass.ds(p, 1)]
                                         .rearrange("b (t p) k -> p (b t) k", p=P)).then_inc(s["mask_in"], 16)
                    if front and gated:
                        if output and i > 0:
                            sp.wait_ge(s["pg_ready"], NU * i)
                        sp.dma_start(G[:, buf], core.dram["gate_prob"][bass.ds(p, 1)]
                                     .rearrange("b (t p) k -> p (b t) k", p=P)).then_inc(s["gp_in"], 16)
                    if front:
                        p, i, buf = front
                        for what in "kq":
                            sp.wait_ge(s[what + "_p2"], i + 1)
                            sp.wait_ge(s[what + "_p3"], i + 1)
                            for par in range(2):
                                sp.dma_start(core.dram[what + "_bounce"][buf, par].rearrange("c r t -> r c t"),
                                             part[what][64 * par:64 * par + 64]).then_inc(s[what + "_bounce"], 16)
                        if output and i > 0:
                            sp.wait_ge(s["st_psum"], NU * i)
                        if first:
                            sp.wait_ge(s["setup"], core.n_setup if output else set_ready + 2 * (i + 1))
                        for what in "kq":
                            sp.wait_ge(s[what + "_bounce"], 32 * (i + 1))
                            for par in range(2):
                                slots = core.dram[what + "_bounce"][buf, par].rearrange("c (d p) t -> (c d) (p t)", p=HP)
                                stack = Kst[:, buf] if what == "k" else Qm[:, buf, par]
                                twice = lambda rows, n: rows.unsqueeze(0).broadcast_to([2, n, HP * S])
                                if what == "k":
                                    runs = ((0, 4, twice(slots[DH:3 * DH], 2 * DH)), (PAIR_ROW, 2, slots[0:2 * DH]))
                                else:
                                    pair = slots.rearrange("(c d) x -> c d x", d=DH)[0:3:2]
                                    runs = ((0, 2, twice(slots[0:DH], DH)), (2 * DH, 2, twice(slots[DH:2 * DH], DH)),
                                            (PAIR_ROW, 2, pair))
                                for row, blocks, src in runs:
                                    sp.dma_start(stack[64 * par + row:64 * par + row + blocks * DH], src)\
                                        .then_inc(s[f"{what}_stack{buf}"], 16)
                    if maxima:
                        p, i, buf = maxima
                        sp.wait_ge(s["mT_ready"], i + 1)
                        sp.dma_start(core.dram["m_bounce"], mT[:, :]).then_inc(s["m_bounce"], 16)
                        sp.wait_ge(s["m_bounce"], 16 * (i + 1))
                        for par in range(2):
                            sp.dma_start(Qm[64 * par + MAX_ROW:64 * par + MAX_ROW + NMAX, buf, par],
                                         core.dram["m_bounce"].rearrange("(c r p) t -> r c p t", c=NMAX, r=2)[par])\
                                .then_inc(s["m_stack"], 16)

                stages_of(run_step, lambda: end_pass_sync(core, sp, "attention"), sp.Fori)
                await_next_weights(core, sp)

            @block.gpsimd
            def _(pool):
                g = nc.gpsimd
                def set_up(k):
                    g.memset(Kst[:, k], -1.0).then_inc(s["setup"], 1)
                    g.memset(Qm[:, k], 0.0).then_inc(s["setup"], 1)

                def run_step(front, maxima, output, tail, norm=None):
                    if front:
                        p, i, buf = front
                        if cross:
                            if i > 0:
                                pool.wait_ge(s["v_psum"], i)
                            g.tensor_copy(kvT[:, :], core.ctxT[:, bass.ds(p * S, S)]).then_inc(s["kv_ready"], 1)
                        if masked:
                            pool.wait_ge(s["mask_in"], 32 * (i + 1))
                            if output and i > 0:
                                pool.wait_ge(s["st_psum"], NU * i)
                            for k in range(2):
                                if st == "L1x":
                                    ops = (0.0, -BIG, ALU.is_equal, ALU.mult)
                                else:
                                    ops = (2.0 ** 31, -2.0 ** 31, ALU.mult, ALU.add)
                                g.tensor_scalar(neg[:, buf, k], msk[:, k], *ops).then_inc(s["mask_ready"], 1)
                    if tail and bias:
                        p, i = tail
                        if i > 0:
                            pool.wait_ge(s["x_done"], i)
                        for t in range(TS):
                            g.tensor_tensor(Xb[:, t, :], tok(p, t), w(f"{st}_bo"), ALU.add).then_inc(s["xb_ready"], 1)

                    if first and front and not output:
                        set_up(front[2])
                    if maxima and not output:
                        if first:
                            set_up(DEPTH - 1)
                            g.memset(vaug[:, :, :, :, DH + 1:32], 0.0).then_inc(s["setup"], 1)
                        g.memset(vaug[:, :, :, :, DH:DH + 1], 0.0 if gated else 1.0).then_inc(s["setup"], 1)
                        if gated:
                            g.tensor_scalar(den[:, :], w("ones")[:, 0:32], 0.0, None, ALU.mult)\
                                .then_inc(s["pool_step"], 1)
                            pool.wait_ge(s["pool_step"], 1)
                            g.memset(den[:, DH:DH + 1], 1.0).then_inc(s["setup"], 1)

                stages_of(run_step, lambda: end_pass(core, pool, "go_pool"), pool.Fori)

            @block.tensor
            def _(pe):
                mm, tr = nc.tensor.matmul, nc.tensor.transpose
                free = dict(skip_group_check=True)

                def turn_norm(i):
                    for t in range(TS):
                        pe.wait_ge(s["xn_ready"], TS * i + t + 1)
                        ins = tr(PS[:, FRONT, t * P:(t + 1) * P], L["xn"][:, t, :], w("ident"))
                    ins.then_inc(s["xT_psum"], 1)

                def project(i):
                    if cross:
                        pe.wait_ge(s["kv_ready"], i + 1)
                    pe.wait_ge(s["xT_ready"], i + 1)
                    for what, src in (("k", kvT), ("q", L["xT"])):
                        if rope:
                            mm(PS[:, bank_of[what], S:2 * S], w(f"{st}_w{what}s"), src[:, :], start=True, stop=True, **free)
                        mm(PS[:, bank_of[what], 0:S], w(f"{st}_w{what}"), src[:, :], start=not rope, stop=True, **free)\
                            .then_inc(s[what + "_psum"], 1)

                def project_v(i):
                    pe.wait_ge(s["k_full" if rope else "k_rest"], i + 1)
                    for t in range(TS):
                        ins = mm(PS[:, FRONT + 1, t * P:(t + 1) * P], kvT[:, t * P:(t + 1) * P], w(f"{st}_wv"),
                                 start=(t == 0), stop=True, **free)
                    ins.then_inc(s["v_psum"], 1)

                def scores(i, buf, u, front_here, alone, outputs):
                    tt, g = UNITS[u]
                    if u == 0:
                        for what, dmas in ((f"k_stack{buf}", 4), (f"q_stack{buf}", 6)):
                            pe.wait_ge(s[what], 16 * dmas)
                            pe.sem_clear(s[what])
                    if u == 0 and i > 0:
                        pe.wait_ge(s["mT_ready"], i)
                    if u == 0 and front_here:
                        if i > 0 or not first:
                            pe.wait_ge(s["zero_max"], 2 * max(i, 1))
                        if masked:
                            pe.wait_ge(s["mask_ready"], 2 * max(i, 1))
                    if u == 1 and outputs:
                        pe.wait_ge(s["p_ready"], NU * outputs)
                    if u >= 2:
                        pe.wait_ge(s["s_max"], NU * i + (u if u >= 3 and not alone else u - 1))
                    bank = s_bank(u, alone)
                    nk = (tt + 1) * P if causal else S
                    for pp in range(2):
                        for par in range(2):
                            ins = mm(PS[:, bank + par, pp * S:pp * S + nk],
                                     Qm[:, buf, par, 2 * g + pp, tt * P:(tt + 1) * P], Kst[:, buf, 2 * g + pp, 0:nk],
                                     start=(pp == 0), stop=True, **free)
                    for par in range(2):
                        o = PS[:, bank + par, :].rearrange("p (a k) -> p a k", a=2)
                        if causal:
                            ins = mm(o[:, :, tt * P:tt * P + P], core.ident_b[:, :],
                                     core.neg_q[:, :].unsqueeze(1).broadcast_to([P, 2, P]), start=False, stop=True, **free)
                        if masked:
                            ins = mm(o, core.ident_b[:, :], neg[:, buf, 0, tt].unsqueeze(1).broadcast_to([P, 2, S]),
                                     start=False, stop=True, **free)
                    ins.then_inc(s["s_psum"], 1)

                def turn_max(i):
                    pe.wait_ge(s["m_parts"], i + 1)
                    for tt in range(TS):
                        ins = tr(PS[0:NMAX * H, S_BANK, tt * 64:tt * 64 + 64].bitcast(BF16),
                                 mpart[:, tt].rearrange("p c h -> p (c h)"), core.ident_b[:, :])
                    ins.then_inc(s["mT_psum"], 1)

                def keyed_scores(i, buf, v, alone, maxima):
                    kt, g = UNITS[v]
                    if v == 0:
                        pe.wait_ge(s["m_stack"], 32)
                        pe.sem_clear(s["m_stack"])
                    if maxima and v == 0:
                        pe.wait_ge(s["s_max"], NU * maxima[1] + 2)
                    if alone and v == 1:
                        pe.wait_ge(s["mT_ready"], i)
                    elif NU * i + v > 0:
                        pe.wait_ge(s["p_ready"], NU * i + v - (1 if alone and v > 0 else 0))
                    q0 = kt * P if causal else 0
                    nq = S - q0
                    for pp in range(2):
                        o = PS[:, t_bank(v, alone) + pp, 0:2 * nq].rearrange("p (a q) -> p a q", a=2)
                        ins = mm(o, Kst[:, buf, 2 * g + pp, kt * P:(kt + 1) * P], Qm[:, buf, :, 2 * g + pp, q0:S],
                                 start=True, stop=True, **free)
                        if causal:
                            ins = mm(o[:, :, 0:P], core.ident_b[:, :],
                                     core.neg_k[:, :].unsqueeze(1).broadcast_to([P, 2, P]), start=False, stop=True, **free)
                        if masked:
                            ins = mm(o, core.ident_b[:, :], neg[:, buf, 1, kt].unsqueeze(1).broadcast_to([P, 2, S]),
                                     start=False, stop=True, **free)
                    ins.then_inc(s["st_psum"], 1)

                def times_v(i, buf, v):
                    kt, g = UNITS[v]
                    pe.wait_ge(s["p_ready"], NU * i + v + 1)
                    if gated:
                        pe.wait_ge(s["pg_ready"], NU * i + v + 1)
                    if v == 0:
                        pe.wait_ge(s["setup"], core.n_setup)
                    if v == 0 and i > 0:
                        pe.wait_ge(s["o_ready"], i)
                    q0 = kt * P if causal else 0
                    nq = S - q0
                    for j in range(4):
                        o = PS[32 * j:32 * j + 32, O_BANK + g // 2, (g % 2) * S + q0:(g % 2) * S + S]
                        opening = kt == 0 and g % 2 == 0
                        probs = Pr[:, v % 2, j * nq:(j + 1) * nq]
                        if gated:
                            ins = mm(o, vaug[:, buf, kt, 4 * g + j, :], PG[:, v % 2, j * nq:(j + 1) * nq],
                                     start=opening, stop=True, **free)
                            ins = mm(o, den[:, :], probs, start=False, stop=True, **free)
                        else:
                            ins = mm(o, vaug[:, buf, kt, 4 * g + j, :], probs, start=opening, stop=True, **free)
                    ins.then_inc(s["pv_done"], 1)

                def turn_heads(i, front):
                    pe.wait_ge(s["o_ready"], i + 1)
                    for t in range(TS):
                        if front and t == 0:
                            pe.wait_ge(s["q_full" if rope else "q_rest"], front[1] + 1)
                        if front and t == 1:
                            pe.wait_ge(s["v_ready"], front[1] + 1)
                        for g in range(NG):
                            ins = tr(PS[:, FRONT + t, g * P:(g + 1) * P], Osb[:, g, t * P:(t + 1) * P], w("ident"))
                        ins.then_inc(s["tr_psum"], 1)

                def turn_context(i):
                    pe.wait_ge(s["a_ready"], TS * (i + 1))
                    for t in range(TS):
                        ins = tr(PS[:, FRONT, t * P:(t + 1) * P], A[:, t, :], w("ident"))
                    ins.then_inc(s["aT_psum"], 1)

                def times_wo(i):
                    pe.wait_ge(s["aT_ready"], i + 1)
                    for t in range(TS):
                        ins = mm(PS[:, FRONT + 1, t * P:(t + 1) * P], AT[:, t * P:(t + 1) * P], w(f"{st}_wo"),
                                 start=(t == 0), stop=True, **free)
                    ins.then_inc(s["y_psum"], 1)

                def run_step(front, maxima, output, tail, norm=None):
                    if front and output and output[1] > 1:
                        pe.wait_ge(s["x_done"], output[1] - 1)
                    for u in range(NU + LEAD):
                        if maxima and u < NU:
                            scores(maxima[1], maxima[2], u, maxima[1] > 0 or not output, alone=not output,
                                   outputs=output[1] if output else 0)
                        if output and u >= LEAD:
                            keyed_scores(output[1], output[2], u - LEAD, alone=not maxima, maxima=maxima)
                        if output and u > LEAD:
                            times_v(output[1], output[2], u - LEAD - 1)
                        if front and u == 0:
                            turn_norm(front[1])
                        if front and u == 1:
                            project(front[1])
                        if front and u == 3:
                            project_v(front[1])
                        if tail and u == 6:
                            turn_heads(tail[1], front)
                        if maxima and u == NU:
                            turn_max(maxima[1])
                        if tail and u == 9:
                            turn_context(tail[1])
                    if output:
                        times_v(output[1], output[2], NU - 1)
                    if tail:
                        times_wo(tail[1])

                stages_of(run_step, lambda: end_pass(core, pe, "go_pe"), pe.Fori)

            @block.scalar
            def _(act):
                a = nc.scalar.activation
                step = Step(act, s["act_step"])

                def cut_first(what, i):
                    if rope:
                        act.wait_ge(s[what + "_full"], i + 1)
                        src = dict(in_=rot[what][:, 2, :], func=ACT.Copy)
                    else:
                        act.wait_ge(s[what + "_psum"], i + 1)
                        src = dict(in_=PS[:, bank_of[what], 0:S], func=ACT.Identity, bias=w(f"{st}_b{what}"))
                    if i > 0:
                        act.wait_ge(s[what + "_bounce"], 32 * i)
                    a(part[what][:, SLOT[what][0], :], **src).then_inc(s[what + "_p1"], 1)

                def cut_second(what, i):
                    act.wait_ge(s[what + "_rest"], i + 1)
                    a(part[what][:, SLOT[what][1], :], rest[what][:, :], ACT.Copy).then_inc(s[what + "_p2"], 1)

                def exponentials(i, u, alone):
                    kt, g = UNITS[u]
                    act.wait_ge(s["st_psum"], NU * i + u + 1)
                    if NU * i + u >= 2:
                        act.wait_ge(s["pv_done"], NU * i + u - 1)
                    nq = S - kt * P if causal else S
                    a(Pr[:, u % 2, 0:4 * nq].rearrange("p (a k) -> p a k", a=2),
                      PS[:, t_bank(u, alone):t_bank(u, alone) + 2, 0:2 * nq], ACT.Exp, scale=SCALE)\
                        .then_inc(s["p_ready"], 1)

                def run_step(front, maxima, output, tail, norm=None):
                    for u in range(NU + LEAD):
                        if output and u >= LEAD:
                            exponentials(output[1], u - LEAD, alone=not maxima)
                        if front and u == 0:
                            act_copy(core, act, L["xT"][:, :], PS[:, FRONT, 0:S], s["xT_psum"], front[1] + 1, s["xT_ready"])
                        if front and u == 2:
                            cut_first("k", front[1])
                        if front and u == 3:
                            cut_first("q", front[1])
                        if front and u == 4:
                            cut_second("k", front[1])
                            cut_second("q", front[1])
                        if maxima and u == NU:
                            i = maxima[1]
                            act.wait_ge(s["mT_psum"], i + 1)
                            if i > 0:
                                act.wait_ge(s["m_bounce"], 16 * i)
                            a(mT[:, :], PS[0:NMAX * H, S_BANK, 0:P].bitcast(BF16), ACT.Copy).then_inc(s["mT_ready"], 1)
                        if norm and u == NU:
                            act_layernorm(core, act, step, L, n=norm[1], slot=0)
                    if tail:
                        act_copy(core, act, AT[:, :], PS[:, FRONT, 0:S], s["aT_psum"], tail[1] + 1, s["aT_ready"])

                def segment_end():
                    end_pass(core, act, "go_act")
                    step.n = 0

                stages_of(run_step, segment_end, act.Fori, lambda p: act_layernorm(core, act, step, L, n=0, slot=0))

            @block.vector
            def _(dve):
                v = nc.vector
                step = Step(dve, s["dve_step"])

                def apply_norm(p, i):
                    if i > 0:
                        dve.wait_ge(s["xT_psum"], i)
                    dve_norm_apply(core, dve, step, L, lambda t: tok(p, t), L["xn"], s["xn_ready"], i, TS)

                def first_norm(p):
                    dve_norm_stats(core, dve, step, L, lambda t: tok(p, t), 0, TS)
                    apply_norm(p, 0)

                def rotate(what, i):
                    b = bank_of[what]
                    dve.wait_ge(s[what + "_psum"], i + 1)
                    for n, (tab, sw) in enumerate((("rope_cos", ""), ("rope_sin", "s"))):
                        step.mark(v.scalar_tensor_tensor(rot[what][:, n, :], PS[:, b, n * S:(n + 1) * S],
                                                         w(f"{st}_b{what}{sw}"), w(tab), ALU.add, ALU.mult))
                    dve.wait_ge(s["dve_step"], step.n)
                    v.tensor_tensor(rot[what][:, 2, :], rot[what][:, 0, :], rot[what][:, 1, :], ALU.add)\
                        .then_inc(s[what + "_full"], 1)

                def cut_rest(what, i):
                    dve.wait_ge(s[what + "_p1"], i + 1)
                    if rope:
                        v.tensor_tensor(rest[what][:, :], rot[what][:, 2, :], part[what][:, SLOT[what][0], :], ALU.subtract)\
                            .then_inc(s[what + "_rest"], 1)
                    else:
                        v.scalar_tensor_tensor(rest[what][:, :], PS[:, bank_of[what], 0:S], w(f"{st}_b{what}"),
                                               part[what][:, SLOT[what][0], :], ALU.add, ALU.subtract)\
                            .then_inc(s[what + "_rest"], 1)

                def cut_third(i):
                    for what in "kq":
                        dve.wait_ge(s[what + "_p2"], i + 1)
                        v.tensor_tensor(part[what][:, SLOT[what][2], :], rest[what][:, :], part[what][:, SLOT[what][1], :],
                                        ALU.subtract)\
                            .then_inc(s[what + "_p3"], 1)

                def take_v(i, buf):
                    dve.wait_ge(s["v_psum"], i + 1)
                    for t in range(TS):
                        ins = v.tensor_tensor(vaug[:, buf, t, :, 0:DH],
                                              PS[:, FRONT + 1, t * P:(t + 1) * P].rearrange("p (h d) -> p h d", h=H),
                                              w(f"{st}_bv").rearrange("p (h d) -> p h d", h=H), ALU.add)
                    ins.then_inc(s["v_ready"], 1)

                def row_max(i, u, alone):
                    tt, g = UNITS[u]
                    dve.wait_ge(s["s_psum"], NU * i + u + 1)
                    nk = (tt + 1) * P if causal else S
                    o = mx[:, tt, :].rearrange("p (r a) -> p r a", r=2)[:, :, 2 * g:2 * g + 2]
                    bank = s_bank(u, alone)
                    src = PS[:, bank:bank + 2, :].rearrange("p r (a k) -> p r a k", a=2)[:, :, :, 0:nk]
                    v.tensor_reduce(o, src, AX, ALU.max).then_inc(s["s_max"], 1)

                def cut_max(i):
                    dve.wait_ge(s["s_max"], NU * (i + 1))
                    if i > 0:
                        dve.wait_ge(s["mT_psum"], i)
                    step(v.tensor_copy(mpart[:, :, 0, :], mx[:, :, :]))
                    step(v.tensor_tensor(mrest[:, :, :], mx[:, :, :], mpart[:, :, 0, :], ALU.subtract))
                    step(v.tensor_copy(mpart[:, :, 1, :], mrest[:, :, :]))
                    v.tensor_tensor(mpart[:, :, 2, :], mrest[:, :, :], mpart[:, :, 1, :], ALU.subtract)\
                        .then_inc(s["m_parts"], 1)

                def gate(i, buf, u):
                    dve.wait_ge(s["p_ready"], NU * i + u + 1)
                    if NU * i + u >= 2:
                        dve.wait_ge(s["pv_done"], NU * i + u - 1)
                    v.tensor_tensor(PG[:, u % 2, :].rearrange("p (h q) -> p h q", h=4),
                                    Pr[:, u % 2, :].rearrange("p (h q) -> p h q", h=4),
                                    G[:, buf, UNITS[u][0], :].unsqueeze(1).broadcast_to([P, 4, S]), ALU.mult)\
                        .then_inc(s["pg_ready"], 1)

                def divide(i):
                    for t in range(TS):
                        dve.wait_ge(s["tr_psum"], TS * i + t + 1)
                        o = PS[:, FRONT + t, :].rearrange("p (h r) -> p h r", r=32)
                        step(v.reciprocal(rden[:, t, :].unsqueeze(2), o[:, :, DH:DH + 1]))
                        v.tensor_tensor(A[:, t, :].rearrange("p (h d) -> p h d", h=H), o[:, :, 0:DH],
                                        rden[:, t, :].unsqueeze(2).broadcast_to([P, H, DH]), ALU.mult)\
                            .then_inc(s["a_ready"], 1)

                def residual(p, i):
                    if bias:
                        dve.wait_ge(s["xb_ready"], TS * (i + 1))
                    dve.wait_ge(s["y_psum"], i + 1)
                    x = core.X[:, bass.ds(p * TS, TS), :]
                    v.tensor_tensor(x, PS[:, FRONT + 1, 0:S].rearrange("p (t d) -> p t d", t=TS),
                                    Xb[:, :, :] if bias else x, ALU.add).then_inc(s["x_done"], 1)

                def run_step(front, maxima, output, tail, norm=None):
                    if front:
                        p, i, buf = front
                    for u in range(NU + LEAD):
                        if maxima and u < NU:
                            row_max(maxima[1], u, alone=not output)
                        if front and u == 2:
                            (rotate if rope else cut_rest)("k", i)
                        if front and u == 3:
                            (rotate if rope else cut_rest)("q", i)
                        if front and u == 4:
                            take_v(i, buf)
                            if rope:
                                cut_rest("k", i)
                                cut_rest("q", i)
                        if front and u == 5:
                            cut_third(i)
                        if front and (output or not first) and u == 6:
                            if first:
                                dve.wait_ge(s["setup"], core.n_setup)
                            for par in range(2):
                                v.memset(Qm[64 * par + MAX_ROW:64 * par + MAX_ROW + NMAX, buf, par], 0.0)\
                                    .then_inc(s["zero_max"], 1)
                        if norm and u == NU - 1:
                            dve_norm_stats(core, dve, step, L, lambda t: tok(norm[0], t), norm[1], TS)
                        if maxima and u == NU - 1:
                            cut_max(maxima[1])
                        if output and gated and u >= LEAD:
                            if u == LEAD and output[1] >= 2:
                                dve.wait_ge(s["gp_in"], 16 * (output[1] - 1))
                            gate(output[1], output[2], u - LEAD)
                        if tail and u == NU - 1:
                            divide(tail[1])
                        if norm and u == NU:
                            apply_norm(*norm)
                    if tail:
                        residual(*tail)
                    if output:
                        dve.wait_ge(s["pv_done"], NU * (output[1] + 1))
                        v.tensor_copy(Osb[:, :, :].rearrange("p g q -> p (g q)"),
                                      PS[:, O_BANK:O_BANK + 2, :].rearrange("p a q -> p (a q)"))\
                            .then_inc(s["o_ready"], 1)

                def segment_end():
                    end_pass(core, dve, "go_dve")
                    step.n = 0

                stages_of(run_step, segment_end, dve.Fori, first_norm)


def experts(core, st):
    nc, s, PS, w = core.nc, core.sem, core.PS, core.w
    ly = st[:2]
    core.n_experts += 1
    nth = core.n_experts
    W1, W2 = core.ffn
    two_norms = st == "L0f"
    TT = ALL_TILES
    LOOPS = 2
    NB = BLOCKS // LOOPS
    STORE = NB // 3
    H_BANK, T_BANK, Y_BANK = 0, 2, 4

    with ExitStack() as c:
        sb = core.buffers(c)
        L = ln_buffers(core, c, TT)
        xh = sb("xh", [P, TT, D]) if two_norms else L["xn"]
        lg, eq, sc, msk, cum = (sb(n, [P, TT, E]) for n in ("lg", "eq", "sc", "msk", "cum"))
        mx, mc, gain = (sb(n, [P, TT]) for n in ("mx", "mc", "gain"))
        PAD = TT // 2
        runs = [sb(f"runs{k}", [P, PAD + TT, E]) for k in range(2)]
        ends = [sb(f"ends{k}", [P, E // 2 + E]) for k in range(2)]
        over = sb("over", [P, E, TT])
        past = sb("past", [P, BLOCKS, E])
        nb, base, ebf = sb("nb", [P, E]), sb("base", [P, E]), sb("ebf", [P, BLOCKS])
        posf, pos = sb("posf", [P, TT]), sb("pos", [P, TT], I32)
        STEPS = {"one": 1, "chunks": FC, "channels": D, "hidden": F}
        eb = {n: sb(f"eb_{n}", [P, BLOCKS], I32) for n in STEPS}
        xs = sb("xs", [P, BLOCKS, D])
        xsT = sb("xsT", [P, BLOCKS * P])
        xb = sb("xb", [P, 2, P])
        hs = sb("hs", [P, 2, F])
        hT = sb("hT", [P, 2, FC, P])
        yg = sb("yg", [P, TT, D])

        def experts_of(it, name, engine):
            return nc.values_load_multi_w_load_instructions(
                eb[name][0:1, bass.ds(it * NB, NB)], engines=(engine,), min_val=0, max_val=(E - 1) * STEPS[name])[1]

        with nc.Block() as block:

            @block.sync
            def _(sp):
                load_next_weights(core, sp)
                rows = core.dram["sorted_in"].rearrange("(b p) d -> p b d", p=P)
                sp.wait_ge(s["scattered"], 16 * TT * nth)
                for q in range(BLOCKS // 4):
                    part = slice(4 * q, 4 * q + 4)
                    sp.dma_start(xs[:, part, :], rows[:, part, :]).then_inc(s[f"sorted_in{q}"], 16)
                out = core.dram["sorted_out"].rearrange("(b p) d -> p b d", p=P)
                with sp.Fori(0, LOOPS) as it:
                    for q in range(NB // STORE):
                        sp.wait_ge(s["y_ready"], STORE * (q + 1))
                        part = bass.ds(it * NB + q * STORE, STORE)
                        sp.dma_start(out[:, part, :], xs[:, part, :]).then_inc(s["y_out"], 16)
                    end_pass_sync(core, sp, "experts")
                end_pass_sync(core, sp, "experts")
                await_next_weights(core, sp)

            @block.gpsimd
            def _(pool):
                for k in range(2):
                    nc.gpsimd.memset(runs[k][:, 0:PAD, :], 0.0).then_inc(s["pads"], 1)
                    nc.gpsimd.memset(ends[k][:, 0:E // 2], 0.0).then_inc(s["pads"], 1)
                pool.wait_ge(s["pos_ready"], 1)
                if two_norms:
                    pool.wait_ge(s["xh_ready"], TT)
                for t in range(TT):
                    pool.indirect_dma_start(core.dram["sorted_in"], bass.IndirectOffsetOnAxis(pos[:, t:t + 1], 0),
                                            xh[:, t, :], None).then_inc(s["scattered"], 16)
                with pool.Fori(0, LOOPS) as it:
                    end_pass(core, pool, "go_pool")
                pool.wait_ge(s["y_out"], 16 * LOOPS * (NB // STORE) * nth)
                for t in range(TT):
                    pool.indirect_dma_start(yg[:, t, :], None, core.dram["sorted_out"],
                                            bass.IndirectOffsetOnAxis(pos[:, t:t + 1], 0)).then_inc(s[f"gathered{t}"], 16)
                end_pass(core, pool, "go_pool")

            @block.tensor
            def _(pe):
                mm, tr = nc.tensor.matmul, nc.tensor.transpose
                free = dict(skip_group_check=True)
                for g in range(TT // 4):
                    for t in range(4 * g, 4 * g + 4):
                        pe.wait_ge(s["xn_ready"], t + 1)
                        ins = tr(PS[:, g, (t % 4) * P:(t % 4 + 1) * P], L["xn"][:, t, :], w("ident"))
                    ins.then_inc(s["xT_psum"], 1)
                for t in range(TT):
                    pe.wait_ge(s["xT_ready"], t // 4 + 1)
                    ins = mm(PS[:, 6, t * E:(t + 1) * E], L["xT"][:, t * P:(t + 1) * P], w(f"{ly}_gate"),
                             start=(t == 0), stop=True, **free)
                ins.then_inc(s["gate_psum"], 1)
                pe.wait_ge(s["gate_mask"], 1)
                flat = msk[:, :, :].rearrange("p t e -> p (t e)")
                mm(PS[:, 4, 0:TT * E], w("tri"), flat, start=True, stop=True, **free).then_inc(s["cum_psum"], 1)
                mm(PS[:, 5, 0:TT * E], w("ones"), flat, start=True, stop=True, **free).then_inc(s["cum_psum"], 1)
                pe.wait_ge(s["cum_used"], 1)
                for g in range(BLOCKS // 4):
                    pe.wait_ge(s[f"sorted_in{g}"], 16)
                    for k in range(4):
                        ins = tr(PS[:, g, k * P:(k + 1) * P], xs[:, 4 * g + k, :], w("ident"))
                    ins.then_inc(s["xsT_psum"], 1)
                pe.wait_ge(s["plan_ready"], len(STEPS))
                pe.wait_ge(s[f"ffn_w{ly[1]}"], 32)
                with pe.Fori(0, LOOPS) as it:
                    expert = experts_of(it, "hidden", ENGINE.PE)

                    def first(j):
                        pe.wait_ge(s["xb_ready"], j + 1)
                        if j >= 2:
                            pe.wait_ge(s["h_raw"], j - 1)
                        mm(PS[:, H_BANK + j % 2, :], xb[:, j % 2, :], W1[:, bass.ds(expert[j], F)],
                           start=True, stop=True, **free).then_inc(s["z_psum"], 1)

                    def turn(j):
                        pe.wait_ge(s["h_raw"], j + 1)
                        if j >= 2:
                            pe.wait_ge(s["h_ready"], FC * (j - 1))
                        for ch in range(FC):
                            ins = tr(PS[:, T_BANK + j % 2, ch * P:(ch + 1) * P], hs[:, j % 2, ch * P:(ch + 1) * P], w("ident"))
                        ins.then_inc(s["hT_psum"], 1)

                    def second(j):
                        pe.wait_ge(s["h_ready"], FC * (j + 1))
                        if j >= 2:
                            pe.wait_ge(s["y_ready"], j - 1)
                        for ch in range(FC):
                            ins = mm(PS[:, Y_BANK + j % 2, 0:P], hT[:, j % 2, ch, :],
                                     W2[:, bass.ds(expert[j] + ch * P, P)], start=(ch == 0), stop=(ch == FC - 1), **free)
                        ins.then_inc(s["y_psum"], 1)

                    for j in range(NB + 2):
                        if j < NB:
                            first(j)
                        if 0 <= j - 1 < NB:
                            turn(j - 1)
                        if j >= 2:
                            second(j - 2)
                    end_pass(core, pe, "go_pe")
                end_pass(core, pe, "go_pe")

            @block.scalar
            def _(act):
                a = nc.scalar.activation
                step = Step(act, s["act_step"])
                act_layernorm(core, act, step, L)
                for g in range(TT // 4):
                    act_copy(core, act, L["xT"][:, g * 4 * P:(g + 1) * 4 * P], PS[:, g, :], s["xT_psum"], g + 1, s["xT_ready"])
                if two_norms:
                    act_layernorm(core, act, step, L, n=1)
                if st == "L1f":
                    act.wait_ge(s["gexp_in"], 1)
                    a(sc[:, :, :], eq[:, :, :], ACT.Exp).then_inc(s["gexp_out"], 1)
                if st == "L0f":
                    act.wait_ge(s["gexp_in"], 1)
                    a(gain[:, :], mx[:, :], ACT.Exp, scale=-1.0).then_inc(s["gexp_out"], 1)
                for g in range(BLOCKS // 4):
                    act_copy(core, act, xsT[:, g * 4 * P:(g + 1) * 4 * P], PS[:, g, :], s["xsT_psum"], g + 1, s["xsT_ready"])
                act.wait_ge(s["plan_ready"], len(STEPS))
                with act.Fori(0, LOOPS) as it:
                    expert = experts_of(it, "chunks", ENGINE.Activation)
                    for j in range(NB + 1):
                        if j < NB:
                            act.wait_ge(s["z_psum"], j + 1)
                            if j >= 2:
                                act.wait_ge(s["hT_psum"], j - 1)
                            a(hs[:, j % 2, :], PS[:, H_BANK + j % 2, :], ACT.Copy).then_inc(s["h_raw"], 1)
                        if j >= 1:
                            i = j - 1
                            act.wait_ge(s["hT_psum"], i + 1)
                            if i >= 2:
                                act.wait_ge(s["y_psum"], i - 1)
                            for ch in range(FC):
                                a(hT[:, i % 2, ch, :], PS[:, T_BANK + i % 2, ch * P:(ch + 1) * P], ACT.Relu,
                                  bias=w(f"{ly}_b1")[:, bass.ds(expert[i] + ch, 1)]).then_inc(s["h_ready"], 1)
                    end_pass(core, act, "go_act")
                end_pass(core, act, "go_act")

            @block.vector
            def _(dve):
                v = nc.vector
                bc = lambda ap: ap.unsqueeze(2).broadcast_to([P, TT, E])
                bt = lambda ap: ap.unsqueeze(1).broadcast_to([P, TT, E])
                step = Step(dve, s["dve_step"])
                tile = lambda t: core.X[:, t, :]
                dve_norm_stats(core, dve, step, L, tile, 0, TT)
                dve_norm_apply(core, dve, step, L, tile, L["xn"], s["xn_ready"], 0, TT)
                if two_norms:
                    dve.wait_ge(s["xn_ready"], TT)
                    tile_n = lambda t: L["xn"][:, t, :]
                    dve_norm_stats(core, dve, step, L, tile_n, 1, TT, slot=1)
                    dve_norm_apply(core, dve, step, L, tile_n, xh, s["xh_ready"], 1, TT, slot=1)
                dve.wait_ge(s["gate_psum"], 1)
                logits = PS[:, 6, 0:TT * E].rearrange("p (t e) -> p t e", t=TT)
                if ly == "L0":
                    step(v.tensor_copy(lg[:, :, :], logits))
                else:
                    step(v.tensor_tensor(lg[:, :, :], logits, bt(w(f"{ly}_gate_bias")), ALU.add))
                step(v.tensor_reduce(mx[:, :], lg[:, :, :], AX, ALU.max))
                step(v.tensor_tensor(eq[:, :, :], lg[:, :, :], bc(mx[:, :]), ALU.is_equal))
                step(v.tensor_tensor(sc[:, :, :], eq[:, :, :], bt(w("countdown")), ALU.mult))
                step(v.tensor_reduce(mc[:, :], sc[:, :, :], AX, ALU.max))
                v.tensor_tensor(msk[:, :, :], sc[:, :, :], bc(mc[:, :]), ALU.is_equal).then_inc(s["gate_mask"], 1)
                dve.wait_ge(s["gate_mask"], 1)
                dve.wait_ge(s["pads"], 4)
                dve.wait_ge(s["cum_psum"], 2)
                counts = PS[:, 5, 0:TT * E].rearrange("p (t e) -> p t e", t=TT)
                step(v.tensor_copy(runs[0][:, PAD:, :], counts))
                k = 0
                for shift in (1, 2, 4, 8):
                    step(v.tensor_tensor(runs[1 - k][:, PAD:, :], runs[k][:, PAD:, :],
                                         runs[k][:, PAD - shift:PAD + TT - shift, :], ALU.add))
                    k = 1 - k
                total = runs[k][:, PAD + TT - 1, :]
                step(v.tensor_scalar(base[:, :], total, 1.0 / P, None, ALU.mult))
                step(v.tensor_tensor(over[:, :, :], base[:, :].unsqueeze(2).broadcast_to([P, E, TT]),
                                     w("numbers")[:, 0:TT].unsqueeze(1).broadcast_to([P, E, TT]), ALU.is_gt))
                step(v.tensor_reduce(ends[0][:, E // 2:], over[:, :, :], AX, ALU.add))
                step(v.tensor_copy(nb[:, :], ends[0][:, E // 2:]))
                m = 0
                for shift in (1, 2, 4):
                    step(v.tensor_tensor(ends[1 - m][:, E // 2:], ends[m][:, E // 2:],
                                         ends[m][:, E // 2 - shift:E // 2 + E - shift], ALU.add))
                    m = 1 - m
                end = ends[m][:, E // 2:]
                step(v.tensor_tensor(base[:, :], end, nb[:, :], ALU.subtract))
                step(v.tensor_scalar(base[:, :], base[:, :], float(P), -1.0, ALU.mult, ALU.add))
                step(v.tensor_tensor(cum[:, :, :], PS[:, 4, 0:TT * E].rearrange("p (t e) -> p t e", t=TT),
                                     runs[k][:, PAD:, :], ALU.add))
                step(v.tensor_tensor(cum[:, :, :], cum[:, :, :], bt(base[:, :]), ALU.add))
                v.tensor_tensor(cum[:, :, :], cum[:, :, :], counts, ALU.subtract).then_inc(s["cum_used"], 1)
                dve.wait_ge(s["cum_used"], 1)
                step(v.tensor_tensor(cum[:, :, :], cum[:, :, :], msk[:, :, :], ALU.mult))
                step(v.tensor_reduce(posf[:, :], cum[:, :, :], AX, ALU.add))
                v.tensor_copy(pos[:, :], posf[:, :]).then_inc(s["pos_ready"], 1)
                step(v.tensor_tensor(past[:, :, :], end.unsqueeze(1).broadcast_to([P, BLOCKS, E]),
                                     w("numbers").unsqueeze(2).broadcast_to([P, BLOCKS, E]), ALU.is_le))
                step(v.tensor_reduce(ebf[:, :], past[:, :, :], AX, ALU.add))
                step(v.tensor_scalar(ebf[:, :], ebf[:, :], float(E - 1), None, ALU.min))
                for n, k in STEPS.items():
                    v.tensor_scalar(eb[n][:, :], ebf[:, :], float(k), None, ALU.mult).then_inc(s["plan_ready"], 1)
                if st == "L0f":
                    step(v.tensor_scalar(mx[:, :], mx[:, :], -80.0, None, ALU.max))
                    v.tensor_copy(mc[:, :], mx[:, :]).then_inc(s["gexp_in"], 1)
                    dve.wait_ge(s["gexp_out"], 1)
                    dve.wait_ge(s["gexp_in"], 1)
                    step(v.tensor_scalar(gain[:, :], gain[:, :], 1.0, None, ALU.add))
                    step(v.reciprocal(gain[:, :], gain[:, :]))
                if st == "L1f":
                    v.tensor_tensor(eq[:, :, :], lg[:, :, :], bc(mx[:, :]), ALU.subtract).then_inc(s["gexp_in"], 1)
                    dve.wait_ge(s["gexp_out"], 1)
                    step(v.tensor_reduce(gain[:, :], sc[:, :, :], AX, ALU.add))
                    step(v.reciprocal(gain[:, :], gain[:, :]))
                dve.wait_ge(s["plan_ready"], len(STEPS))
                with dve.Fori(0, LOOPS) as it:
                    channels = experts_of(it, "channels", ENGINE.DVE)
                    expert = experts_of(it, "one", ENGINE.DVE) if two_norms else None
                    dve.wait_ge(s["xsT_ready"], BLOCKS // 4 * nth)
                    for j in range(NB + 2):
                        if j < NB:
                            if j >= 2:
                                dve.wait_ge(s["z_psum"], j - 1)
                            src = xsT[:, bass.ds((it * NB + j) * P, P)]
                            if two_norms:
                                v.tensor_scalar(xb[:, j % 2, :], src, w("L0_gamma")[:, bass.ds(expert[j], 1)],
                                                w("L0_beta")[:, bass.ds(expert[j], 1)], ALU.mult, ALU.add)\
                                    .then_inc(s["xb_ready"], 1)
                            else:
                                v.tensor_copy(xb[:, j % 2, :], src).then_inc(s["xb_ready"], 1)
                        if j >= 2:
                            i = j - 2
                            dve.wait_ge(s["y_psum"], i + 1)
                            v.tensor_tensor(xs[:, bass.ds(it * NB + i, 1), :].rearrange("p a d -> p (a d)"),
                                            PS[:, Y_BANK + i % 2, 0:P], w(f"{ly}_b2")[:, bass.ds(channels[i], D)],
                                            ALU.add).then_inc(s["y_ready"], 1)
                    end_pass(core, dve, "go_dve")
                for t in range(TT):
                    dve.wait_ge(s[f"gathered{t}"], 16 * nth)
                    if st == "L2f":
                        v.tensor_tensor(tile(t), tile(t), yg[:, t, :], ALU.add)
                    if st == "L1f":
                        v.scalar_tensor_tensor(tile(t), yg[:, t, :], gain[:, t:t + 1], tile(t), ALU.mult, ALU.add)
                    if st == "L0f":
                        step.mark(v.scalar_tensor_tensor(xh[:, t, :], yg[:, t, :], gain[:, t:t + 1], L["xn"][:, t, :],
                                                         ALU.mult, ALU.add))
                if st == "L0f":
                    dve.wait_ge(s["dve_step"], TT)
                    v.tensor_tensor(core.X[:, :, :], core.X[:, :, :], xh[:, :, :], ALU.add)
                end_pass(core, dve, "go_dve")


def load_ffn(core, eng, ly):
    for n in (0, 1):
        eng.dma_start(core.ffn[n][:, :], core.dram[f"{ly}_ffn{n + 1}"]).then_inc(core.sem[f"ffn_w{ly[1]}"], 16)


def channel_attention(core):
    nc, s, PS, w = core.nc, core.sem, core.PS, core.w
    with ExitStack() as c:
        sb = core.buffers(c)
        L = ln_buffers(core, c, ALL_TILES)
        f2 = sb("f2", [P, ALL_TILES, D])
        et = sb("et", [P, 1])
        junk = sb("junk", [P, S])
        ss, lns, rs, us = (sb(n, [P, 2, NSEQ]) for n in ("ss", "lns", "rs", "us"))
        qk = sb("qk", [P, 2, NT])
        qkt = sb("qkt", [P, 2, NT])
        vT = sb("vT", [P, NT])
        sm, ex, en = (sb(n, [P, NSEQ, P]) for n in ("sm", "ex", "en"))
        rm, rd = sb("rm", [P, NSEQ]), sb("rd", [P, NSEQ])
        aT = sb("aT", [P, NSEQ, P])
        oT = sb("oT", [P, NT])
        TINY, UP = 1e-24, 2.0 ** 20
        with nc.Block() as block:

            @block.sync
            def _(sp):
                load_next_weights(core, sp)
                load_ffn(core, sp, "L2")
                end_pass_sync(core, sp, "channel_attention")
                with sp.Fori(0, NPASS) as it:
                    end_pass_sync(core, sp, "channel_attention")
                await_next_weights(core, sp)

            @block.gpsimd
            def _(pool):
                end_pass(core, pool, "go_pool")
                with pool.Fori(0, NPASS) as it:
                    end_pass(core, pool, "go_pool")

            @block.tensor
            def _(pe):
                mm, tr = nc.tensor.matmul, nc.tensor.transpose
                free = dict(skip_group_check=True)
                pe_turn_all(core, pe, f2, "xh_ready")
                pe.wait_ge(s["xT_ready"], ALL_TILES // 4)
                end_pass(core, pe, "go_pe")
                with pe.Fori(0, NPASS) as it:
                    xT = L["xT"][:, bass.ds(it * NT, NT)]
                    for n in range(3):
                        mm(PS[:, n, :], w("L2a_qkv")[:, n * P:(n + 1) * P], xT, start=True, stop=True)\
                            .then_inc(s["q_psum"], 1)
                    for n in range(2):
                        pe.wait_ge(s["a_in"], 2 * n + 2)
                        for t in range(T):
                            ins = tr(PS[:, 3 + n, t * P:(t + 1) * P], qk[:, n, t * P:(t + 1) * P], w("ident"))
                        ins.then_inc(s["a_out"], 1)
                    pe.wait_ge(s["b_in"], 2)
                    for b in range(NSEQ):
                        for tt in range(TS):
                            t = b * TS + tt
                            ins = mm(PS[:, 5, b * P:(b + 1) * P], qkt[:, 0, t * P:(t + 1) * P],
                                     qkt[:, 1, t * P:(t + 1) * P], start=(tt == 0), stop=(tt == TS - 1), **free)
                    ins.then_inc(s["b_out"], 1)
                    pe.wait_ge(s["c_in"], 1)
                    for b in range(NSEQ):
                        ins = tr(PS[:, 6, b * P:(b + 1) * P], en[:, b, :], w("ident"))
                    ins.then_inc(s["c_out"], 1)
                    pe.wait_ge(s["d_in"], 1)
                    pe.wait_ge(s["v_ready"], 1)
                    for b in range(NSEQ):
                        ins = mm(PS[:, 7, b * S:(b + 1) * S], aT[:, b, :], vT[:, b * S:(b + 1) * S],
                                 start=(b == 0), stop=True, **free)
                    ins.then_inc(s["d_out"], 1)
                    pe.wait_ge(s["e_in"], 1)
                    for t in range(T):
                        ins = mm(PS[:, 0, t * P:(t + 1) * P], oT[:, t * P:(t + 1) * P], w("L2a_out"),
                                 start=(t == 0), stop=True, **free)
                    ins.then_inc(s["y_psum"], 1)
                    end_pass(core, pe, "go_pe")

            @block.scalar
            def _(act):
                a = nc.scalar.activation
                step = Step(act, s["act_step"])
                act_layernorm(core, act, step, L)
                act_layernorm(core, act, step, L, n=1)
                for g in range(ALL_TILES // 4):
                    act.wait_ge(s["xT_psum"], g + 1)
                    a(L["xT"][:, g * 4 * P:(g + 1) * 4 * P], PS[:, g, :], ACT.Copy, scale=w("L2a_norm"))\
                        .then_inc(s["xT_ready"], 1)
                end_pass(core, act, "go_act")
                with act.Fori(0, NPASS) as it:
                    step = Step(act, s["act_step"])
                    step(a(et[:, :], w("L2a_temp"), ACT.Exp))
                    for n in range(2):
                        act.wait_ge(s["q_psum"], n + 1)
                        for b in range(NSEQ):
                            step.mark(a(junk[:, :], PS[:, n, b * S:(b + 1) * S], ACT.Square,
                                        accum_out=ss[:, n, b:b + 1]))
                            act.wait_ge(s["act_step"], step.n)
                    a(junk[:, 0:1], et[:, :], ACT.Copy).then_inc(s["f_in"], 1)
                    act_copy(core, act, vT[:, :], PS[:, 2, :], s["q_psum"], 3, s["v_ready"])
                    act.wait_ge(s["f_out"], 1)
                    step(a(lns[:, :, :], us[:, :, :], ACT.Ln, scale=UP))
                    a(rs[:, :, :], lns[:, :, :], ACT.Exp, scale=-0.5).then_inc(s["f_in"], 1)
                    act_copy(core, act, qkt[:, 0, :], PS[:, 3, :], s["a_out"], 1, s["b_in"])
                    act_copy(core, act, qkt[:, 1, :], PS[:, 4, :], s["a_out"], 2, s["b_in"])
                    act.wait_ge(s["gexp_in"], 1)
                    a(ex[:, :, :], sm[:, :, :], ACT.Exp).then_inc(s["gexp_out"], 1)
                    act_copy(core, act, aT[:, :, :].rearrange("p b i -> p (b i)"), PS[:, 6, 0:NSEQ * P],
                             s["c_out"], 1, s["d_in"])
                    act_copy(core, act, oT[:, :], PS[:, 7, :], s["d_out"], 1, s["e_in"])
                    end_pass(core, act, "go_act")

            @block.vector
            def _(dve):
                v = nc.vector
                step = Step(dve, s["dve_step"])
                dve_layernorm(core, dve, step, L, lambda t: core.X[:, t, :], L["xn"], s["xn_ready"], tiles=ALL_TILES)
                dve.wait_ge(s["xn_ready"], ALL_TILES)
                dve_layernorm(core, dve, step, L, lambda t: L["xn"][:, t, :], f2, s["xh_ready"], n=1,
                              rms=True, eps=1e-6, tiles=ALL_TILES)
                end_pass(core, dve, "go_dve")
                with dve.Fori(0, NPASS) as it:
                    step = Step(dve, s["dve_step"])
                    dve.wait_ge(s["f_in"], 1)
                    v.tensor_scalar(us[:, :, :], ss[:, :, :], TINY, None, ALU.max).then_inc(s["f_out"], 1)
                    dve.wait_ge(s["f_in"], 2)
                    step(v.tensor_scalar(rs[:, :, :], rs[:, :, :], UP ** 0.5, None, ALU.mult))
                    dve.wait_ge(s["f_out"], 1)
                    step(v.tensor_tensor(us[:, :, :], us[:, :, :], rs[:, :, :], ALU.mult))
                    step(v.tensor_tensor(us[:, :, :], us[:, :, :], rs[:, :, :], ALU.mult))
                    step(v.tensor_scalar(us[:, :, :], us[:, :, :], -0.5, 1.5, ALU.mult, ALU.add))
                    step(v.tensor_tensor(rs[:, :, :], rs[:, :, :], us[:, :, :], ALU.mult))
                    step(v.tensor_scalar(rs[:, 0, :], rs[:, 0, :], et[:, :], None, ALU.mult))
                    for n in range(2):
                        for b in range(NSEQ):
                            v.tensor_scalar(qk[:, n, b * S:(b + 1) * S], PS[:, n, b * S:(b + 1) * S],
                                            rs[:, n, b:b + 1], None, ALU.mult).then_inc(s["a_in"], 1)
                    dve.wait_ge(s["b_out"], 1)
                    step(v.tensor_tensor(sm[:, :, :], PS[:, 5, 0:NSEQ * P].rearrange("p (b j) -> p b j", b=NSEQ),
                                         w("block_diag").unsqueeze(1).broadcast_to([P, NSEQ, P]), ALU.add))
                    step(v.tensor_reduce(rm[:, :], sm[:, :, :], AX, ALU.max))
                    v.tensor_tensor(sm[:, :, :], sm[:, :, :], rm[:, :].unsqueeze(2).broadcast_to([P, NSEQ, P]),
                                    ALU.subtract).then_inc(s["gexp_in"], 1)
                    dve.wait_ge(s["gexp_out"], 1)
                    step(v.tensor_reduce(rd[:, :], ex[:, :, :], AX, ALU.add))
                    step(v.reciprocal(rd[:, :], rd[:, :]))
                    v.tensor_tensor(en[:, :, :], ex[:, :, :], rd[:, :].unsqueeze(2).broadcast_to([P, NSEQ, P]),
                                    ALU.mult).then_inc(s["c_in"], 1)
                    dve_residual(core, dve, it, PS[:, 0, :], s["y_psum"])
                    end_pass(core, dve, "go_dve")


def retention(core):
    nc, s, PS, w = core.nc, core.sem, core.PS, core.w
    with ExitStack() as c:
        sb = core.buffers(c)
        L = ln_buffers(core, c, ALL_TILES)
        t1, t2, rot = (sb(n, [P, 2, NT]) for n in ("t1", "t2", "rot"))
        V = sb("V", [P, ALL_TILES, D])
        D0 = sb("D0", [P, NSEQ, S])
        D1 = sb("D1", [P, NSEQ, P])
        with nc.Block() as block:

            @block.sync
            def _(sp):
                load_next_weights(core, sp)
                end_pass_sync(core, sp, "retention")
                with sp.Fori(0, NPASS) as it:
                    end_pass_sync(core, sp, "retention")
                await_next_weights(core, sp)

            @block.gpsimd
            def _(pool):
                end_pass(core, pool, "go_pool")
                with pool.Fori(0, NPASS) as it:
                    end_pass(core, pool, "go_pool")

            @block.tensor
            def _(pe):
                mm = nc.tensor.matmul
                free = dict(skip_group_check=True)
                for t in range(ALL_TILES):
                    ins = mm(PS[:, 4 + t // 4, (t % 4) * P:(t % 4 + 1) * P], core.ctxT[:, t * P:(t + 1) * P], w("L2x_v"),
                             start=(t % 4 == 0), stop=True, **free)
                    if t % 4 == 3:
                        ins.then_inc(s["v_psum"], 1)
                pe_turn_all(core, pe, L["xn"], "xn_ready")
                end_pass(core, pe, "go_pe")
                with pe.Fori(0, NPASS) as it:
                    part = bass.ds(it * NT, NT)
                    for bank, name, src in ((2, "k", core.ctxT), (3, "ks", core.ctxT), (0, "q", L["xT"]), (1, "qs", L["xT"])):
                        ins = mm(PS[:, bank, :], w(f"L2x_{name}"), src[:, part], start=True, stop=True)
                        if bank % 2:
                            ins.then_inc(s[name[0] + "_psum"], 1)
                    pe.wait_ge(s["a_in"], 2)
                    for b in range(NSEQ):
                        q0 = b * S
                        mm(PS[:, 5, q0:q0 + S], rot[:, 1, q0:q0 + P], rot[:, 0, q0:q0 + S],
                           start=(b == 0), stop=True, **free)
                        ins = mm(PS[:, 6, b * P:(b + 1) * P], rot[:, 1, q0 + P:q0 + S], rot[:, 0, q0 + P:q0 + S],
                                 start=(b == 0), stop=True, **free)
                    ins.then_inc(s["a_out"], 1)
                    pe.wait_ge(s["b_in"], 2)
                    for b in range(NSEQ):
                        for tt in range(TS):
                            t = b * TS + tt
                            o = PS[:, 7, t * P:(t + 1) * P]
                            ins = mm(o, D0[:, b, tt * P:(tt + 1) * P], V[:, bass.ds(it * T + b * TS, 1), :].rearrange("p a d -> p (a d)"), start=(t == 0),
                                     stop=(tt == 0), **free)
                            if tt == 1:
                                ins = mm(o, D1[:, b, :], V[:, bass.ds(it * T + b * TS + 1, 1), :].rearrange("p a d -> p (a d)"), start=False, stop=True, **free)
                    ins.then_inc(s["y_psum"], 1)
                    end_pass(core, pe, "go_pe")

            @block.scalar
            def _(act):
                step = Step(act, s["act_step"])
                act_layernorm(core, act, step, L)
                for g in range(4):
                    act_copy(core, act, V[:, 4 * g:4 * g + 4, :].rearrange("p t d -> p (t d)"), PS[:, 4 + g, :],
                             s["v_psum"], g + 1, s["v_ready"])
                for g in range(4):
                    act_copy(core, act, L["xT"][:, g * 4 * P:(g + 1) * 4 * P], PS[:, g, :], s["xT_psum"], g + 1, s["xT_ready"])
                end_pass(core, act, "go_act")
                with act.Fori(0, NPASS) as it:
                    end_pass(core, act, "go_act")

            @block.vector
            def _(dve):
                v = nc.vector
                two = lambda ap: ap.rearrange("p (b t) -> p b t", b=NSEQ)
                tab = lambda n: w(n).unsqueeze(1).broadcast_to([P, NSEQ, S])
                step = Step(dve, s["dve_step"])
                dve_layernorm(core, dve, step, L, lambda t: core.X[:, t, :], L["xn"], s["xn_ready"], tiles=ALL_TILES)
                end_pass(core, dve, "go_dve")
                with dve.Fori(0, NPASS) as it:
                    step = Step(dve, s["dve_step"])
                    for n, what in ((1, "k"), (0, "q")):
                        dve.wait_ge(s[what + "_psum"], 1)
                        step.mark(v.tensor_tensor(two(t1[:, n, :]), two(PS[:, 2 * n, :]), tab(f"x{what}_cos"), ALU.mult))
                        step(v.tensor_tensor(two(t2[:, n, :]), two(PS[:, 2 * n + 1, :]), tab(f"x{what}_sin"), ALU.mult))
                        v.tensor_tensor(rot[:, n, :], t1[:, n, :], t2[:, n, :], ALU.add).then_inc(s["a_in"], 1)
                    dve.wait_ge(s["a_out"], 1)
                    v.tensor_tensor(D0[:, :, :], two(PS[:, 5, :]), tab("decay0"), ALU.mult).then_inc(s["b_in"], 1)
                    v.tensor_tensor(D1[:, :, :], PS[:, 6, 0:NSEQ * P].rearrange("p (b t) -> p b t", b=NSEQ),
                                    w("decay0")[:, 0:P].unsqueeze(1).broadcast_to([P, NSEQ, P]), ALU.mult)\
                        .then_inc(s["b_in"], 1)
                    dve_residual(core, dve, it, PS[:, 7, :], s["y_psum"])
                    end_pass(core, dve, "go_dve")


def state_space(core):
    nc, s, PS, w = core.nc, core.sem, core.PS, core.w
    NH = 2
    PAD = TAPS - 1
    QW = S + P
    with ExitStack() as c:
        sb = core.buffers(c)
        L = ln_buffers(core, c, ALL_TILES, turned=False)
        xTp = sb("xTp", [P, B, PAD + S])
        Wx = sb("Wx", [P, TAPS, NH * P])
        Wbc = sb("Wbc", [P, 2, TAPS, 64])
        xs = sb("xs", [P, NH, NT])
        BC = sb("BC", [64, 2, NT])
        zs = sb("zs", [P, NH, NT])
        Xt = sb("Xt", [P, NH, T, P])
        An = sb("An", [P, NH])
        dt, nv, av, u, w1, dd, ez, q1, dA = (sb(n, [P, T, NH]) for n in
                                             ("dt", "nv", "av", "u", "w1", "dd", "ez", "q1", "dA"))
        raw = sb("raw", [P, ALL_TILES, NH])
        dAb = sb("dAb", [P, T, NH, P])
        cs = sb("cs", [P, T, NH])
        Ld = sb("Ld", [P, NSEQ, NH, QW])
        Lx = sb("Lx", [P, NSEQ, NH, QW])
        Gm0, Gm1 = sb("Gm0", [P, NSEQ, S]), sb("Gm1", [P, NSEQ, P])
        Wk = sb("Wk", [P, NSEQ, NH, QW])
        y2 = sb("y2", [P, NH, NT])
        y3 = sb("y3", [P, NH, NT])
        tri2 = core.W[:, COLS["tri"][0]:COLS["tri"][0] + S]
        core.n_setup += 4
        with nc.Block() as block:

            @block.sync
            def _(sp):
                load_next_weights(core, sp)
                end_pass_sync(core, sp, "state_space")
                with sp.Fori(0, NPASS) as it:
                    end_pass_sync(core, sp, "state_space")
                await_next_weights(core, sp)

            @block.gpsimd
            def _(pool):
                g = nc.gpsimd
                g.memset(xTp[:, :, 0:PAD], 0.0).then_inc(s["setup"], 1)
                g.tensor_tensor(Wx[:, :, :], w("L3a_xs").unsqueeze(1).broadcast_to([P, TAPS, NH * P]),
                                w("L3a_taps_xs").rearrange("p (k c) -> p k c", k=TAPS), ALU.mult).then_inc(s["setup"], 1)
                for n, name in enumerate("bc"):
                    g.tensor_tensor(Wbc[:, n], w(f"L3a_{name}").unsqueeze(1).broadcast_to([P, TAPS, 64]),
                                    w(f"L3a_taps_{name}").rearrange("p (k c) -> p k c", k=TAPS), ALU.mult)\
                        .then_inc(s["setup"], 1)
                end_pass(core, pool, "go_pool")
                with pool.Fori(0, NPASS) as it:
                    pool.wait_ge(s["b_in"], 1)
                    g.tensor_copy(dAb[:, :, :, :], dA[:, :, :].unsqueeze(3).broadcast_to([P, T, NH, P]))\
                        .then_inc(s["b_out"], 1)
                    end_pass(core, pool, "go_pool")

            @block.tensor
            def _(pe):
                mm, tr = nc.tensor.matmul, nc.tensor.transpose
                free = dict(skip_group_check=True)
                pe.wait_ge(s["setup"], core.n_setup)
                pe_turn_all(core, pe, L["xn"], "xn_ready")
                for t in range(ALL_TILES):
                    pe.wait_ge(s["xT_ready"], t // 4 + 1)
                    q0 = PAD + (t % TS) * P
                    ins = mm(PS[:, 6, t * NH:(t + 1) * NH], xTp[:, t // TS, q0:q0 + P], w("L3a_dt"),
                             start=(t == 0), stop=True, **free)
                ins.then_inc(s["a_out"], 1)
                end_pass(core, pe, "go_pe")
                with pe.Fori(0, NPASS) as it:
                    seqs = bass.ds(it * NSEQ, NSEQ)
                    for n in range(2):
                        for k in range(TAPS):
                            ins = mm(PS[0:64, 2 + n, :].rearrange("p (b t) -> p b t", b=NSEQ), Wbc[:, n, k, :],
                                     xTp[:, seqs, k:k + S], start=(k == 0), stop=(k == PAD))
                        ins.then_inc(s["z_psum"], 1)
                    for n in range(NH):
                        for k in range(TAPS):
                            ins = mm(PS[:, n, :].rearrange("p (b t) -> p b t", b=NSEQ), Wx[:, k, n * P:(n + 1) * P],
                                     xTp[:, seqs, k:k + S], start=(k == 0), stop=(k == PAD))
                        ins.then_inc(s["z_psum"], 1)
                    for n in range(NH):
                        mm(PS[:, 4 + n, :].rearrange("p (b t) -> p b t", b=NSEQ), w("L3a_z")[:, n * P:(n + 1) * P],
                           xTp[:, seqs, PAD:PAD + S], start=True, stop=True).then_inc(s["z_psum"], 1)
                    pe.wait_ge(s["b_in"], 1)
                    for t in range(T):
                        o = PS[:, 6, 64 + t * NH:64 + (t + 1) * NH]
                        ins = mm(o, w("tri"), dA[:, t, :], start=(t == 0), stop=True, **free)
                        if t % TS:
                            ins = mm(o, w("ones"), dA[:, t - 1, :], start=False, stop=True, **free)
                    ins.then_inc(s["c_out"], 1)
                    pe.wait_ge(s["b_out"], 1)
                    pe.wait_ge(s["h_raw"], 6)
                    for b in range(NSEQ):
                        bank = (7, 0)[b]
                        for h in range(NH):
                            mm(PS[:, bank, h * S:(h + 1) * S], dAb[:, b * TS, h, :], tri2, start=(h == 0), stop=True, **free)
                            ins = mm(PS[:, bank, h * S + P:(h + 1) * S], dAb[:, b * TS + 1, h, :], w("tri"),
                                     start=False, stop=True, **free)
                        ins.then_inc(s["d_out"], 1)
                    for b in range(NSEQ):
                        q0 = b * S
                        mm(PS[:, 2, q0:q0 + S], BC[:, 0, q0:q0 + P], BC[:, 1, q0:q0 + S], start=(b == 0), stop=True, **free)
                        ins = mm(PS[:, 3, b * P:(b + 1) * P], BC[:, 0, q0 + P:q0 + S], BC[:, 1, q0 + P:q0 + S],
                                 start=(b == 0), stop=True, **free)
                    ins.then_inc(s["e_out"], 1)
                    for h in range(NH):
                        for t in range(T):
                            ins = tr(PS[:, 4 + h, t * P:(t + 1) * P], xs[:, h, t * P:(t + 1) * P], w("ident"))
                        ins.then_inc(s["tr_psum"], 1)
                    pe.wait_ge(s["h_ready"], 2 * NSEQ * NH)
                    pe.wait_ge(s["v_ready"], NH)
                    for h in range(NH):
                        for b in range(NSEQ):
                            mm(PS[:, 1 - h, b * S:(b + 1) * S], Xt[:, h, b * TS, :], Wk[:, b, h, 0:S],
                               start=(b == 0), stop=True, **free)
                            ins = mm(PS[:, 1 - h, b * S + P:(b + 1) * S], Xt[:, h, b * TS + 1, :], Wk[:, b, h, S:QW],
                                     start=False, stop=True, **free)
                        ins.then_inc(s["f_out"], 1)
                    pe.wait_ge(s["f_in"], NH)
                    for t in range(T):
                        for h in range(NH):
                            ins = mm(PS[:, 2, t * P:(t + 1) * P], y3[:, h, t * P:(t + 1) * P],
                                     w("L3a_out")[:, h * P:(h + 1) * P], start=(t == 0 and h == 0), stop=True, **free)
                    ins.then_inc(s["y_psum"], 1)
                    end_pass(core, pe, "go_pe")

            @block.scalar
            def _(act):
                a = nc.scalar.activation
                act.wait_ge(s["setup"], core.n_setup)
                step = Step(act, s["act_step"])
                act_layernorm(core, act, step, L)
                for g in range(ALL_TILES // 4):
                    act.wait_ge(s["xT_psum"], g + 1)
                    a(xTp[:, g * NSEQ:(g + 1) * NSEQ, PAD:PAD + S], PS[:, g, :].rearrange("p (b t) -> p b t", b=NSEQ),
                      ACT.Copy).then_inc(s["xT_ready"], 1)
                end_pass(core, act, "go_act")
                with act.Fori(0, NPASS) as it:
                    nc.scalar.preload_act_table_set("natural_log_exp_and_others")
                    a(An[:, :], w("L3a_alog"), ACT.Exp).then_inc(s["a_in"], 1)
                    act.wait_ge(s["gexp_in"], 1)
                    a(u[:, :, :], av[:, :, :], ACT.Exp, scale=-1.0).then_inc(s["gexp_out"], 1)
                    act.wait_ge(s["gexp_in"], 2)
                    a(q1[:, :, :], w1[:, :, :], ACT.Ln).then_inc(s["gexp_out"], 1)
                    for n in range(2):
                        act.wait_ge(s["z_psum"], n + 1)
                        a(BC[:, n, :], PS[0:64, 2 + n, :], ACT.Silu, bias=w(f"L3a_bias_{'bc'[n]}", 64))\
                            .then_inc(s["h_raw"], 1)
                    for n in range(NH):
                        act.wait_ge(s["z_psum"], 3 + n)
                        a(xs[:, n, :], PS[:, n, :], ACT.Silu, bias=w("L3a_bias_xs")[:, n:n + 1]).then_inc(s["h_raw"], 1)
                    for n in range(NH):
                        act.wait_ge(s["z_psum"], 5 + n)
                        a(zs[:, n, :], PS[:, 4 + n, :], ACT.Silu).then_inc(s["h_raw"], 1)
                    nc.scalar.preload_act_table_set("natural_log_exp_and_others")
                    for b in range(NSEQ):
                        act.wait_ge(s["c_in"], b + 1)
                        a(Lx[:, b], Ld[:, b], ACT.Exp).then_inc(s["d_in"], 1)
                    for h in range(NH):
                        act_copy(core, act, Xt[:, h].rearrange("p t c -> p (t c)"), PS[:, 4 + h, :], s["tr_psum"], h + 1,
                                 s["v_ready"])
                    end_pass(core, act, "go_act")

            @block.vector
            def _(dve):
                v = nc.vector
                step = Step(dve, s["dve_step"])
                dve_layernorm(core, dve, step, L, lambda t: core.X[:, t, :], L["xn"], s["xn_ready"], tiles=ALL_TILES)
                dve.wait_ge(s["a_out"], 1)
                v.tensor_tensor(raw[:, :, :], PS[:, 6, 0:ALL_TILES * NH].rearrange("p (t h) -> p t h", h=NH),
                                w("L3a_dtb").unsqueeze(1).broadcast_to([P, ALL_TILES, NH]), ALU.add)
                end_pass(core, dve, "go_dve")
                with dve.Fori(0, NPASS) as it:
                    step = Step(dve, s["dve_step"])
                    step(v.tensor_copy(dt[:, :, :], raw[:, bass.ds(it * T, T), :]))
                    step(v.tensor_scalar(nv[:, :, :], dt[:, :, :], -1.0, None, ALU.mult))
                    v.tensor_tensor(av[:, :, :], dt[:, :, :], nv[:, :, :], ALU.max).then_inc(s["gexp_in"], 1)
                    dve.wait_ge(s["gexp_out"], 1)
                    v.tensor_scalar(w1[:, :, :], u[:, :, :], 1.0, None, ALU.add).then_inc(s["gexp_in"], 1)
                    dve.wait_ge(s["gexp_in"], 2)
                    step(v.tensor_scalar(dd[:, :, :], w1[:, :, :], 1.0, None, ALU.subtract))
                    step(v.tensor_scalar(ez[:, :, :], dd[:, :, :], 0.0, None, ALU.is_equal))
                    step(v.tensor_tensor(dd[:, :, :], dd[:, :, :], ez[:, :, :], ALU.add))
                    step(v.reciprocal(dd[:, :, :], dd[:, :, :]))
                    dve.wait_ge(s["gexp_out"], 2)
                    step(v.tensor_tensor(dd[:, :, :], dd[:, :, :], q1[:, :, :], ALU.mult))
                    step(v.tensor_tensor(dd[:, :, :], dd[:, :, :], ez[:, :, :], ALU.add))
                    step(v.tensor_tensor(dd[:, :, :], dd[:, :, :], u[:, :, :], ALU.mult))
                    step(v.tensor_scalar(dt[:, :, :], dt[:, :, :], 0.0, None, ALU.max))
                    step(v.tensor_tensor(dt[:, :, :], dt[:, :, :], dd[:, :, :], ALU.add))
                    dve.wait_ge(s["a_in"], 1)
                    step(v.tensor_tensor(dd[:, :, :], dt[:, :, :], An[:, :].unsqueeze(1).broadcast_to([P, T, NH]), ALU.mult))
                    v.tensor_scalar(dA[:, :, :], dd[:, :, :], -1.0, None, ALU.mult).then_inc(s["b_in"], 1)
                    dve.wait_ge(s["c_out"], 1)
                    step(v.tensor_copy(cs[:, :, :], PS[:, 6, 64:64 + T * NH].rearrange("p (t h) -> p t h", t=T)))
                    for b in range(NSEQ):
                        dve.wait_ge(s["d_out"], b + 1)
                        bank = (7, 0)[b]
                        for h in range(NH):
                            v.tensor_scalar(Ld[:, b, h, 0:S], PS[:, bank, h * S:(h + 1) * S], cs[:, b * TS, h:h + 1], 0.0,
                                            ALU.subtract, ALU.min)
                            ins = v.tensor_scalar(Ld[:, b, h, S:QW], PS[:, bank, h * S + P:(h + 1) * S],
                                                  cs[:, b * TS + 1, h:h + 1], 0.0, ALU.subtract, ALU.min)
                        ins.then_inc(s["c_in"], 1)
                    dve.wait_ge(s["e_out"], 1)
                    step.mark(v.tensor_tensor(Gm0[:, :, :], PS[:, 2, :].rearrange("p (b t) -> p b t", b=NSEQ),
                                              tri2.unsqueeze(1).broadcast_to([P, NSEQ, S]), ALU.mult))
                    step(v.tensor_tensor(Gm1[:, :, :], PS[:, 3, 0:NSEQ * P].rearrange("p (b t) -> p b t", b=NSEQ),
                                         w("tri").unsqueeze(1).broadcast_to([P, NSEQ, P]), ALU.mult))
                    for b in range(NSEQ):
                        dve.wait_ge(s["d_in"], b + 1)
                        for h in range(NH):
                            v.scalar_tensor_tensor(Wk[:, b, h, 0:S], Lx[:, b, h, 0:S], dt[:, b * TS, h:h + 1],
                                                   Gm0[:, b, :], ALU.mult, ALU.mult).then_inc(s["h_ready"], 1)
                            v.scalar_tensor_tensor(Wk[:, b, h, S:QW], Lx[:, b, h, S:QW], dt[:, b * TS + 1, h:h + 1],
                                                   Gm1[:, b, :], ALU.mult, ALU.mult).then_inc(s["h_ready"], 1)
                    for h in range(NH):
                        dve.wait_ge(s["f_out"], h + 1)
                        step(v.scalar_tensor_tensor(y2[:, h, :], xs[:, h, :], w("L3a_skip")[:, h:h + 1], PS[:, 1 - h, :],
                                                    ALU.mult, ALU.add))
                        v.tensor_tensor(y3[:, h, :], y2[:, h, :], zs[:, h, :], ALU.mult).then_inc(s["f_in"], 1)
                    dve_residual(core, dve, it, PS[:, 2, :], s["y_psum"])
                    end_pass(core, dve, "go_dve")


def latent_experts(core):
    nc, s, PS, w = core.nc, core.sem, core.PS, core.w
    NR = 4
    NK = NR + 4
    RING = 3
    with ExitStack() as c:
        sb = core.buffers(c)
        L = ln_buffers(core, c, ALL_TILES)
        sg, sf, oh, eq, sc, wt, o2 = (sb(n, [P, ALL_TILES, E]) for n in ("sg", "sf", "oh", "eq", "sc", "wt", "o2"))
        pairs = sb("pairs", [P, ALL_TILES, 2, 6])
        gs, keep = sb("gs", [P, ALL_TILES, 2]), sb("keep", [P, ALL_TILES, 2])
        mx, mc = sb("mx", [P, ALL_TILES]), sb("mc", [P, ALL_TILES])
        wT = sb("wT", [P, B * S])
        lat = sb("lat", [P, NT])
        comb = sb("comb", [P, NT])
        hs, hm, ht = (sb(n, [P, RING, NT]) for n in ("hs", "hm", "ht"))
        YT = sb("YT", [P, NT])
        core.n_setup += 1
        with nc.Block() as block:

            @block.sync
            def _(sp):
                load_next_weights(core, sp)
                end_pass_sync(core, sp, "latent_experts")
                with sp.Fori(0, NPASS) as it:
                    end_pass_sync(core, sp, "latent_experts")
                await_next_weights(core, sp)

            @block.gpsimd
            def _(pool):
                nc.gpsimd.memset(wT[:, :], 0.0).then_inc(s["setup"], 1)
                end_pass(core, pool, "go_pool")
                with pool.Fori(0, NPASS) as it:
                    end_pass(core, pool, "go_pool")

            @block.tensor
            def _(pe):
                mm, tr = nc.tensor.matmul, nc.tensor.transpose
                free = dict(skip_group_check=True)
                pe_turn_all(core, pe, L["xn"], "xn_ready")
                for t in range(ALL_TILES):
                    pe.wait_ge(s["xT_ready"], t // 4 + 1)
                    ins = mm(PS[:, 6, t * E:(t + 1) * E], L["xT"][:, t * P:(t + 1) * P], w("L3f_gate"),
                             start=(t == 0), stop=True, **free)
                ins.then_inc(s["gate_psum"], 1)
                pe.wait_ge(s["gate_mask"], 1)
                for g in range(4):
                    for t in range(4):
                        ins = tr(PS[0:E, g, t * P:(t + 1) * P], wt[:, 4 * g + t, :], w("ident"))
                    ins.then_inc(s["maskT_psum"], 1)
                end_pass(core, pe, "go_pe")
                with pe.Fori(0, NPASS) as it:
                    part = bass.ds(it * NT, NT)
                    mm(PS[:, 4, :], w("L3f_fc1"), L["xT"][:, part], start=True, stop=True, **free).then_inc(s["a_out"], 1)

                    def second(i):
                        k = ORDER[i]
                        pe.wait_ge(s["h_ready"], i + 1)
                        if k >= NR:
                            ins = mm(PS[:, 7, :], w("L3f_down")[:, (k - NR) * P:(k - NR + 1) * P], hm[:, i % RING, :],
                                     start=(k == NR), stop=False, **free)
                        else:
                            ins = mm(PS[:, 3, :], w("L3f_w2")[:, k * P:(k + 1) * P], hm[:, i % RING, :],
                                     start=(k == 0), stop=(k == NR - 1), **free)
                        ins.then_inc(s["h_used"], 1)

                    for i, k in enumerate(ORDER):
                        if i >= RING:
                            pe.wait_ge(s["h_raw"], i - RING + 1)
                        if k < NR:
                            if k == 0:
                                pe.wait_ge(s["a_in"], 1)
                            if k >= 2:
                                pe.wait_ge(s["h_ready"], i - 1)
                            mm(PS[:, 4 + k % 2, :], w("pick_pairs")[:, k * P:(k + 1) * P], wT[:, part], start=True, stop=True, **free)\
                                .then_inc(s["g_psum"], 1)
                            mm(PS[:, i % RING, :], w("L3f_w1")[:, k * P:(k + 1) * P], lat[:, :],
                               start=True, stop=True, **free).then_inc(s["z_psum"], 1)
                        else:
                            mm(PS[:, i % RING, :], w("L3f_up")[:, (k - NR) * P:(k - NR + 1) * P], L["xT"][:, part],
                               start=True, stop=True, **free).then_inc(s["z_psum"], 1)
                        if i >= 2:
                            second(i - 2)
                    second(NK - 2)
                    second(NK - 1)
                    pe.wait_ge(s["b_in"], 1)
                    mm(PS[:, 7, :], w("L3f_fc2"), comb[:, :], start=False, stop=True, **free).then_inc(s["b_out"], 1)
                    pe.wait_ge(s["yT_ready"], 1)
                    for t in range(T):
                        ins = tr(PS[:, 0, t * P:(t + 1) * P], YT[:, t * P:(t + 1) * P], w("ident"))
                    ins.then_inc(s["y_psum"], 1)
                    end_pass(core, pe, "go_pe")

            @block.scalar
            def _(act):
                a = nc.scalar.activation
                step = Step(act, s["act_step"])
                act_layernorm(core, act, step, L)
                for g in range(4):
                    act_copy(core, act, L["xT"][:, g * 4 * P:(g + 1) * 4 * P], PS[:, g, :], s["xT_psum"], g + 1, s["xT_ready"])
                act.wait_ge(s["gexp_in"], 1)
                a(sg[:, :, :], sf[:, :, :], ACT.Exp, scale=-1.0).then_inc(s["gexp_out"], 1)
                act.wait_ge(s["setup"], core.n_setup)
                for g in range(4):
                    act_copy(core, act, wT[0:E, g * 4 * P:(g + 1) * 4 * P], PS[0:E, g, :], s["maskT_psum"], g + 1,
                             s["maskT_ready"])
                end_pass(core, act, "go_act")
                with act.Fori(0, NPASS) as it:
                    act_copy(core, act, lat[:, :], PS[:, 4, :], s["a_out"], 1, s["a_in"])
                    for i, k in enumerate(ORDER):
                        act.wait_ge(s["z_psum"], i + 1)
                        if i >= RING:
                            act.wait_ge(s["h_ready"], i - RING + 1)
                        a(hs[:, i % RING, :], PS[:, i % RING, :], ACT.Relu).then_inc(s["h_raw"], 1)
                    act_copy(core, act, comb[:, :], PS[:, 3, :], s["h_used"], NK, s["b_in"])
                    act_copy(core, act, YT[:, :], PS[:, 7, :], s["b_out"], 1, s["yT_ready"])
                    end_pass(core, act, "go_act")

            @block.vector
            def _(dve):
                v = nc.vector
                bc = lambda ap: ap.unsqueeze(2).broadcast_to([P, ALL_TILES, E])
                bt = lambda ap: ap.unsqueeze(1).broadcast_to([P, ALL_TILES, E])

                def hidden(dve, i):
                    k = ORDER[i]
                    dve.wait_ge(s["h_raw"], i + 1)
                    if i >= RING:
                        dve.wait_ge(s["h_used"], i - RING + 1)
                    if k < NR:
                        dve.wait_ge(s["g_psum"], k + 1)
                        v.tensor_tensor(ht[:, i % RING, :], hs[:, i % RING, :], PS[:, 4 + k % 2, :], ALU.mult)\
                            .then_inc(s["c_in"], 1)
                        dve.wait_ge(s["c_in"], k + 1)
                    other = ht if k < NR else hs
                    v.tensor_tensor(hm[:, i % RING, :], hs[:, i % RING, :], other[:, i % RING, :], ALU.mult)\
                        .then_inc(s["h_ready"], 1)

                step = Step(dve, s["dve_step"])

                def first_largest(values, out):
                    step(v.tensor_reduce(mx[:, :], values, AX, ALU.max))
                    step(v.tensor_tensor(eq[:, :, :], values, bc(mx[:, :]), ALU.is_equal))
                    step(v.tensor_tensor(sc[:, :, :], eq[:, :, :], bt(w("countdown")), ALU.mult))
                    step(v.tensor_reduce(mc[:, :], sc[:, :, :], AX, ALU.max))
                    step(v.tensor_tensor(out, sc[:, :, :], bc(mc[:, :]), ALU.is_equal))

                dve_layernorm(core, dve, step, L, lambda t: core.X[:, t, :], L["xn"], s["xn_ready"],
                              tiles=ALL_TILES)
                dve.wait_ge(s["gate_psum"], 1)
                v.tensor_scalar(sf[:, :, :], PS[:, 6, 0:ALL_TILES * E].rearrange("p (t e) -> p t e", t=ALL_TILES), -80.0, None, ALU.max)\
                    .then_inc(s["gexp_in"], 1)
                dve.wait_ge(s["gexp_out"], 1)
                step(v.tensor_scalar(sg[:, :, :], sg[:, :, :], 1.0, None, ALU.add))
                step(v.reciprocal(sg[:, :, :], sg[:, :, :]))
                step(v.tensor_tensor(sf[:, :, :], sg[:, :, :], bt(w("L3f_corr")), ALU.add))
                sv = sf[:, :, :].rearrange("p t (g e) -> p t g e", g=2)
                for at, gap in ((0, 1), (3, 2), (5, 3)):
                    step.mark(v.tensor_tensor(pairs[:, :, :, at:at + 4 - gap], sv[:, :, :, 0:4 - gap],
                                              sv[:, :, :, gap:4], ALU.add))
                dve.wait_ge(s["dve_step"], step.n)
                step(v.tensor_reduce(gs[:, :, :], pairs[:, :, :, :], AX, ALU.max))
                step.mark(v.tensor_tensor(keep[:, :, 0:1], gs[:, :, 0:1], gs[:, :, 1:2], ALU.is_ge))
                step(v.tensor_tensor(keep[:, :, 1:2], gs[:, :, 0:1], gs[:, :, 1:2], ALU.is_lt))
                step(v.tensor_tensor(sv, sv, keep[:, :, :].unsqueeze(3).broadcast_to([P, ALL_TILES, 2, 4]), ALU.mult))
                first_largest(sf[:, :, :], oh[:, :, :])
                step(v.tensor_scalar(o2[:, :, :], oh[:, :, :], -BIG, None, ALU.mult))
                step(v.tensor_tensor(sf[:, :, :], sf[:, :, :], o2[:, :, :], ALU.add))
                first_largest(sf[:, :, :], o2[:, :, :])
                step(v.tensor_tensor(oh[:, :, :], oh[:, :, :], o2[:, :, :], ALU.add))
                step(v.tensor_tensor(oh[:, :, :], oh[:, :, :], sg[:, :, :], ALU.mult))
                step(v.tensor_reduce(mx[:, :], oh[:, :, :], AX, ALU.add))
                step(v.tensor_scalar(mx[:, :], mx[:, :], 1e-20, None, ALU.add))
                step(v.reciprocal(mx[:, :], mx[:, :]))
                v.tensor_tensor(wt[:, :, :], oh[:, :, :], bc(mx[:, :]), ALU.mult).then_inc(s["gate_mask"], 1)
                end_pass(core, dve, "go_dve")
                with dve.Fori(0, NPASS) as it:
                    for i in range(NK):
                        hidden(dve, i)
                    dve_residual(core, dve, it, PS[:, 0, :], s["y_psum"])
                    end_pass(core, dve, "go_dve")


ORDER = (4, 5, 6, 7, 0, 1, 2, 3)


def start(core):
    nc, s, PS, w = core.nc, core.sem, core.PS, core.w
    with ExitStack() as c:
        ctx_tok = c.enter_context(nc.sbuf_tensor("ctx_tok_", [P, B * TS, D], F32))
        zeros = c.enter_context(nc.sbuf_tensor("zeros", [P, D], F32))
        with nc.Block() as block:

            @block.sync
            def _(sp):
                sp.dma_start(core.W[:, :], core.dram["small_common"]).then_inc(s["w_in"], 16)
                sp.dma_start(core.stage_W[0][:, 0:width(WEIGHTS[STAGES[0]])], core.dram[f"small_{STAGES[0]}"])\
                    .then_inc(s["stage_w"], 16)
                sp.dma_start(ctx_tok[:, :, :], core.dram["ctx"].rearrange("(t p) d -> p t d", p=P)).then_inc(s["ctx_tok"], 16)
                sp.dma_start(core.X[:, :, :], core.dram["x"].rearrange("(t p) d -> p t d", p=P)).then_inc(s["x_in"], 16)
                sp.wait_ge(s["rows_zero"], 1)
                sp.dma_start(core.dram["sorted_in"].rearrange("(b p) d -> p b d", p=P),
                             zeros[:, :].unsqueeze(1).broadcast_to([P, BLOCKS, D])).then_inc(s["rows_zero"], 16)
                sp.wait_ge(s["x_in"], 16)
                sp.wait_ge(s["stage_w"], 16)
                sp.wait_ge(s["rows_zero"], 17)
                load_ffn(core, sp, "L0")

            @block.gpsimd
            def _(pool):
                nc.gpsimd.memset(zeros[:, :], 0.0).then_inc(s["rows_zero"], 1)

            @block.tensor
            def _(pe):
                pe.wait_ge(s["w_in"], 16)
                pe.wait_ge(s["ctx_tok"], 16)
                for k in range(4):
                    for t in range(4):
                        ins = nc.tensor.transpose(PS[:, k, t * P:(t + 1) * P], ctx_tok[:, 4 * k + t, :], w("ident"))
                    ins.then_inc(s["ctx_psum"], 1)

            @block.scalar
            def _(act):
                nc.scalar.preload_act_table_set("natural_log_exp_and_others")
                act.wait_ge(s["w_in"], 16)
                for k in range(4):
                    act_copy(core, act, core.ctxT[:, k * 512:(k + 1) * 512], PS[:, k, :], s["ctx_psum"], k + 1, s["ctx_done"])

            @block.vector
            def _(dve):
                v = nc.vector
                dve.wait_ge(s["w_in"], 16)
                v.tensor_copy(core.ident_b[:, :], w("ident"))
                v.tensor_copy(core.neg_q[:, :], w("neg_q"))
                v.tensor_copy(core.neg_k[:, :], w("neg_k")).then_inc(s["ctx_done"], 1)
                dve.wait_ge(s["ctx_done"], 5)


def finish(core):
    nc, s = core.nc, core.sem
    with nc.Block() as block:

        @block.sync
        def _(sp):
            sp.dma_start(core.dram["out"].rearrange("(t p) d -> p t d", p=P), core.X[:, :, :]).then_inc(s["out_done"], 16)
            sp.wait_ge(s["out_done"], 16)


def program(nc, dram):
    with ExitStack() as ctx:
        core = Core(nc, ctx, dram)
        start(core)
        for core.at, st in enumerate(STAGES):
            if st in ATTN:
                attention(core, st)
            elif st in ("L0f", "L1f", "L2f"):
                experts(core, st)
            else:
                {"L2a": channel_attention, "L2x": retention, "L3a": state_space, "L3f": latent_experts}[st](core)
        finish(core)


def tables():
    f = np.float32
    t = {"ident": np.eye(P, dtype=f), "ones": np.ones((P, P), f)}
    r, c = np.arange(P)[:, None], np.arange(P)[None, :]
    t["tri"] = (r <= c).astype(f)
    t["neg_q"] = np.where(c > r, f(-BIG), f(0))
    t["neg_k"] = np.where(r > c, f(-BIG), f(0))
    t["block_diag"] = np.where(r // 16 == c // 16, f(0), f(-BIG))
    t["pick_pairs"] = np.zeros((P, E, 64), f)
    t["pick_pairs"][np.arange(E), np.arange(E), :] = 1
    t["pick_pairs"] = t["pick_pairs"].reshape(P, E * 64)
    t["numbers"] = np.tile(np.arange(BLOCKS, dtype=f), (P, 1))
    t["countdown"] = np.tile(np.arange(E, 0, -1, dtype=f), (P, 1))
    d = np.arange(P) % 64 // DH
    inv = f(1) / np.power(f(10000), np.arange(0, DH, 2, dtype=f) / f(DH))
    ang = (np.arange(S, dtype=f)[None, :] * inv[d // 2][:, None]).astype(f)
    t["rope_cos"] = np.cos(ang).astype(f)
    t["rope_sin"] = np.where(d[:, None] % 2 == 0, -np.sin(ang), np.sin(ang)).astype(f)
    ch = np.arange(P)
    half = D // 2
    sv = (np.arange(0, D, 2, dtype=f) + f(0.4 * D)) / f(1.4 * D)
    pos = np.arange(S, dtype=f)
    scale = np.power(sv[None, :], (pos / f(512))[:, None]).astype(f)
    freqs = f(1) / np.power(f(10000), np.arange(half, dtype=f) / f(half))
    ang = (pos[:, None] * freqs[None, :]).astype(f)
    for q, sc in (("q", scale), ("k", f(1) / scale)):
        co = (np.cos(ang) * sc).astype(f)[:, ch // 2].T
        si = (np.sin(ang) * sc).astype(f)[:, ch // 2].T
        t[f"x{q}_cos"] = co
        t[f"x{q}_sin"] = np.where(ch[:, None] % 2 == 0, -si, si)
    diff = np.arange(S, dtype=f)[None, :] - np.arange(P, dtype=f)[:, None]
    t["decay0"] = np.where(diff >= 0, np.power(f(0.96875), np.maximum(diff, 0)), f(0)).astype(f)
    return t


def lay_out(i):
    f = np.float32
    a = {k: np.asarray(v) for k, v in i.items()}
    col = dict(tables())

    def stack_order(wt, swap=False):
        x = wt.reshape(wt.shape[:-1] + (H // 2, 2, DH // 2, 2))
        if swap:
            x = x[..., ::-1]
        n = x.ndim
        x = x.transpose(tuple(range(n - 4)) + (n - 3, n - 2, n - 1, n - 4))
        return x.reshape(wt.shape)

    spread = lambda x: np.broadcast_to(x.reshape(1, -1), (P, x.size))
    rows = lambda x: np.concatenate([x, np.zeros((P - x.shape[0],) + x.shape[1:], f)], axis=0)
    wide = lambda x: np.concatenate([x, np.zeros(x.shape[:-1] + (P - x.shape[-1],), f)], axis=-1)
    zero = np.zeros(P, f)
    att = {
        "L0a": (a["L0_attn_Wq"].T, a["L0_attn_bq"], a["L0_attn_Wk"].T, a["L0_attn_bk"], a["L0_attn_Wv"].T,
                a["L0_attn_bv"], a["L0_attn_Wo"].T, a["L0_attn_bo"]),
        "L0x": (a["L0_xattn_wq_k"], a["L0_xattn_wq_b"], a["L0_xattn_wk_k"], a["L0_xattn_wk_b"], a["L0_xattn_wv_k"],
                a["L0_xattn_wv_b"], a["L0_xattn_wo_k"], a["L0_xattn_wo_b"]),
        "L1a": (a["L1_attn_W_q"].T, zero, a["L1_attn_W_k"].T, zero, a["L1_attn_W_v"].T, zero, a["L1_attn_W_o"].T, zero),
        "L1x": (a["L1_xattn_WQ"], a["L1_xattn_bQ"], a["L1_xattn_WK"], a["L1_xattn_bK"], a["L1_xattn_WV"],
                a["L1_xattn_bV"], a["L1_xattn_WO"], a["L1_xattn_bO"]),
        "L3x": (a["L3_xattn_Wq"].T, a["L3_xattn_bq"], a["L3_xattn_Wk"].T, a["L3_xattn_bk"], a["L3_xattn_Wv"].T,
                a["L3_xattn_bv"], a["L3_xattn_Wo"].T, a["L3_xattn_bo"]),
    }
    for st, (wq, bq, wk, bk, wv, bv, wo, bo) in att.items():
        for n, wt, b in (("q", wq, bq), ("k", wk, bk)):
            col[f"{st}_w{n}"], col[f"{st}_w{n}s"] = stack_order(wt), stack_order(wt, True)
            col[f"{st}_b{n}"], col[f"{st}_b{n}s"] = stack_order(b)[:, None], stack_order(b, True)[:, None]
        col[f"{st}_wv"], col[f"{st}_wo"] = wv, wo
        col[f"{st}_bv"], col[f"{st}_bo"] = spread(bv), spread(bo)
    chunked = lambda b: b.reshape(E, FC, P).transpose(2, 0, 1).reshape(P, E * FC)
    col["L0_gate"], col["L0_b1"], col["L0_b2"] = a["L0_ffn_centroids"].T, chunked(a["L0_ffn_b1"]), spread(a["L0_ffn_b2"])
    col["L0_gamma"], col["L0_beta"] = a["L0_ffn_gamma"].T, a["L0_ffn_beta"].T
    col["L1_gate"], col["L1_gate_bias"] = a["L1_ffn_w_gate"], spread(a["L1_ffn_b_gate"])
    col["L1_b1"], col["L1_b2"] = chunked(a["L1_ffn_b1"]), spread(a["L1_ffn_b2"])
    col["L2_gate"], col["L2_gate_bias"] = a["L2_ffn_Wr"].T, spread(a["L2_ffn_br"])
    col["L2_b1"], col["L2_b2"] = chunked(a["L2_ffn_b1"]), spread(a["L2_ffn_b2"])
    col["L2a_qkv"], col["L2a_out"] = a["L2_attn_w_qkv"].T, a["L2_attn_w_out"].T
    col["L2a_norm"] = a["L2_attn_norm_weight"][:, None]
    col["L2a_temp"] = np.repeat(a["L2_attn_temperature"].reshape(-1), 16)[:, None]
    swap = lambda x: x.reshape(D, D // 2, 2)[:, :, ::-1].reshape(D, D)
    for n in "qkv":
        col[f"L2x_{n}"] = a[f"L2_xattn_W{n}"]
        if n != "v":
            col[f"L2x_{n}s"] = swap(a[f"L2_xattn_W{n}"])
    win = a["L3_attn_W_in"].T
    taps = a["L3_attn_conv_w"][:, 0, :].T
    cb = a["L3_attn_conv_b"]
    col["L3a_z"], col["L3a_xs"], col["L3a_b"], col["L3a_c"], col["L3a_dt"] = (
        win[:, 0:256], win[:, 256:512], win[:, 512:576], win[:, 576:640], win[:, 640:642])
    col["L3a_taps_xs"], col["L3a_taps_b"], col["L3a_taps_c"] = (
        spread(taps[:, 0:256]), spread(taps[:, 256:320]), spread(taps[:, 320:384]))
    col["L3a_bias_xs"] = cb[0:256].reshape(2, P).T
    col["L3a_bias_b"], col["L3a_bias_c"] = rows(cb[256:320, None]), rows(cb[320:384, None])
    col["L3a_alog"], col["L3a_dtb"], col["L3a_skip"] = (
        spread(a["L3_attn_A_log"]), spread(a["L3_attn_dt_bias"]), spread(a["L3_attn_D_skip"]))
    col["L3a_out"] = a["L3_attn_W_out"].T.reshape(2, P, D).transpose(1, 0, 2).reshape(P, 2 * D)
    col["L3f_gate"], col["L3f_corr"] = a["L3_ffn_gate"].T, spread(a["L3_ffn_corr_bias"])
    col["L3f_fc1"] = wide(a["L3_ffn_fc1_w"].T)
    col["L3f_w1"] = rows(a["L3_ffn_w1"].transpose(2, 0, 1).reshape(64, E * 64))
    col["L3f_w2"] = wide(a["L3_ffn_w2"].transpose(0, 2, 1).reshape(4, P, 64)).transpose(1, 0, 2).reshape(P, 4 * P)
    col["L3f_fc2"] = rows(a["L3_ffn_fc2_w"].T)
    col["L3f_up"] = a["L3_ffn_up_w"].T
    col["L3f_down"] = a["L3_ffn_down_w"].T.reshape(4, P, D).transpose(1, 0, 2).reshape(P, 4 * D)
    packs = {f"small_{st}": np.concatenate([col[n] for n, _ in pairs], axis=1).astype(f, copy=False)
             for st, pairs in {"common": COMMON, **WEIGHTS}.items()}

    first = lambda x: np.ascontiguousarray(x.transpose(1, 0, 2).reshape(P, E * F))
    second = lambda x: np.ascontiguousarray(x.reshape(E, FC, P, D).transpose(2, 0, 1, 3).reshape(P, E * F))
    return {
        **packs,
        "x": a["x"].reshape(B * S, D), "ctx": a["ctx_1024"].reshape(B * S, D),
        "mask0q": a["mask_BxSxS2_ik1"], "mask0k": np.ascontiguousarray(a["mask_BxSxS2_ik1"].transpose(0, 2, 1)),
        "mask1q": np.ascontiguousarray(a["mask_Bx1xSxS2_ik1"][:, 0]),
        "mask1k": np.ascontiguousarray(a["mask_Bx1xSxS2_ik1"][:, 0].transpose(0, 2, 1)),
        "gate_prob": np.ascontiguousarray(a["fside_BxSxS2_0"].transpose(0, 2, 1)),
        "L0_ffn1": first(a["L0_ffn_w1"]), "L0_ffn2": second(a["L0_ffn_w2"]),
        "L1_ffn1": first(a["L1_ffn_W1"]), "L1_ffn2": second(a["L1_ffn_W2"]),
        "L2_ffn1": first(a["L2_ffn_W1"].transpose(0, 2, 1)), "L2_ffn2": second(a["L2_ffn_W2"].transpose(0, 2, 1)),
    }


def kernel(**inputs):
    import concourse.bacc as bacc
    from concourse.bass_utils import run_bass_kernel_spmd

    nc = bacc.Bacc("TRN2", target_bir_lowering=False, num_devices=1)
    arrays = lay_out(inputs)
    dram = {n: nc.dram_tensor(n, a.shape, mybir.dt.from_np(a.dtype), kind="ExternalInput").ap()
            for n, a in arrays.items()}
    dram["out"] = nc.dram_tensor("out", (B * S, D), F32, kind="ExternalOutput").ap()
    for n in "qk":
        dram[f"{n}_bounce"] = nc.dram_tensor(f"{n}_bounce", (3, 2, 3, P // 2, S), BF16, kind="Internal").ap()
    dram["m_bounce"] = nc.dram_tensor("m_bounce", (NMAX * H, S), BF16, kind="Internal").ap()
    for n in ("sorted_in", "sorted_out"):
        dram[n] = nc.dram_tensor(n, (BLOCKS * P, D), F32, kind="Internal").ap()
    program(nc, dram)
    r = run_bass_kernel_spmd(nc, [arrays], core_ids=[0])
    return r.results[0]["out"].reshape(B, S, D)
```
